# Optimizing a Trainium2 kernel written in Bass

```python
import numpy as np
import jax
import jax.numpy as jnp

def _softmax(x, axis=-1):
    return jax.nn.softmax(x, axis=axis)

def _gelu(x):
    return jax.nn.gelu(x, approximate=True)

def _silu(x):
    return jax.nn.silu(x)

def _sigmoid(x):
    return jax.nn.sigmoid(x)

def _layernorm(x, axis=-1, eps=1e-05):
    m = jnp.mean(x, axis=axis, keepdims=True)
    v = jnp.var(x, axis=axis, keepdims=True)
    return (x - m) / jnp.sqrt(v + eps)

def _scatter_add(tgt, idx, src, axis=0):
    return tgt.at[idx].add(src)

def _segment_sum(src, seg, n):
    return jax.ops.segment_sum(src, seg, n)
kernel_name = 'mk_flamingo_gated_d1_seqx_r4_f7a218'

def setup_inputs(seed: int=0):
    np.random.seed(seed)
    _w = jnp.asarray

    def _rec_inputs():
        import jax
        import jax.numpy as jnp
        _rk = jax.random.key(seed)
        x = 0.002226 + 0.9996 * jax.random.normal(jax.random.fold_in(_rk, 1), (16, 112, 256), jnp.float32)
        _lenS = 112 - jax.random.randint(jax.random.fold_in(_rk, 7), (16,), 0, max(1, 112 // 4) + 1, jnp.int32)
        _lenS2 = 375 - jax.random.randint(jax.random.fold_in(_rk, 8), (16,), 0, max(1, 375 // 4) + 1, jnp.int32)
        _ctx_1024P = jax.random.normal(jax.random.fold_in(_rk, 11), (16, 16, 256), jnp.float32)
        _ctx_1024c = jax.random.dirichlet(jax.random.fold_in(_rk, 511), 0.3 * jnp.ones((16,), jnp.float32), (16, 375))
        _ctx_1024t = jnp.einsum('bsk,bkd->bsd', _ctx_1024c, _ctx_1024P)
        _ctx_1024t = _ctx_1024t * jax.lax.rsqrt(jnp.mean(jnp.square(_ctx_1024t)) + 1e-12) * 0.953939
        ctx_1024 = -7.10856e-05 + 0.999911 * (_ctx_1024t + 0.3 * jax.random.normal(jax.random.fold_in(_rk, 611), (16, 375, 256), jnp.float32))
        _validS = jnp.arange(112)[None, :] < _lenS[:, None]
        _validS2 = jnp.arange(375)[None, :] < _lenS2[:, None]
        _causal = jnp.tril(jnp.ones((112, 112), dtype=bool))
        mask_BxS2_bk0 = jnp.logical_not(jnp.broadcast_to(_validS2[:, :], (16, 375)))
        _g = jax.random.normal(jax.random.fold_in(_rk, 9001), (2, 1), jnp.float32)
        _g = jnp.sign(_g) * jnp.maximum(jnp.abs(_g), 1.0) + (_g == 0) * 1.0
        g_xattn = _g[0]
        g_ffn = _g[1]
        return (x, ctx_1024, mask_BxS2_bk0, g_xattn, g_ffn)
    x, ctx_1024, mask_BxS2_bk0, g_xattn, g_ffn = _rec_inputs()

    def _L0_xattn_setup():
        import jax, jax.numpy as jnp
        import numpy as np
        DIM, DIM_HEAD, HEADS, SCALE = (256, 64, 8, 8.0)
        INNER = DIM_HEAD * HEADS
        LN_EPS = 1e-05
        L2_EPS = 1e-12

        def layer_norm(x, w, b):
            mu = jnp.mean(x, axis=-1, keepdims=True)
            var = jnp.mean(jnp.square(x - mu), axis=-1, keepdims=True)
            return (x - mu) * jax.lax.rsqrt(var + LN_EPS) * w + b

        def l2norm(t):
            n = jnp.sqrt(jnp.sum(jnp.square(t), axis=-1, keepdims=True))
            return t / jnp.maximum(n, L2_EPS)
        key = jax.random.key(seed)
        ks = jax.random.split(key, 8)
        b, n, m = (8, 2048, 64)
        x = jax.random.normal(ks[0], (b, n, DIM), dtype=jnp.float32)
        latents = jax.random.normal(ks[1], (b, m, DIM), dtype=jnp.float32)
        mask = jax.random.randint(ks[2], (b, n), 0, 2) > 0
        Wq = jax.random.normal(ks[3], (DIM, INNER), dtype=jnp.float32) * DIM ** (-0.5)
        Wkv = jax.random.normal(ks[4], (DIM, 2 * INNER), dtype=jnp.float32) * DIM ** (-0.5)
        Wo = jax.random.normal(ks[5], (INNER, DIM), dtype=jnp.float32) * INNER ** (-0.5)
        return {'x': x, 'latents': latents, 'mask': mask, 'ln_x_w': jnp.ones((DIM,)), 'ln_x_b': jnp.zeros((DIM,)), 'ln_l_w': jnp.ones((DIM,)), 'ln_l_b': jnp.zeros((DIM,)), 'Wq': Wq, 'Wkv': Wkv, 'q_scale': jnp.ones((DIM_HEAD,)), 'k_scale': jnp.ones((DIM_HEAD,)), 'Wo': Wo, 'ln_o_w': jnp.ones((DIM,)), 'ln_o_b': jnp.zeros((DIM,))}
    _L0_xattn_all = _L0_xattn_setup()
    _L0_xattn_in = {k: v for k, v in _L0_xattn_all.items() if k in ('ln_x_w', 'ln_x_b', 'ln_l_w', 'ln_l_b', 'Wq', 'Wkv', 'q_scale', 'k_scale', 'Wo', 'ln_o_w', 'ln_o_b')}
    del _L0_xattn_all

    def _L0_ffn_setup():
        import jax, jax.numpy as jnp
        import numpy as np
        B, L, H, E, FF, C = (4, 512, 256, 8, 1024, 2)
        key = jax.random.key(seed)
        ks = jax.random.split(key, 6)
        s = 0.02
        return {'x': jax.random.normal(ks[0], (B, L, H), dtype=jnp.float32), 'Wg': jax.random.normal(ks[1], (H, E), dtype=jnp.float32) * s, 'W1': jax.random.normal(ks[2], (E, H, FF), dtype=jnp.float32) * s, 'b1': jnp.zeros((E, FF), dtype=jnp.float32), 'W2': jax.random.normal(ks[3], (E, FF, H), dtype=jnp.float32) * s, 'b2': jnp.zeros((E, H), dtype=jnp.float32)}
    _L0_ffn_all = _L0_ffn_setup()
    _L0_ffn_in = {k: v for k, v in _L0_ffn_all.items() if k in ('Wg', 'W1', 'b1', 'W2', 'b2')}
    del _L0_ffn_all
    return {'x': x, 'ctx_1024': ctx_1024, 'mask_BxS2_bk0': mask_BxS2_bk0, 'g_xattn': g_xattn, 'g_ffn': g_ffn, 'L0_xattn_ln_x_w': _L0_xattn_in['ln_x_w'], 'L0_xattn_ln_x_b': _L0_xattn_in['ln_x_b'], 'L0_xattn_ln_l_w': _L0_xattn_in['ln_l_w'], 'L0_xattn_ln_l_b': _L0_xattn_in['ln_l_b'], 'L0_xattn_Wq': _L0_xattn_in['Wq'], 'L0_xattn_Wkv': _L0_xattn_in['Wkv'], 'L0_xattn_q_scale': _L0_xattn_in['q_scale'], 'L0_xattn_k_scale': _L0_xattn_in['k_scale'], 'L0_xattn_Wo': _L0_xattn_in['Wo'], 'L0_xattn_ln_o_w': _L0_xattn_in['ln_o_w'], 'L0_xattn_ln_o_b': _L0_xattn_in['ln_o_b'], 'L0_ffn_Wg': _L0_ffn_in['Wg'], 'L0_ffn_W1': _L0_ffn_in['W1'], 'L0_ffn_b1': _L0_ffn_in['b1'], 'L0_ffn_W2': _L0_ffn_in['W2'], 'L0_ffn_b2': _L0_ffn_in['b2']}

def reference(x, ctx_1024, mask_BxS2_bk0, g_xattn, g_ffn, L0_xattn_ln_x_w, L0_xattn_ln_x_b, L0_xattn_ln_l_w, L0_xattn_ln_l_b, L0_xattn_Wq, L0_xattn_Wkv, L0_xattn_q_scale, L0_xattn_k_scale, L0_xattn_Wo, L0_xattn_ln_o_w, L0_xattn_ln_o_b, L0_ffn_Wg, L0_ffn_W1, L0_ffn_b1, L0_ffn_W2, L0_ffn_b2):
    import jax
    import jax.numpy as jnp

    def _L0_xattn_ref(x, latents, mask, ln_x_w, ln_x_b, ln_l_w, ln_l_b, Wq, Wkv, q_scale, k_scale, Wo, ln_o_w, ln_o_b):
        import jax, jax.numpy as jnp
        import numpy as np
        DIM, DIM_HEAD, HEADS, SCALE = (256, 64, 8, 8.0)
        INNER = DIM_HEAD * HEADS
        LN_EPS = 1e-05
        L2_EPS = 1e-12

        def layer_norm(x, w, b):
            mu = jnp.mean(x, axis=-1, keepdims=True)
            var = jnp.mean(jnp.square(x - mu), axis=-1, keepdims=True)
            return (x - mu) * jax.lax.rsqrt(var + LN_EPS) * w + b

        def l2norm(t):
            n = jnp.sqrt(jnp.sum(jnp.square(t), axis=-1, keepdims=True))
            return t / jnp.maximum(n, L2_EPS)
        b, n, _ = x.shape
        m = latents.shape[1]
        x = layer_norm(x, ln_x_w, ln_x_b)
        latents = layer_norm(latents, ln_l_w, ln_l_b)
        q = latents @ Wq
        kv_input = jnp.concatenate([x, latents], axis=1)
        kv = kv_input @ Wkv
        k, v = jnp.split(kv, 2, axis=-1)

        def to_heads(t):
            return t.reshape(t.shape[0], t.shape[1], HEADS, DIM_HEAD).transpose(0, 2, 1, 3)
        q, k, v = map(to_heads, (q, k, v))
        q = l2norm(q) * q_scale
        k = l2norm(k) * k_scale
        sim = jnp.einsum('bhid,bhjd->bhij', q, k) * SCALE
        full_mask = jnp.concatenate([mask, jnp.ones((b, m), dtype=bool)], axis=1)[:, None, None, :]
        max_neg = -jnp.finfo(sim.dtype).max
        sim = jnp.where(full_mask, sim, max_neg)
        attn = jax.nn.softmax(sim.astype(jnp.float32), axis=-1).astype(sim.dtype)
        out = jnp.einsum('bhij,bhjd->bhid', attn, v)
        out = out.transpose(0, 2, 1, 3).reshape(b, m, INNER)
        return layer_norm(out @ Wo, ln_o_w, ln_o_b)

    def _L0_ffn_ref(x, Wg, W1, b1, W2, b2):
        import jax, jax.numpy as jnp
        import numpy as np
        B, L, H, E, FF, C = (4, 512, 256, 8, 1024, 2)
        b, l, h = x.shape
        e = Wg.shape[1]
        n = b * l
        k = min(max(int(n * C / e), 1), n)
        xt = x.reshape(n, h)
        S = jax.nn.sigmoid(xt @ Wg).T
        G, I = jax.lax.top_k(S, k)
        ex = xt[I]
        hid = jax.nn.gelu(jnp.einsum('ekh,ehf->ekf', ex, W1) + b1[:, None, :], approximate=False)
        out = (jnp.einsum('ekf,efh->ekh', hid, W2) + b2[:, None, :]) * G[..., None]
        new_x = jnp.zeros_like(xt).at[I.reshape(-1)].add(out.reshape(-1, h))
        return new_x.reshape(b, l, h)
    x = x + jnp.tanh(g_xattn[0]) * _L0_xattn_ref(ctx_1024, _layernorm(x, axis=-1), mask_BxS2_bk0, L0_xattn_ln_x_w, L0_xattn_ln_x_b, L0_xattn_ln_l_w, L0_xattn_ln_l_b, L0_xattn_Wq, L0_xattn_Wkv, L0_xattn_q_scale, L0_xattn_k_scale, L0_xattn_Wo, L0_xattn_ln_o_w, L0_xattn_ln_o_b)
    x = x + jnp.tanh(g_ffn[0]) * _L0_ffn_ref(_layernorm(x, axis=-1), L0_ffn_Wg, L0_ffn_W1, L0_ffn_b1, L0_ffn_W2, L0_ffn_b2)
    return x

_drawn_inputs = setup_inputs


def setup_inputs(seed=0):
    import zlib

    import numpy as np

    out = dict(_drawn_inputs(seed))
    spreads = {'L0_xattn_ln_x_w': (1.0, 0.2),
     'L0_xattn_ln_x_b': (0.0, 0.1),
     'L0_xattn_ln_l_w': (1.0, 0.2),
     'L0_xattn_ln_l_b': (0.0, 0.1),
     'L0_xattn_q_scale': (1.0, 0.2),
     'L0_xattn_k_scale': (1.0, 0.2),
     'L0_xattn_ln_o_w': (1.0, 0.2),
     'L0_xattn_ln_o_b': (0.0, 0.1),
     'L0_ffn_b1': (0.0, 0.343),
     'L0_ffn_b2': (0.0, 0.1)}
    factors = {}
    for name, (base, spread) in spreads.items():
        noise = np.random.default_rng([zlib.crc32(name.encode()), seed]).standard_normal(out[name].shape)
        drawn = base * np.exp(spread * noise) if base else spread * noise
        out[name] = jnp.asarray(drawn.astype(out[name].dtype))
    for name, factor in factors.items():
        out[name] = (out[name] * factor).astype(out[name].dtype)
    return out
```

```python
from contextlib import ExitStack

import concourse.bass as bass
from concourse import mybir

ALU = mybir.AluOpType
ACT = mybir.ActivationFunctionType
AX = mybir.AxisListType
F32 = mybir.dt.float32
BF16 = mybir.dt.bfloat16
F16 = mybir.dt.float16
I32 = mybir.dt.int32
U32 = mybir.dt.uint32
U8 = mybir.dt.uint8

P = 128
LN_EPS = 1e-5
L2_EPS = 1e-12
SCALE = 8.0
MASKED = 1e30
MIN_START = 3e38
SIGMOID_ONE = 17.328680
ABOVE = 100000.0


class Slot:

    def __init__(self, half, par, batches, steady=False):
        self.half, self.par, self.steady = half, par, steady
        self.s = s = 2 * half + par
        self.norm = steady or 0 <= s + 2 < batches
        self.project = steady or 0 <= s + 1 < batches
        self.heads = steady or 0 <= s < batches
        self.tail = steady or 0 <= s - 1 < batches
        self.gate = steady or 0 <= s - 2 < batches

    def at(self, k):
        return self.s + k, (self.par + k) % 2, self.half + (self.par + k) // 2


def flamingo_block_kernel(
    nc, x, ctx_1024, mask, g_xattn, g_ffn, ln_x_w, ln_x_b, ln_l_w, ln_l_b, Wq, Wkv, q_scale, k_scale,
    Wo, ln_o_w, ln_o_b, Wg, W1, b1, W2, b2, out,
):
    B, S, D = x.shape
    M = ctx_1024.shape[1]
    DH = q_scale.shape[0]
    INNER = Wq.shape[1]
    H = INNER // DH
    E, _, FF = W1.shape
    KD = D // P
    KI = INNER // P
    KF = FF // P
    R = 3
    CP = M // R
    KEYS = M + S
    KT = 4
    KR = (KEYS + KT - 1) // KT
    KP = KR * KT
    TOK = B * S
    CAP = TOK * 2 // E
    ST = CAP // S
    assert CP * R == M and ST * S == CAP and B * E == P and KEYS < 512

    tokens = nc.dram_tensor("tokens_scratch", [TOK, D], F32).ap()
    out_rows = out.rearrange("b t d -> (b t) d")

    T_ORDER = ("xT0", "xT1", "x2T", "kT0", "gate", "oT", "kT1", "kT2", "kT3", "qT")

    def t_present(slot):
        return [n for n in T_ORDER if (slot.tail if n == "oT" else slot.gate if n in ("x2T", "gate") else slot.project)]

    FIRST = [Slot(-1, 0, B), Slot(-1, 1, B), Slot(0, 0, B), Slot(0, 1, B)]
    LOOP = (1, B // 2 - 1)
    LAST = [Slot(B // 2 - 1, 0, B), Slot(B // 2 - 1, 1, B), Slot(B // 2, 0, B), Slot(B // 2, 1, B)]
    START2 = sum(len(t_present(s)) for s in FIRST)

    def t_number(slot, name):
        names = t_present(slot)
        if slot.steady or 2 <= slot.s <= B - 1:
            before = START2 + (slot.s - 2) * len(T_ORDER)
        elif slot.s < 2:
            before = sum(len(t_present(s)) for s in FIRST if s.s < slot.s)
        else:
            before = START2 + sum(len(t_present(Slot(s // 2, s % 2, B))) for s in range(2, slot.s))
        return before + names.index(name) + 1

    T_ALL = t_number(LAST[-1], "gate")

    def wait_for(eng, sem, count):
        if isinstance(count, int) and count <= 0:
            return
        eng.wait_ge(sem, count)

    def run_slots(eng, do):
        for slot in FIRST:
            do(slot)
        with eng.Fori(*LOOP) as half:
            for par in range(2):
                do(Slot(half, par, B, steady=True))
        for slot in LAST:
            do(slot)

    with ExitStack() as stack:
        def sb(name, shape, dt=F32):
            return stack.enter_context(nc.sbuf_tensor(name, shape, dt))

        def ps(name, shape, dt=F32):
            return stack.enter_context(nc.psum_tensor(name, shape, dt))

        def sem(name):
            return stack.enter_context(nc.semaphore(name))

        diff = sb("diff", [P, P], I32)
        same = sb("same", [P, P], I32)
        ident = sb("ident", [P, P])
        ident_b = sb("ident_b", [P, P], BF16)
        same_e = sb("same_e", [P, P], BF16)
        before_e = sb("before_e", [P, P], BF16)
        upto = sb("upto", [P, P], BF16)
        ones_b = sb("ones_b", [P, S], BF16)
        minus_half = sb("minus_half", [P, 8])
        wkv = sb("wkv", [P, KD, 2 * INNER])
        wq = sb("wq", [P, KD, INNER])
        wo = sb("wo", [P, KI, D])
        wg = sb("wg", [P, KD, E])
        ctx_w = sb("ctx_w", [P, 2, D])
        lat_w = sb("lat_w", [P, 2, D])
        o_w = sb("o_w", [P, 2, D])
        gains = sb("gains", [P, 2])
        tanhs = sb("tanhs", [P, 2])
        qk = sb("qk", [P, 2])
        qk_scale = sb("qk_scale", [P, 1])
        mask8 = sb("mask8", [S, B * M], U8)
        ctx_in = sb("ctx_in", [CP, 2, R, D])
        x_in = sb("x_in", [S, 2, D])
        x_res = sb("x_res", [S, 2, D])
        stat = sb("stat", [P, 4, 6])
        mean_var = sb("mean_var", [P, 4, 2])
        var_eps = sb("var_eps", [P, 4])
        rstd = sb("rstd", [P, 4])
        stat2 = sb("stat2", [P, 6])
        mean_var2 = sb("mean_var2", [P, 2])
        var_eps2 = sb("var_eps2", [P, 1])
        rstd2 = sb("rstd2", [P, 1])
        z0 = sb("z0", [P, 4, D])
        xn = sb("xn", [S, D])
        z = sb("z", [P, 4, D])
        xT = sb("xT", [P, KD, KP])
        sq = sb("sq", [P, 2, INNER])
        ss = sb("ss", [P, 5, H])
        ss_max = sb("ss_max", [P, 5, H])
        rnorm = sb("rnorm", [P, 5, H])
        kn = sb("kn", [P, 2, INNER])
        qn = sb("qn", [S, INNER])
        kT = sb("kT", [P, 2, KI, KP])
        qT = sb("qT", [P, 2, KI, S])
        V = sb("V", [P, 2, KT, INNER])
        nm = sb("nm", [S, 2, KP])
        negs = sb("negs", [S, 2, KP])
        least = sb("least", [S, H])
        prob = sb("prob", [S, 2, KP])
        den = sb("den", [S, 2, H])
        rden = sb("rden", [S, H])
        pT = sb("pT", [P, 2, KT, S])
        on = sb("on", [S, INNER])
        oT = sb("oT", [P, KI, S])
        stat_o = sb("stat_o", [S, 6])
        mv_o = sb("mv_o", [S, 2])
        ve_o = sb("ve_o", [S, 1])
        rstd_o = sb("rstd_o", [S, 1])
        y_o = sb("y_o", [S, D])
        x1 = sb("x1", [S, 2, D])
        stat_g = sb("stat_g", [S, 6])
        mv_g = sb("mv_g", [S, 2])
        ve_g = sb("ve_g", [S, 1])
        rstd_g = sb("rstd_g", [S, 1])
        x2 = sb("x2", [S, 2, D])
        x2T = sb("x2T", [P, KD, S])
        logits = sb("logits", [S, B * E])
        tied = sb("tied", [S, B * E])
        score = sb("score", [P, S])
        fold = sb("fold", [P, S], I32)
        key = sb("key", [P, S], I32)
        half_i = sb("half_i", [P, 2, S], I32)
        hi_f = sb("hi_f", [P, S])
        lo_f = sb("lo_f", [P, S])
        hit = sb("hit", [P, S])
        above = sb("above", [P, S])
        equal = sb("equal", [P, S])
        cand = sb("cand", [P, 2])
        step = sb("step", [P, 2])
        take = sb("take", [P, 1])
        count = sb("count", [P, 1], BF16)
        bound = sb("bound", [P, 1])
        need = sb("need", [P, 1])
        earlier = sb("earlier", [P, 1])
        gt_b = sb("gt_b", [P, S], BF16)
        eq_b = sb("eq_b", [P, S], BF16)
        eq_count = sb("eq_count", [P, 1], BF16)
        gt_count = sb("gt_count", [P, 1], BF16)
        first_eq = sb("first_eq", [P, S])
        chosen = sb("chosen", [P, S], BF16)
        chosen_count = sb("chosen_count", [P, 1])
        before_c = sb("before_c", [P, P], BF16)
        eqT = sb("eqT", [S, P], BF16)
        chosenT = sb("chosenT", [S, P], BF16)
        place = sb("place", [S, P])
        sig = sb("sig", [S, P])
        rest = sb("rest", [S, P])
        carry = sb("carry", [S, P, 5], BF16)
        ids_i = sb("ids_i", [S, B * E], I32)
        tok_i = sb("tok_i", [S, B * E], I32)
        slots_i = sb("slots_i", [S, CAP], I32)
        slots16 = sb("slots16", [S, CAP], F16)
        onehot = V[0:S, :, :, :].rearrange("s a t n -> s (a t n)").bitcast(BF16)[:, 0:B * CAP].rearrange(
            "s (b c) -> s b c", b=B)
        idx_f = sb("idx_f", [S, ST])
        idx = sb("idx", [S, 2, ST], I32)
        gate_s = sb("gate_s", [S, ST])
        gate_v = sb("gate_v", [S, 2, ST])
        ex = sb("ex", [S, 2, ST, D])
        exT = sb("exT", [P, KD, CAP])
        w1 = sb("w1", [P, 2, KD, FF])
        w2 = sb("w2", [P, 2, KF, D])
        b1_rows = sb("b1_rows", [E * KF, P])
        b1T = sb("b1T", [P, E * KF])
        b2_all = sb("b2_all", [S, E, D])
        hidT = kT[:, :, :, :].rearrange("p a c k -> p (a c k)")[:, 0:KF * CAP].rearrange("p (f c) -> p f c", f=KF)
        y_b = sb("y_b", [S, ST, D])
        y = sb("y", [S, 2, ST, D])

        bankS = ps("bankS", [P, 2, 512])
        bankP = ps("bankP", [P, 2, 512])
        bankT = ps("bankT", [P, 512])
        bankK = ps("bankK", [P, 512])
        bankV = ps("bankV", [P, 512])
        bankO = ps("bankO", [P, 512])
        bankY = (bankK, bankV)

        raw_in = [sem("raw_in0"), sem("raw_in1")]
        res_in = [sem("res_in0"), sem("res_in1")]
        small_in = sem("small_in")
        wkv_in, wq_in, wo_in = sem("wkv_in"), sem("wq_in"), sem("wo_in")
        mask_in = sem("mask_in")
        x1_out = [sem("x1_out0"), sem("x1_out1")]
        x2_out = [sem("x2_out0"), sem("x2_out1")]
        w_in = [sem("w_in0"), sem("w_in1")]
        ex_in = [sem("ex_in0"), sem("ex_in1")]
        y_out = [sem("y_out0"), sem("y_out1")]
        iota_done = sem("iota_done")

        waited = sem("waited")

        def settle(eng):
            eng.sem_inc(waited, 1)

        const_done = sem("const_done")
        pool_set = sem("pool_set")
        tanh_done = sem("tanh_done")
        stat_done, mv_done, rstd_done = sem("stat_done"), sem("mv_done"), sem("rstd_done")
        xn_done, z0_done = sem("xn_done"), sem("z0_done")
        stat2_done, mv2_done, rstd2_done, z0x_done = sem("stat2_done"), sem("mv2_done"), sem("rstd2_done"), sem("z0x_done")
        eps_done, eps2_done = sem("eps_done"), sem("eps2_done")
        zc_mul, zc_done, zl_mul, zl_done = sem("zc_mul"), sem("zc_done"), sem("zl_mul"), sem("zl_done")
        t_full, t_free = sem("t_full"), sem("t_free")
        k_full, k_free = sem("k_full"), sem("k_free")
        sq_done, ss_done, max_done, rn_done = sem("sq_done"), sem("ss_done"), sem("max_done"), sem("rn_done")
        v_full, v_free = sem("v_full"), sem("v_free")
        nm_done = sem("nm_done")
        s_full, neg_done, exp_done = sem("s_full"), sem("neg_done"), sem("exp_done")
        p_full, p_free = sem("p_full"), sem("p_free")
        pv_done = sem("pv_done")
        rden_done, on_done = sem("rden_done"), sem("on_done")
        wo_full, wo_stat, wo_mv, wo_eps, wo_rstd, wo_free = (
            sem(n) for n in ("wo_full", "wo_stat", "wo_mv", "wo_eps", "wo_rstd", "wo_free"))
        yw_done, yb_done, x1_done = sem("yw_done"), sem("yb_done"), sem("x1_done")
        g_stat, g_mv, g_eps, g_rstd, x2_done = (sem(n) for n in ("g_stat", "g_mv", "g_eps", "g_rstd", "x2_done"))
        v_step = sem("v_step")
        score_full = sem("score_full")
        counted, totalled = sem("counted"), sem("totalled")
        eqT_full, eqT_copied, prefix_full = sem("eqT_full"), sem("eqT_copied"), sem("prefix_full")
        chosen_full, chosenT_copied, place_full = sem("chosen_full"), sem("chosenT_copied"), sem("place_full")
        tied_done, eq_done, chosen_done = sem("tied_done"), sem("eq_done"), sem("chosen_done")
        sig_done = sem("sig_done")
        b1_full, b1_done = sem("b1_full"), sem("b1_done")
        hot_done, id_full, idx_done = sem("hot_done"), sem("id_full"), sem("idx_done")
        ext_full, ext_free = sem("ext_full"), sem("ext_free")
        h_full, h_free = sem("h_full"), sem("h_free")
        y_full, y_free, y_done = sem("y_full"), sem("y_free"), sem("y_done")
        v_exp, gate_sum = sem("v_exp"), sem("gate_sum")

        N_SMALL = 15
        block = stack.enter_context(nc.Block())

        @block.sync
        def _(sp):
            def load_raw(slot, k):
                b, par, n = slot.at(k)
                wait_for(sp, z0_done, b - 1)
                wait_for(sp, xn_done, b - 1)
                sp.dma_start(ctx_in[:, par, :, :], ctx_1024[b].rearrange("(p r) d -> p r d", r=R)).then_inc(raw_in[par], 16)
                sp.dma_start(x_in[:, par, :], x[b]).then_inc(raw_in[par], 16)

            def load_res(slot, k):
                b, par, n = slot.at(k)
                wait_for(sp, x1_done, b - 1)
                sp.dma_start(x_res[:, par, :], x[b]).then_inc(res_in[par], 16)

            for par in range(2):
                sp.sem_inc(x1_out[par], 16)
                sp.sem_inc(x2_out[par], 16)

            start = Slot(0, 0, B)
            load_raw(start, 0)
            for n, row in enumerate((ln_x_w, ln_x_b)):
                sp.dma_start(ctx_w[:, n, :], row.partition_broadcast(P)).then_inc(small_in, 16)
            for n, row in enumerate((ln_l_w, ln_l_b)):
                sp.dma_start(lat_w[:, n, :], row.partition_broadcast(P)).then_inc(small_in, 16)
            sp.dma_start(wkv[:, :, :], Wkv.rearrange("(k p) n -> p k n", p=P)).then_inc(wkv_in, 16)
            load_raw(start, 1)
            sp.dma_start(wq[:, :, :], Wq.rearrange("(k p) n -> p k n", p=P)).then_inc(wq_in, 16)
            for n, row in enumerate((ln_o_w, ln_o_b)):
                sp.dma_start(o_w[:, n, :], row.partition_broadcast(P)).then_inc(small_in, 16)
            for n, g in enumerate((g_xattn, g_ffn)):
                sp.dma_start(gains[:, n:n + 1], g.partition_broadcast(P)).then_inc(small_in, 16)
            for n, s_ in enumerate((q_scale, k_scale)):
                for half in range(P // DH):
                    sp.dma_start(qk[half * DH:(half + 1) * DH, n:n + 1], s_.rearrange("(p o) -> p o", o=1)).then_inc(small_in, 16)
            sp.dma_start(mask8[:, :], mask.rearrange("b m -> (b m)").partition_broadcast(S)).then_inc(mask_in, 16)
            sp.dma_start(wo[:, :, :], Wo.rearrange("(k p) n -> p k n", p=P)).then_inc(wo_in, 16)
            sp.dma_start(wg[:, :, :], Wg.rearrange("(k p) n -> p k n", p=P)).then_inc(small_in, 16)
            sp.dma_start(b1_rows[:, :], b1.rearrange("e (k p) -> (e k) p", p=P)).then_inc(small_in, 16)
            sp.dma_start(b2_all[:, :, :], b2.partition_broadcast(S)).then_inc(small_in, 16)
            sp.dma_start(x_res[:, 0, :], x[0]).then_inc(res_in[0], 16)

            def do(slot):
                if slot.gate:
                    b, par, n = slot.at(-2)
                    wait_for(sp, x2_done, b + 1)
                    sp.dma_start(tokens.rearrange("(b t) d -> b t d", t=S)[b], x2[:, par, :]).then_inc(x2_out[par], 16)
                if slot.steady or 2 <= slot.s + 4 < B:
                    load_raw(slot, 4)
                if slot.tail:
                    b, par, n = slot.at(-1)
                    wait_for(sp, x1_done, b + 1)
                    sp.dma_start(out[b], x1[:, par, :]).then_inc(x1_out[par], 16)
                if slot.steady or 1 <= slot.s + 1 < B:
                    load_res(slot, 1)

            for slot in FIRST:
                do(slot)
            with sp.Fori(LOOP[0], LOOP[1] - 1) as half:
                for par in range(2):
                    do(Slot(half, par, B, steady=True))
            for slot in [Slot(B // 2 - 2, 0, B), Slot(B // 2 - 2, 1, B)] + LAST:
                do(slot)

            def load_expert(e, par, n):
                wait_for(sp, y_full, 2 * (e - 1))
                sp.dma_start(w1[:, par, :, :], W1[e].rearrange("(k p) n -> p k n", p=P)).then_inc(w_in[par], 16)
                sp.dma_start(w2[:, par, :, :], W2[e].rearrange("(k p) n -> p k n", p=P)).then_inc(w_in[par], 16)

            load_expert(0, 0, 0)
            load_expert(1, 1, 0)
            with sp.Fori(1, E // 2) as n:
                for par in range(2):
                    load_expert(2 * n + par, par, n)

        @block.gpsimd
        def _(pool):
            nc.gpsimd.iota(diff[:, :], [[1, P]], base=P, channel_multiplier=-1).then_inc(iota_done, 1)
            nc.gpsimd.memset(minus_half[:, :], -0.5)
            nc.gpsimd.memset(var_eps[:, :], 1.0).then_inc(pool_set, 1)
            nc.gpsimd.iota(slots_i[:, :], [[1, CAP]], base=1, channel_multiplier=0)
            nc.gpsimd.iota(ids_i[:, :], [[1, B], [0, E]], base=0, channel_multiplier=0)
            nc.gpsimd.iota(tok_i[:, :], [[0, B * E]], base=0, channel_multiplier=1).then_inc(iota_done, 1)
            pool.wait_ge(pool_set, 1)

            def do(slot):
                if slot.gate:
                    b, par, n = slot.at(-2)
                    wait_for(pool, g_mv, b + 1)
                    settle(pool)
                    nc.gpsimd.tensor_scalar(ve_g[:, :], mv_g[:, 1:2], LN_EPS, None, ALU.add).then_inc(g_eps, 1)
                    wait_for(pool, g_eps, b + 1)
                    nc.gpsimd.tensor_tensor(rstd_g[:, :], ve_g[:, :], minus_half[0:S, 0:1], ALU.pow).then_inc(g_rstd, 1)
                if slot.norm:
                    b, _, _ = slot.at(2)
                    wait_for(pool, mv_done, b + 1)
                    settle(pool)
                    nc.gpsimd.tensor_scalar(var_eps[0:CP, 0:R], mean_var[0:CP, 0:R, 1], LN_EPS, None, ALU.add)
                    nc.gpsimd.tensor_scalar(var_eps[0:S, R:R + 1], mean_var[0:S, R, 1:2], LN_EPS, None, ALU.add).then_inc(eps_done, 1)
                    wait_for(pool, eps_done, b + 1)
                    nc.gpsimd.tensor_tensor(rstd[:, :], var_eps[:, :], minus_half[:, 0:4], ALU.pow).then_inc(rstd_done, 1)

                def rnorms(m):
                    b, _, _ = slot.at(1)
                    rows = KR if m < KT else S
                    wait_for(pool, ss_done, 5 * b + m + 1)
                    settle(pool)
                    nc.gpsimd.tensor_scalar(ss_max[0:rows, m, :], ss[0:rows, m, :], L2_EPS ** 2, None, ALU.max).then_inc(max_done, 1)
                    wait_for(pool, max_done, 5 * b + m + 1)
                    nc.gpsimd.tensor_tensor(rnorm[0:rows, m, :], ss_max[0:rows, m, :], minus_half[0:rows, 0:H], ALU.pow).then_inc(rn_done, 1)

                if slot.project:
                    rnorms(0)
                    rnorms(1)
                if slot.norm:
                    b, _, _ = slot.at(2)
                    wait_for(pool, small_in, 16 * N_SMALL)
                    wait_for(pool, z0_done, b + 1)
                    if slot.project:
                        wait_for(pool, t_full, t_number(slot, "xT1"))
                    w_row = ctx_w[0:CP, 0:1, :].to_broadcast([CP, R, D])
                    nc.gpsimd.tensor_tensor(z[0:CP, 0:R, :], z0[0:CP, 0:R, :], w_row, ALU.mult).then_inc(zc_mul, 1)
                if slot.project:
                    rnorms(2)
                if slot.norm:
                    b, _, _ = slot.at(2)
                    wait_for(pool, mv2_done, b + 1)
                    settle(pool)
                    nc.gpsimd.tensor_scalar(var_eps2[0:S, :], mean_var2[0:S, 1:2], LN_EPS, None, ALU.add).then_inc(eps2_done, 1)
                    wait_for(pool, eps2_done, b + 1)
                    nc.gpsimd.tensor_tensor(rstd2[0:S, :], var_eps2[0:S, :], minus_half[0:S, 0:1], ALU.pow).then_inc(rstd2_done, 1)
                    wait_for(pool, zc_mul, b + 1)
                    b_row = ctx_w[0:CP, 1:2, :].to_broadcast([CP, R, D])
                    nc.gpsimd.tensor_tensor(z[0:CP, 0:R, :], z[0:CP, 0:R, :], b_row, ALU.add).then_inc(zc_done, 1)
                if slot.project:
                    rnorms(3)
                if slot.norm:
                    b, _, _ = slot.at(2)
                    wait_for(pool, z0x_done, b + 1)
                    nc.gpsimd.tensor_tensor(z[0:S, R, :], z0[0:S, R, :], lat_w[0:S, 0, :], ALU.mult).then_inc(zl_mul, 1)
                    wait_for(pool, zl_mul, b + 1)
                    nc.gpsimd.tensor_tensor(z[0:S, R, :], z[0:S, R, :], lat_w[0:S, 1, :], ALU.add).then_inc(zl_done, 1)
                if slot.tail:
                    b, par, n = slot.at(-1)
                    wait_for(pool, wo_mv, b + 1)
                    settle(pool)
                    nc.gpsimd.tensor_scalar(ve_o[:, :], mv_o[:, 1:2], LN_EPS, None, ALU.add).then_inc(wo_eps, 1)
                    wait_for(pool, wo_eps, b + 1)
                    nc.gpsimd.tensor_tensor(rstd_o[:, :], ve_o[:, :], minus_half[0:S, 0:1], ALU.pow).then_inc(wo_rstd, 1)
                if slot.project:
                    rnorms(4)
                if slot.tail:
                    b, par, n = slot.at(-1)
                    wait_for(pool, wo_free, b + 1)
                    wait_for(pool, const_done, 2)
                    wait_for(pool, x1_out[par], 16 * (n + 1))
                    nc.gpsimd.tensor_tensor(x1[:, par, :], y_o[:, :], o_w[0:S, 0, :], ALU.mult).then_inc(yw_done, 1)
                    wait_for(pool, yw_done, b + 1)
                    nc.gpsimd.tensor_tensor(x1[:, par, :], x1[:, par, :], o_w[0:S, 1, :], ALU.add).then_inc(yb_done, 1)
                    wait_for(pool, yb_done, b + 1)
                    wait_for(pool, res_in[par], 16 * (n + 1))
                    nc.gpsimd.tensor_tensor(x1[:, par, :], x1[:, par, :], x_res[:, par, :], ALU.add).then_inc(x1_done, 1)

            run_slots(pool, do)

            def gather(e, par, n):
                wait_for(pool, idx_done, e + 1)
                wait_for(pool, ext_full, 2 * (e - 1))
                settle(pool)
                for t in range(ST):
                    nc.gpsimd.indirect_dma_start(
                        ex[:, par, t, :], None, tokens[:, :],
                        bass.IndirectOffsetOnAxis(ap=idx[:, par, t:t + 1], axis=0),
                        bounds_check=TOK - 1).then_inc(ex_in[par], 16)

            def scatter(e, par, n):
                wait_for(pool, y_done, e + 1)
                if par:
                    wait_for(pool, y_out[0], 16 * ST * (n + 1))
                else:
                    wait_for(pool, y_out[1], 16 * ST * n)
                settle(pool)
                for t in range(ST):
                    nc.gpsimd.indirect_dma_start(
                        out_rows[:, :], bass.IndirectOffsetOnAxis(ap=idx[:, par, t:t + 1], axis=0),
                        y[:, par, t, :], None, bounds_check=TOK - 1,
                        compute_op=ALU.add).then_inc(y_out[par], 16)

            for par in range(2):
                pool.wait_ge(x2_out[par], 16 * (B // 2 + 1))
            gather(0, 0, 0)
            for par in range(2):
                pool.wait_ge(x1_out[par], 16 * (B // 2 + 1))
            gather(1, 1, 0)
            scatter(0, 0, 0)
            with pool.Fori(1, E // 2) as n:
                gather(2 * n, 0, n)
                scatter(2 * n - 1, 1, n - 1)
                gather(2 * n + 1, 1, n)
                scatter(2 * n, 0, n)
            scatter(E - 1, 1, E // 2 - 1)
            for par in range(2):
                pool.wait_ge(y_out[par], 16 * ST * (E // 2))

        @block.scalar
        def _(act):
            act.wait_ge(small_in, 16 * N_SMALL)
            nc.scalar.activation(tanhs[:, :], gains[:, :], ACT.Tanh).then_inc(tanh_done, 1)

            def empty_t(slot, name, dst, src, **kw):
                wait_for(act, t_full, t_number(slot, name))
                nc.scalar.activation(dst, src, ACT.Copy, **kw).then_inc(t_free, 1)

            def square(slot, m):
                b, _, _ = slot.at(1)
                rows = KR if m < KT else S
                wait_for(act, k_full, 5 * b + m + 1)
                wait_for(act, ss_done, 5 * b + (m - 1 if m else 0))
                nc.scalar.activation(sq[0:rows, m % 2, :], bankK[0:rows, 0:INNER], ACT.Square).then_inc(sq_done, 1)

            def empty_v(slot, t):
                b, par, _ = slot.at(1)
                wait_for(act, v_full, KT * b + t + 1)
                nc.scalar.activation(V[0:KR, par, t, :], bankV[0:KR, 0:INNER], ACT.Copy).then_inc(v_free, 1)

            def empty_k(slot, t):
                b, par, _ = slot.at(1)
                src = bankT[:, 0:KI * KR].rearrange("p (c k) -> p c k", c=KI)
                empty_t(slot, f"kT{t}", kT[:, par, :, t * KR:(t + 1) * KR], src)

            def exp(slot, h):
                b, par, _ = slot.at(0)
                wait_for(act, neg_done, H * b + h + 1)
                wait_for(act, p_full, H * b + h - 1)
                if h == 0:
                    wait_for(act, rden_done, b - 1)
                nc.scalar.activation(prob[:, h % 2, :], negs[:, h % 2, :], ACT.Exp, bias=least[:, h:h + 1],
                                     scale=-1.0, accum_out=den[:, par, h:h + 1]).then_inc(exp_done, 1)

            def empty_p(n, h):
                wait_for(act, p_full, n)
                wait_for(act, pv_done, n - 2)
                nc.scalar.activation(pT[0:KR, h % 2, :, :],
                                     bankP[0:KR, h % 2, 0:KT * S].rearrange("p (t s) -> p t s", t=KT),
                                     ACT.Copy).then_inc(p_free, 1)

            def do(slot):
                for h in range(H):
                    if slot.heads:
                        exp(slot, h)
                    if slot.project:
                        if h == 0:
                            empty_t(slot, "xT0", xT[:, 0, 0:KEYS], bankT[:, 0:KEYS])
                        if h == 1:
                            square(slot, 0)
                    if h == 2 and slot.gate:
                        empty_t(slot, "x2T", x2T[:, :, :], bankT[:, 0:KD * S].rearrange("p (k s) -> p k s", k=KD))
                    if h == 2 and slot.project:
                        square(slot, 1)
                    if h == 3:
                        if slot.gate:
                            b, _, _ = slot.at(-2)
                            empty_t(slot, "gate", logits[:, bass.ds(b * E, E)], bankT[0:S, 0:E])
                        if slot.project:
                            empty_v(slot, 1)
                        if slot.tail:
                            empty_t(slot, "oT", oT[:, :, :], bankT[:, 0:KI * S].rearrange("p (c s) -> p c s", c=KI))
                    if slot.project:
                        if h == 4:
                            empty_k(slot, 1)
                        if h == 5:
                            square(slot, 3)
                        if h == 6:
                            square(slot, 4)
                        if h == 7:
                            empty_v(slot, 3)
                    b, _, _ = slot.at(0)
                    if h == 0 and slot.tail:
                        empty_p(H * b, H - 1)
                    if h > 0 and slot.heads:
                        empty_p(H * b + h, h - 1)
                    if slot.project:
                        if h == 0:
                            empty_t(slot, "xT1", xT[:, 1, 0:KEYS], bankT[:, 0:KEYS])
                        if h == 1:
                            empty_v(slot, 0)
                        if h == 2:
                            empty_k(slot, 0)
                        if h == 3:
                            square(slot, 2)
                        if h == 4:
                            empty_v(slot, 2)
                        if h == 5:
                            empty_k(slot, 2)
                        if h == 6:
                            empty_k(slot, 3)
                        if h == 7:
                            b, par, _ = slot.at(1)
                            wait_for(act, const_done, 3)
                            empty_t(slot, "qT", qT[:, par, :, :],
                                    bankT[:, 0:KI * S].rearrange("p (c s) -> p c s", c=KI), scale=qk_scale[:, 0:1])

            run_slots(act, do)

            act.wait_ge(t_free, T_ALL)
            nc.scalar.activation(sig[:, :], logits[:, :], ACT.Sigmoid).then_inc(sig_done, 1)

            def empty_ex(e, kc):
                wait_for(act, ext_full, 2 * e + kc + 1)
                nc.scalar.activation(exT[:, kc, :], bankP[:, kc, 0:CAP], ACT.Copy).then_inc(ext_free, 1)

            def hidden(e):
                for f in range(KF):
                    wait_for(act, h_full, KF * e + f + 1)
                    wait_for(act, y_full, 2 * e)
                    nc.scalar.activation(hidT[:, f, :], bankS[:, f % 2, 0:CAP], ACT.Gelu,
                                         bias=b1T[:, bass.ds(e * KF + f, 1)]).then_inc(h_free, 1)

            act.wait_ge(b1_done, 1)
            for kc in range(KD):
                empty_ex(0, kc)
            hidden(0)
            with act.Fori(1, E) as e:
                for kc in range(KD):
                    empty_ex(e, kc)
                hidden(e)

        @block.vector
        def _(dve):
            dve.wait_ge(iota_done, 1)
            nc.vector.tensor_scalar(ident[:, :], diff[:, :], float(P), None, ALU.is_equal)
            nc.vector.tensor_scalar(same[:, :], diff[:, :], E - 1, None, ALU.bitwise_and).then_inc(v_step, 1)
            nc.vector.memset(nm[:, :, M:KEYS], 0.0)
            nc.vector.memset(nm[:, :, KEYS:KP], MASKED)
            nc.vector.memset(xT[:, :, KEYS:KP], 0.0)
            nc.vector.memset(ones_b[:, :], 1.0)
            nc.vector.tensor_scalar(upto[:, :], diff[:, :], float(P), None, ALU.is_ge)
            nc.vector.tensor_scalar(before_e[:, :], diff[:, :], float(P), None, ALU.is_gt).then_inc(const_done, 1)
            n_steps = [1]

            def link(ins):
                n_steps[0] += 1
                ins.then_inc(v_step, 1)
                dve.wait_ge(v_step, n_steps[0])

            dve.wait_ge(v_step, 1)
            link(nc.vector.tensor_scalar(same_e[:, :], same[:, :], 0.0, None, ALU.is_equal))
            link(nc.vector.tensor_tensor(before_e[:, :], before_e[:, :], same_e[:, :], ALU.mult))
            link(nc.vector.tensor_copy(ident_b[:, :], ident[:, :]))
            dve.wait_ge(iota_done, 2)
            nc.vector.tensor_copy(slots16[:, :], slots_i[:, :])
            nc.vector.tensor_copy(carry[:, :, 0], ids_i[:, :])
            link(nc.vector.tensor_copy(carry[:, :, 1], tok_i[:, :]))

            def norm_begin(slot):
                b, par, n = slot.at(2)
                wait_for(dve, raw_in[par], 32 * (n + 1))
                for r in range(R):
                    nc.vector.bn_stats(stat[0:CP, r, :], ctx_in[:, par, r, :])
                nc.vector.bn_stats(stat[0:S, R, :], x_in[:, par, :]).then_inc(stat_done, 1)
                wait_for(dve, stat_done, b + 1)
                wait_for(dve, eps_done, b)
                settle(dve)
                for r in range(R):
                    nc.vector.bn_aggr(mean_var[0:CP, r, :], stat[0:CP, r, :])
                nc.vector.bn_aggr(mean_var[0:S, R, :], stat[0:S, R, :]).then_inc(mv_done, 1)

            def norm_rows(slot):
                b, par, n = slot.at(2)
                wait_for(dve, rstd_done, b + 1)
                wait_for(dve, zc_mul, b)
                nc.vector.tensor_scalar(xn[:, :], x_in[:, par, :], mean_var[0:S, R, 0:1], rstd[0:S, R:R + 1],
                                        ALU.subtract, ALU.mult).then_inc(xn_done, 1)
                for r in range(R):
                    last = nc.vector.tensor_scalar(z0[0:CP, r, :], ctx_in[:, par, r, :], mean_var[0:CP, r, 0:1],
                                                   rstd[0:CP, r:r + 1], ALU.subtract, ALU.mult)
                last.then_inc(z0_done, 1)
                wait_for(dve, xn_done, b + 1)
                nc.vector.bn_stats(stat2[0:S, :], xn[:, :]).then_inc(stat2_done, 1)

            def norm_again(slot):
                b, _, _ = slot.at(2)
                wait_for(dve, stat2_done, b + 1)
                wait_for(dve, eps2_done, b)
                settle(dve)
                nc.vector.bn_aggr(mean_var2[0:S, :], stat2[0:S, :]).then_inc(mv2_done, 1)

            def norm_end(slot):
                b, _, _ = slot.at(2)
                wait_for(dve, rstd2_done, b + 1)
                wait_for(dve, zl_mul, b)
                nc.vector.tensor_scalar(z0[0:S, R, :], xn[:, :], mean_var2[0:S, 0:1], rstd2[0:S, :],
                                        ALU.subtract, ALU.mult).then_inc(z0x_done, 1)

            def sum_squares(slot, m):
                b, _, _ = slot.at(1)
                rows = KR if m < KT else S
                wait_for(dve, sq_done, 5 * b + m + 1)
                wait_for(dve, max_done, 5 * (b - 1) + m + 1)
                nc.vector.tensor_reduce(ss[0:rows, m, :], sq[0:rows, m % 2, :].rearrange("p (h d) -> p h d", h=H),
                                        AX.X, ALU.add).then_inc(ss_done, 1)

            def unit(slot, m):
                b, _, _ = slot.at(1)
                rows = KR if m < KT else S
                wait_for(dve, rn_done, 5 * b + m + 1)
                src = bankK[0:rows, 0:INNER].rearrange("p (h d) -> p h d", h=H)
                scale = rnorm[0:rows, m, :].unsqueeze(2).to_broadcast([rows, H, DH])
                if m < KT:
                    if m >= 2:
                        wait_for(dve, t_full, t_number(slot, f"kT{m - 2}"))
                    dst = kn[0:rows, m % 2, :]
                else:
                    dst = qn[:, :]
                nc.vector.tensor_tensor(dst.rearrange("p (h d) -> p h d", h=H), src, scale, ALU.mult).then_inc(k_free, 1)

            def mask_row(slot):
                b, par, _ = slot.at(1)
                wait_for(dve, mask_in, 16)
                nc.vector.tensor_scalar(nm[:, par, 0:M].rearrange("s (r p) -> s r p", r=R),
                                        mask8[:, bass.ds(b * M, M)].rearrange("s (p r) -> s r p", r=R),
                                        0.0, MASKED, ALU.is_equal, ALU.mult).then_inc(nm_done, 1)

            def negated(slot, h):
                b, par, _ = slot.at(0)
                if h == 0:
                    wait_for(dve, nm_done, b + 1)
                wait_for(dve, s_full, H * b + h + 1)
                wait_for(dve, exp_done, H * b + h - 1)
                settle(dve)
                nc.vector.tensor_tensor_reduce(negs[:, h % 2, :], bankS[0:S, h % 2, 0:KP], nm[:, par, :], 1.0, MIN_START,
                                               ALU.add, ALU.min, least[:, h:h + 1]).then_inc(neg_done, 1)

            def divide(slot):
                b, par, _ = slot.at(-1)
                wait_for(dve, exp_done, H * (b + 1))
                nc.vector.reciprocal(rden[:, :], den[:, par, :]).then_inc(rden_done, 1)
                wait_for(dve, rden_done, b + 1)
                wait_for(dve, pv_done, H * (b + 1))
                if slot.s is not None and (slot.gate):
                    wait_for(dve, wo_full, b)
                nc.vector.tensor_tensor(on[:, :].rearrange("s (h d) -> s h d", h=H),
                                        bankO[0:S, 0:INNER].rearrange("s (h d) -> s h d", h=H),
                                        rden[:, :].unsqueeze(2).to_broadcast([S, H, DH]), ALU.mult).then_inc(on_done, 1)

            def out_stats(slot):
                b, _, _ = slot.at(-1)
                wait_for(dve, wo_full, b + 1)
                nc.vector.bn_stats(stat_o[:, :], bankV[0:S, 0:D]).then_inc(wo_stat, 1)
                wait_for(dve, wo_stat, b + 1)
                settle(dve)
                nc.vector.bn_aggr(mv_o[:, :], stat_o[:, :]).then_inc(wo_mv, 1)

            def out_norm(slot):
                b, _, _ = slot.at(-1)
                wait_for(dve, wo_rstd, b + 1)
                wait_for(dve, yw_done, b)
                nc.vector.tensor_scalar(y_o[:, :], bankV[0:S, 0:D], mv_o[:, 0:1], rstd_o[:, :],
                                        ALU.subtract, ALU.mult).then_inc(wo_free, 1)

            def gate_stats(slot):
                b, par, _ = slot.at(-2)
                wait_for(dve, x1_done, b + 1)
                nc.vector.bn_stats(stat_g[:, :], x1[:, par, :]).then_inc(g_stat, 1)
                wait_for(dve, g_stat, b + 1)
                settle(dve)
                nc.vector.bn_aggr(mv_g[:, :], stat_g[:, :]).then_inc(g_mv, 1)

            def gate_norm(slot):
                b, par, n = slot.at(-2)
                wait_for(dve, g_rstd, b + 1)
                wait_for(dve, x2_out[par], 16 * (n + 1))
                nc.vector.tensor_scalar(x2[:, par, :], x1[:, par, :], mv_g[:, 0:1], rstd_g[:, :],
                                        ALU.subtract, ALU.mult).then_inc(x2_done, 1)

            dve.wait_ge(small_in, 16 * N_SMALL)
            dve.wait_ge(tanh_done, 1)
            nc.vector.tensor_scalar(o_w[:, :, :], o_w[:, :, :], tanhs[:, 0:1], None, ALU.mult).then_inc(const_done, 1)
            nc.vector.tensor_scalar(qk_scale[:, :], qk[:, 0:1], qk[:, 1:2], -SCALE, ALU.mult, ALU.mult).then_inc(const_done, 1)

            def do(slot):
                for h in range(H):
                    if slot.heads:
                        negated(slot, h)
                    if h == 0:
                        if slot.gate:
                            gate_stats(slot)
                        if slot.norm:
                            norm_begin(slot)
                    if h == 1:
                        if slot.gate:
                            gate_norm(slot)
                        if slot.project:
                            sum_squares(slot, 0)
                            unit(slot, 0)
                    if h == 2:
                        if slot.tail:
                            divide(slot)
                        if slot.project:
                            sum_squares(slot, 1)
                            unit(slot, 1)
                    if h == 3 and slot.norm:
                        norm_rows(slot)
                    if h == 4:
                        if slot.project:
                            sum_squares(slot, 2)
                            unit(slot, 2)
                        if slot.norm:
                            norm_again(slot)
                    if h == 5:
                        if slot.project:
                            sum_squares(slot, 3)
                            unit(slot, 3)
                        if slot.norm:
                            norm_end(slot)
                        if slot.project:
                            mask_row(slot)
                    if h == 6:
                        if slot.tail:
                            out_stats(slot)
                        if slot.project:
                            sum_squares(slot, 4)
                        if slot.tail:
                            out_norm(slot)
                        if slot.project:
                            unit(slot, 4)

            run_slots(dve, do)

            dve.wait_ge(t_free, T_ALL)
            nc.vector.tensor_scalar(tied[:, :], logits[:, :], SIGMOID_ONE, 0.0, ALU.min, ALU.add).then_inc(tied_done, 1)
            dve.wait_ge(score_full, 1)
            link(nc.vector.tensor_copy(score[:, :], bankT[:, 0:S]))
            bits = score[:, :].bitcast(I32)
            link(nc.vector.tensor_scalar(fold[:, :], bits, 31, 0x7FFFFFFF, ALU.arith_shift_right, ALU.bitwise_and))
            link(nc.vector.tensor_tensor(key[:, :], bits, fold[:, :], ALU.bitwise_xor))
            nc.vector.tensor_scalar(half_i[:, 0, :], key[:, :], 16, None, ALU.arith_shift_right)
            link(nc.vector.tensor_scalar(half_i[:, 1, :], key[:, :], 0xFFFF, None, ALU.bitwise_and))
            nc.vector.tensor_copy(hi_f[:, :], half_i[:, 0, :])
            link(nc.vector.tensor_copy(lo_f[:, :], half_i[:, 1, :]))

            BITS = 16
            n_count = [0]

            def tally(values, threshold, op, dst=None, total=count):
                n_count[0] += 1
                with nc.allow_low_precision(reason="counts up to 112 are exact"):
                    nc.vector.tensor_scalar(hit[:, :] if dst is None else dst, values, threshold, None if dst is None else 0.0,
                                            op, ALU.add, accum_out=total[:, :]).then_inc(counted, 1)
                dve.wait_ge(totalled, n_count[0])

            def search(values, least_value, base):
                nc.vector.memset(cand[:, 0:1], float(least_value + 2 ** (BITS - 1)))
                link(nc.vector.memset(step[:, 0:1], float(2 ** (BITS - 1))))
                first = n_steps[0]
                with dve.Fori(0, BITS) as i:
                    with nc.allow_low_precision(reason="counts up to 112 are exact"):
                        nc.vector.tensor_scalar(hit[:, :], values, cand[:, 0:1], None, ALU.is_ge, ALU.add,
                                                accum_out=count[:, :]).then_inc(counted, 1)
                    dve.wait_ge(totalled, base + i + 1)
                    nc.vector.tensor_scalar(take[:, :], bankO[:, 0:1], float(CAP), step[:, 0:1],
                                            ALU.is_ge, ALU.mult)
                    nc.vector.tensor_scalar(step[:, 0:1], step[:, 0:1], 0.5, None, ALU.mult).then_inc(v_step, 1)
                    dve.wait_ge(v_step, first + 2 * i + 1)
                    nc.vector.scalar_tensor_tensor(out=cand[:, 0:1], in0=take[:, :], scalar=step[:, 0:1], in1=cand[:, 0:1],
                                                   op0=ALU.subtract, op1=ALU.add).then_inc(v_step, 1)
                    dve.wait_ge(v_step, first + 2 * i + 2)
                n_steps[0] = first + 2 * BITS

            search(hi_f[:, :], -2 ** 15, 0)
            link(nc.vector.tensor_scalar(bound[:, :], cand[:, 0:1], -0.5, None, ALU.add))
            nc.vector.tensor_scalar(above[:, :], hi_f[:, :], bound[:, :], ABOVE, ALU.is_gt, ALU.mult)
            link(nc.vector.tensor_scalar(equal[:, :], hi_f[:, :], bound[:, :], None, ALU.is_equal))
            link(nc.vector.scalar_tensor_tensor(out=equal[:, :], in0=lo_f[:, :], scalar=1.0, in1=equal[:, :],
                                                op0=ALU.add, op1=ALU.mult))
            link(nc.vector.tensor_tensor(lo_f[:, :], equal[:, :], above[:, :], ALU.add))
            search(lo_f[:, :], 1, BITS)
            link(nc.vector.tensor_scalar(bound[:, :], cand[:, 0:1], -0.5, None, ALU.add))
            with nc.allow_low_precision(reason="counts up to 112 are exact"):
                nc.vector.tensor_scalar(eq_b[:, :], lo_f[:, :], bound[:, :], None, ALU.is_equal, ALU.add,
                                        accum_out=eq_count[:, :]).then_inc(eq_done, 1)
                nc.vector.tensor_scalar(gt_b[:, :], lo_f[:, :], bound[:, :], None, ALU.is_gt, ALU.add,
                                        accum_out=gt_count[:, :]).then_inc(eq_done, 1)
            dve.wait_ge(eqT_full, 1)
            nc.vector.tensor_copy(eqT[:, :], bankP[0:S, 0, 0:P // 2].bitcast(BF16)).then_inc(eqT_copied, 1)
            dve.wait_ge(prefix_full, 1)
            link(nc.vector.tensor_copy(earlier[:, :], bankO[:, 1:2]))
            link(nc.vector.tensor_scalar(need[:, :], bankO[:, 0:1], -1.0, float(CAP), ALU.mult, ALU.add))
            link(nc.vector.tensor_scalar(first_eq[:, :], bankS[:, 0, 0:S], earlier[:, :], need[:, :], ALU.add, ALU.is_le))
            link(nc.vector.tensor_tensor(first_eq[:, :], first_eq[:, :], eq_b[:, :], ALU.mult))
            link(nc.vector.tensor_tensor(first_eq[:, :], first_eq[:, :], gt_b[:, :], ALU.add))
            link(nc.vector.tensor_scalar(chosen[:, :], first_eq[:, :], 1.0, None, ALU.mult, ALU.add,
                                         accum_out=chosen_count[:, :]))
            nc.vector.tensor_scalar(before_c[:, :], before_e[:, :], chosen_count[:, :], None, ALU.mult).then_inc(chosen_done, 1)
            dve.wait_ge(chosen_full, 1)
            link(nc.vector.tensor_copy(chosenT[:, :], bankP[0:S, 0, 0:P // 2].bitcast(BF16)))
            nc.vector.tensor_copy(first_eq[0:S, 0:1], chosenT[:, 0:1]).then_inc(chosenT_copied, 1)
            dve.wait_ge(place_full, 1)
            link(nc.vector.tensor_tensor(place[:, :], bankS[0:S, 0, 0:P], chosenT[:, :], ALU.mult))

            dve.wait_ge(sig_done, 1)
            link(nc.vector.tensor_copy(carry[:, :, 2], sig[:, :]))
            link(nc.vector.tensor_tensor(rest[:, :], sig[:, :], carry[:, :, 2], ALU.subtract))
            link(nc.vector.tensor_copy(carry[:, :, 3], rest[:, :]))
            link(nc.vector.tensor_tensor(rest[:, :], rest[:, :], carry[:, :, 3], ALU.subtract))
            link(nc.vector.tensor_copy(carry[:, :, 4], rest[:, :]))

            dve.wait_ge(b1_full, 1)
            nc.vector.tensor_copy(b1T[:, :], bankT[:, 0:E * KF]).then_inc(b1_done, 1)

            def hot(e):
                wait_for(dve, id_full, e)
                for b in range(B):
                    last = nc.vector.tensor_scalar(onehot[:, b, :], slots16[:, :], place[:, bass.ds(b * E + e, 1)],
                                                   None, ALU.is_equal)
                last.then_inc(hot_done, 1)

            def ids(e, par, n):
                wait_for(dve, id_full, e + 1)
                wait_for(dve, y_out[par], 16 * ST * n)
                got = bankO[0:S, 0:8 * ST].rearrange("s (t c) -> s t c", c=8)
                nc.vector.tensor_copy(idx_f[:, :], got[:, :, 1])
                nc.vector.tensor_copy(gate_s[:, :], got[:, :, 2]).then_inc(v_exp, 1)
                wait_for(dve, v_exp, 2 * e + 1)
                nc.vector.scalar_tensor_tensor(out=idx[:, par, :], in0=got[:, :, 0], scalar=float(S), in1=idx_f[:, :],
                                               op0=ALU.mult, op1=ALU.add).then_inc(idx_done, 1)
                nc.vector.tensor_tensor(gate_s[:, :], got[:, :, 3], gate_s[:, :], ALU.add).then_inc(v_exp, 1)
                wait_for(dve, v_exp, 2 * e + 2)
                nc.vector.tensor_tensor(gate_v[:, par, :], got[:, :, 4], gate_s[:, :], ALU.add).then_inc(gate_sum, 1)
                wait_for(dve, gate_sum, 2 * e + 1)
                nc.vector.tensor_scalar(gate_v[:, par, :], gate_v[:, par, :], tanhs[0:S, 1:2], None, ALU.mult).then_inc(gate_sum, 1)

            def results(e, par, n):
                wait_for(dve, y_done, e)
                for half in range(2):
                    wait_for(dve, y_full, 2 * e + half + 1)
                    nc.vector.tensor_tensor(y_b[:, 2 * half:2 * half + 2, :],
                                            bankY[half][0:S, 0:2 * D].rearrange("s (t d) -> s t d", t=2),
                                            b2_all[:, bass.ds(e, 1), :].to_broadcast([S, 2, D]), ALU.add).then_inc(y_free, 1)
                wait_for(dve, y_free, 2 * e + 2)
                wait_for(dve, gate_sum, 2 * e + 2)
                for t in range(ST):
                    last = nc.vector.tensor_scalar(y[:, par, t, :], y_b[:, t, :], gate_v[:, par, t:t + 1], None, ALU.mult)
                last.then_inc(y_done, 1)

            hot(0)
            ids(0, 0, 0)
            hot(1)
            ids(1, 1, 0)
            hot(2)
            results(0, 0, 0)
            with dve.Fori(1, E // 2 - 1) as n:
                ids(2 * n, 0, n)
                hot(2 * n + 1)
                results(2 * n - 1, 1, n - 1)
                ids(2 * n + 1, 1, n)
                hot(2 * n + 2)
                results(2 * n, 0, n)
            n = E // 2 - 1
            ids(2 * n, 0, n)
            hot(2 * n + 1)
            results(2 * n - 1, 1, n - 1)
            ids(2 * n + 1, 1, n)
            results(2 * n, 0, n)
            results(2 * n + 1, 1, n)

        @block.tensor
        def _(pe):
            pe.wait_ge(const_done, 1)

            def t_bank(slot, name):
                wait_for(pe, t_free, t_number(slot, name) - 1)

            def transpose_x(slot, kc):
                b, _, _ = slot.at(1)
                wait_for(pe, zc_done, b + 1)
                wait_for(pe, zl_done, b + 1)
                t_bank(slot, f"xT{kc}")
                for r in range(R):
                    nc.tensor.transpose(bankT[:, r * CP:(r + 1) * CP], z[0:CP, r, kc * P:(kc + 1) * P], ident[0:CP, 0:CP])
                nc.tensor.transpose(bankT[:, M:KEYS], z[0:S, R, kc * P:(kc + 1) * P], ident[0:S, 0:S]).then_inc(t_full, 1)

            def keys(slot, t):
                b, _, _ = slot.at(1)
                wait_for(pe, t_free, t_number(slot, "xT1"))
                wait_for(pe, wkv_in, 16)
                wait_for(pe, k_free, 5 * b + t)
                for kc in range(KD):
                    last = nc.tensor.matmul(bankK[0:KR, 0:INNER], xT[:, kc, t * KR:(t + 1) * KR], wkv[:, kc, 0:INNER],
                                            start=(kc == 0), stop=(kc == KD - 1))
                last.then_inc(k_full, 1)

            def queries(slot):
                b, _, _ = slot.at(1)
                wait_for(pe, wq_in, 16)
                wait_for(pe, k_free, 5 * b + KT)
                for kc in range(KD):
                    last = nc.tensor.matmul(bankK[0:S, 0:INNER], xT[:, kc, M:KEYS], wq[:, kc, :],
                                            start=(kc == 0), stop=(kc == KD - 1))
                last.then_inc(k_full, 1)

            def values(slot, t):
                b, _, _ = slot.at(1)
                if t < KT - 1 or not slot.tail:
                    wait_for(pe, v_free, KT * b + t)
                else:
                    wait_for(pe, wo_free, b - 1)
                for kc in range(KD):
                    last = nc.tensor.matmul(bankV[0:KR, 0:INNER], xT[:, kc, t * KR:(t + 1) * KR], wkv[:, kc, INNER:],
                                            start=(kc == 0), stop=(kc == KD - 1))
                last.then_inc(v_full, 1)

            def transpose_k(slot, t):
                b, _, _ = slot.at(1)
                wait_for(pe, k_free, 5 * b + t + 1)
                t_bank(slot, f"kT{t}")
                for c in range(KI):
                    last = nc.tensor.transpose(bankT[:, c * KR:(c + 1) * KR], kn[0:KR, t % 2, c * P:(c + 1) * P],
                                               ident[0:KR, 0:KR])
                last.then_inc(t_full, 1)

            def transpose_q(slot):
                b, _, _ = slot.at(1)
                wait_for(pe, k_free, 5 * b + KT + 1)
                t_bank(slot, "qT")
                for c in range(KI):
                    last = nc.tensor.transpose(bankT[:, c * S:(c + 1) * S], qn[:, c * P:(c + 1) * P], ident[0:S, 0:S])
                last.then_inc(t_full, 1)

            def scores(slot, h):
                b, par, _ = slot.at(0)
                if h == 0:
                    wait_for(pe, t_free, t_number(slot, "xT0") - 1 if slot.project else t_before(slot))
                wait_for(pe, neg_done, H * b + h - 1)
                r = DH * (h % 2)
                nc.tensor.matmul(bankS[0:S, h % 2, 0:KP], qT[r:r + DH, par, h // 2, :], kT[r:r + DH, par, h // 2, :],
                                 start=True, stop=True).then_inc(s_full, 1)

            def t_before(slot):
                return t_number(slot, t_present(slot)[0]) - 1

            def transpose_p(n, h):
                wait_for(pe, exp_done, n)
                wait_for(pe, p_free, n - 2)
                for t in range(KT):
                    last = nc.tensor.transpose(bankP[0:KR, h % 2, t * S:(t + 1) * S], prob[:, h % 2, t * KR:(t + 1) * KR],
                                               ident[0:S, 0:S])
                last.then_inc(p_full, 1)

            def attend(n, b, par, h):
                wait_for(pe, p_free, n)
                if h == 0:
                    wait_for(pe, on_done, b)
                    wait_for(pe, v_free, KT * (b + 1))
                for t in range(KT):
                    last = nc.tensor.matmul(bankO[0:S, h * DH:(h + 1) * DH], pT[0:KR, h % 2, t, :],
                                            V[0:KR, par, t, h * DH:(h + 1) * DH], start=(t == 0), stop=(t == KT - 1))
                last.then_inc(pv_done, 1)

            def transpose_o(slot):
                b, _, _ = slot.at(-1)
                wait_for(pe, on_done, b + 1)
                t_bank(slot, "oT")
                for c in range(KI):
                    last = nc.tensor.transpose(bankT[:, c * S:(c + 1) * S], on[:, c * P:(c + 1) * P], ident[0:S, 0:S])
                last.then_inc(t_full, 1)

            def project_out(slot):
                b, _, _ = slot.at(-1)
                wait_for(pe, wo_in, 16)
                wait_for(pe, t_free, t_number(slot, "oT"))
                if slot.project:
                    wait_for(pe, v_free, KT * (b + 2) + KT - 1)
                else:
                    wait_for(pe, v_free, KT * B)
                    wait_for(pe, wo_free, b)
                for c in range(KI):
                    last = nc.tensor.matmul(bankV[0:S, 0:D], oT[:, c, :], wo[:, c, :], start=(c == 0), stop=(c == KI - 1))
                last.then_inc(wo_full, 1)

            def transpose_x2(slot):
                b, par, _ = slot.at(-2)
                wait_for(pe, x2_done, b + 1)
                t_bank(slot, "x2T")
                for kc in range(KD):
                    last = nc.tensor.transpose(bankT[:, kc * S:(kc + 1) * S], x2[:, par, kc * P:(kc + 1) * P], ident[0:S, 0:S])
                last.then_inc(t_full, 1)

            def gate_logits(slot):
                wait_for(pe, small_in, 16 * N_SMALL)
                wait_for(pe, t_free, t_number(slot, "x2T"))
                t_bank(slot, "gate")
                for kc in range(KD):
                    last = nc.tensor.matmul(bankT[0:S, 0:E], x2T[:, kc, :], wg[:, kc, :], start=(kc == 0), stop=(kc == KD - 1))
                last.then_inc(t_full, 1)

            def do(slot):
                for h in range(H):
                    b, par, _ = slot.at(0)
                    if slot.heads:
                        scores(slot, h)
                    if slot.project:
                        if h == 0:
                            transpose_x(slot, 0)
                        if h == 1:
                            keys(slot, 0)
                    if h == 2:
                        if slot.gate:
                            transpose_x2(slot)
                        if slot.project:
                            keys(slot, 1)
                    if h == 3:
                        if slot.gate:
                            gate_logits(slot)
                        if slot.project:
                            values(slot, 1)
                        if slot.tail:
                            transpose_o(slot)
                    if slot.project:
                        if h == 4:
                            transpose_k(slot, 1)
                        if h == 5:
                            keys(slot, 3)
                        if h == 6:
                            queries(slot)
                        if h == 7:
                            values(slot, 3)
                    if h == 0 and slot.tail:
                        transpose_p(H * b, H - 1)
                    if h > 0 and slot.heads:
                        transpose_p(H * b + h, h - 1)
                    if h < 2 and slot.tail:
                        b1_, par1, _ = slot.at(-1)
                        attend(H * b - 1 + h, b1_, par1, H - 2 + h)
                    if h >= 2 and slot.heads:
                        attend(H * b + h - 1, b, par, h - 2)
                    if slot.project:
                        if h == 0:
                            transpose_x(slot, 1)
                        if h == 1:
                            values(slot, 0)
                        if h == 2:
                            transpose_k(slot, 0)
                        if h == 3:
                            keys(slot, 2)
                        if h == 4:
                            values(slot, 2)
                        if h == 5:
                            transpose_k(slot, 2)
                    if h == 5 and slot.tail:
                        project_out(slot)
                    if slot.project:
                        if h == 6:
                            transpose_k(slot, 3)
                        if h == 7:
                            transpose_q(slot)

            run_slots(pe, do)

            pe.wait_ge(tied_done, 1)
            nc.tensor.transpose(bankT[:, 0:S], tied[:, :], ident[0:S, 0:S]).then_inc(score_full, 1)
            with pe.Fori(0, 32) as i:
                pe.wait_ge(counted, i + 1)
                nc.tensor.matmul(bankO[:, 0:1], same_e[:, :], count[:, :], start=True, stop=True).then_inc(totalled, 1)
            pe.wait_ge(eq_done, 1)
            nc.tensor.transpose(bankP[0:S, 0, 0:P // 2].bitcast(BF16), eq_b[:, :], ident_b[:, :]).then_inc(eqT_full, 1)
            pe.wait_ge(eq_done, 2)
            nc.tensor.matmul(bankO[:, 0:1], same_e[:, :], gt_count[:, :], start=True, stop=True)
            nc.tensor.matmul(bankO[:, 1:2], before_e[:, :], eq_count[:, :], start=True, stop=True)
            pe.wait_ge(eqT_copied, 1)
            nc.tensor.matmul(bankS[:, 0, 0:S], eqT[:, :], upto[0:S, 0:S], start=True, stop=True).then_inc(prefix_full, 1)
            pe.wait_ge(chosen_done, 1)
            nc.tensor.transpose(bankP[0:S, 0, 0:P // 2].bitcast(BF16), chosen[:, :], ident_b[:, :]).then_inc(chosen_full, 1)
            pe.wait_ge(chosenT_copied, 1)
            nc.tensor.matmul(bankS[0:S, 0, 0:P], upto[0:S, 0:S], chosenT[:, :], start=True, stop=False)
            nc.tensor.matmul(bankS[0:S, 0, 0:P], ones_b[:, :], before_c[:, :], start=False, stop=True).then_inc(place_full, 1)
            nc.tensor.transpose(bankT[:, 0:E * KF], b1_rows[:, :], ident[0:E * KF, 0:E * KF]).then_inc(b1_full, 1)

            def find(e):
                wait_for(pe, hot_done, e + 1)
                wait_for(pe, gate_sum, 2 * e)
                for t in range(ST):
                    for b in range(B):
                        last = nc.tensor.matmul(bankO[0:S, 8 * t:8 * t + 5], onehot[:, b, t * S:(t + 1) * S],
                                                carry[:, bass.ds(b * E + e, 1), :].rearrange("s o c -> s (o c)"),
                                                start=(b == 0), stop=(b == B - 1))
                last.then_inc(id_full, 1)

            def transpose_ex(e, par, n):
                wait_for(pe, ex_in[par], 16 * ST * (n + 1))
                wait_for(pe, ext_free, 2 * e)
                for kc in range(KD):
                    for t in range(ST):
                        last = nc.tensor.transpose(bankP[:, kc, t * S:(t + 1) * S], ex[:, par, t, kc * P:(kc + 1) * P],
                                                   ident[0:S, 0:S])
                    last.then_inc(ext_full, 1)

            def expert_in(e, par, n):
                wait_for(pe, w_in[par], 32 * (n + 1))
                wait_for(pe, ext_free, 2 * (e + 1))
                for f in range(KF):
                    wait_for(pe, h_free, KF * e + f - 1)
                    for kc in range(KD):
                        last = nc.tensor.matmul(bankS[:, f % 2, 0:CAP], w1[:, par, kc, f * P:(f + 1) * P], exT[:, kc, :],
                                                start=(kc == 0), stop=(kc == KD - 1))
                    last.then_inc(h_full, 1)

            def expert_out(e, par, n):
                wait_for(pe, h_free, KF * (e + 1))
                for half in range(2):
                    wait_for(pe, y_free, 2 * (e - 1) + half + 1)
                    for t in range(2):
                        rows = (2 * half + t) * S
                        for f in range(KF):
                            last = nc.tensor.matmul(bankY[half][0:S, t * D:(t + 1) * D], hidT[:, f, rows:rows + S],
                                                    w2[:, par, f, :], start=(f == 0), stop=(f == KF - 1))
                    last.then_inc(y_full, 1)

            find(0)
            transpose_ex(0, 0, 0)

            def expert(e, par, n, more=True):
                if more:
                    find(e + 1)
                expert_in(e, par, n)
                if more:
                    transpose_ex(e + 1, 1 - par, n + par)
                expert_out(e, par, n)

            for par in range(2):
                expert(par, par, 0)
            with pe.Fori(1, E // 2 - 1) as n:
                for par in range(2):
                    expert(2 * n + par, par, n)
            expert(E - 2, 0, E // 2 - 1)
            expert(E - 1, 1, E // 2 - 1, more=False)


_INS = ['x', 'ctx_1024', 'mask_BxS2_bk0', 'g_xattn', 'g_ffn', 'L0_xattn_ln_x_w', 'L0_xattn_ln_x_b',
        'L0_xattn_ln_l_w', 'L0_xattn_ln_l_b', 'L0_xattn_Wq', 'L0_xattn_Wkv', 'L0_xattn_q_scale',
        'L0_xattn_k_scale', 'L0_xattn_Wo', 'L0_xattn_ln_o_w', 'L0_xattn_ln_o_b', 'L0_ffn_Wg', 'L0_ffn_W1',
        'L0_ffn_b1', 'L0_ffn_W2', 'L0_ffn_b2']
_OUTS = [((16, 112, 256), 'float32')]


def kernel(**inputs):
    import numpy as _np
    import concourse.bacc as _bacc
    from concourse import mybir as _mybir
    from concourse.bass_utils import run_bass_kernel_spmd as _run

    nc = _bacc.Bacc("TRN2", target_bir_lowering=False, num_devices=1)
    arrays, args = {}, []
    for name in _INS:
        a = _np.ascontiguousarray(inputs[name])
        arrays[f"in_{name}_dram"] = a
        args.append(nc.dram_tensor(f"in_{name}_dram", a.shape, _mybir.dt.from_np(a.dtype), kind="ExternalInput").ap())
    for i, (shape, dtype) in enumerate(_OUTS):
        dt = _mybir.dt.from_np(_np.dtype(dtype))
        args.append(nc.dram_tensor(f"out_{i}_dram", shape, dt, kind="ExternalOutput").ap())
    flamingo_block_kernel(nc, *args)
    r = _run(nc, [arrays], core_ids=[0])
    got = tuple(r.results[0][f"out_{i}_dram"] for i in range(len(_OUTS)))
    return got[0]
```

```python
from contextlib import ExitStack

import concourse.bass as bass
from concourse import mybir

ALU = mybir.AluOpType
ACT = mybir.ActivationFunctionType
AX = mybir.AxisListType
F32 = mybir.dt.float32
F32R = mybir.dt.float32r
BF16 = mybir.dt.bfloat16
F16 = mybir.dt.float16
I32 = mybir.dt.int32
U32 = mybir.dt.uint32
U8 = mybir.dt.uint8

P = 128
LN_EPS = 1e-5
L2_EPS = 1e-12
SCALE = 8.0
MASKED = 1e30
MIN_START = 3e38
SIGMOID_ONE = 17.328680
HI_UNIT = 2.0 ** 17


class Slot:

    def __init__(self, half, par, batches, steady=False):
        self.half, self.par, self.steady = half, par, steady
        self.s = s = 2 * half + par
        self.norm = steady or 0 <= s + 2 < batches
        self.project = steady or 0 <= s + 1 < batches
        self.heads = steady or 0 <= s < batches
        self.tail = steady or 0 <= s - 1 < batches
        self.gate = steady or 0 <= s - 2 < batches

    def at(self, k):
        return self.s + k, (self.par + k) % 2, self.half + (self.par + k) // 2


def flamingo_block_kernel(
    nc, x, ctx_1024, mask, g_xattn, g_ffn, ln_x_w, ln_x_b, ln_l_w, ln_l_b, Wq, Wkv, q_scale, k_scale,
    Wo, ln_o_w, ln_o_b, Wg, W1, b1, W2, b2, out,
):
    B, S, D = x.shape
    M = ctx_1024.shape[1]
    DH = q_scale.shape[0]
    INNER = Wq.shape[1]
    H = INNER // DH
    E, _, FF = W1.shape
    KD = D // P
    KI = INNER // P
    KF = FF // P
    R = 3
    CP = M // R
    KEYS = M + S
    KT = 4
    KR = (KEYS + KT - 1) // KT
    KP = KR * KT
    TOK = B * S
    CAP = TOK * 2 // E
    ST = CAP // S
    HOT = 4
    TRIES = 3
    BITS = 16
    assert CP * R == M and ST * S == CAP and B * E == P and KEYS < 512

    tokens = nc.dram_tensor("tokens_scratch", [TOK, D], F32).ap()
    out_rows = out.rearrange("b t d -> (b t) d")

    T_ORDER = ("xT0", "xT1", "x2T", "oT", "kT0", "gate", "kT1", "kT2", "kT3", "qT")

    def t_bank_of(name):
        return T_ORDER.index(name) % 2

    def t_present(slot, bank):
        return [n for n in T_ORDER[bank::2]
                if (slot.tail if n == "oT" else slot.gate if n in ("x2T", "gate") else slot.project)]

    FIRST = [Slot(-1, 0, B), Slot(-1, 1, B), Slot(0, 0, B), Slot(0, 1, B)]
    LOOP = (1, B // 2 - 1)
    LAST = [Slot(B // 2 - 1, 0, B), Slot(B // 2 - 1, 1, B), Slot(B // 2, 0, B), Slot(B // 2, 1, B)]

    def t_before(slot, bank):
        start = sum(len(t_present(s, bank)) for s in FIRST)
        if slot.steady or 2 <= slot.s <= B - 1:
            return start + (slot.s - 2) * (len(T_ORDER) // 2)
        if slot.s < 2:
            return sum(len(t_present(s, bank)) for s in FIRST if s.s < slot.s)
        return start + sum(len(t_present(Slot(s // 2, s % 2, B), bank)) for s in range(2, slot.s))

    def t_number(slot, name):
        bank = t_bank_of(name)
        return t_before(slot, bank) + t_present(slot, bank).index(name) + 1

    T_ALL = [t_before(Slot(B // 2 + 1, 0, B), bank) for bank in range(2)]

    def wait_for(eng, sem, count):
        if isinstance(count, int) and count <= 0:
            return
        eng.wait_ge(sem, count)

    def run_slots(eng, do):
        for slot in FIRST:
            do(slot)
        with eng.Fori(*LOOP) as half:
            for par in range(2):
                do(Slot(half, par, B, steady=True))
        for slot in LAST:
            do(slot)

    with ExitStack() as stack:
        def sb(name, shape, dt=F32):
            return stack.enter_context(nc.sbuf_tensor(name, shape, dt))

        def ps(name, shape, dt=F32):
            return stack.enter_context(nc.psum_tensor(name, shape, dt))

        def sem(name):
            return stack.enter_context(nc.semaphore(name))

        diff = sb("diff", [P, P], I32)
        same = sb("same", [P, P], I32)
        ident = sb("ident", [P, P])
        ident_b = sb("ident_b", [P, P], BF16)
        same_e = sb("same_e", [P, P], BF16)
        before_e = sb("before_e", [P, P], BF16)
        upto = sb("upto", [P, P], BF16)
        ones_b = sb("ones_b", [P, S], BF16)
        minus_half = sb("minus_half", [P, 8])
        raw1 = sb("raw1", [P, KD * FF])
        raw2 = sb("raw2", [P, KF * D])
        wg = sb("wg", [P, KD, E])
        gains = sb("gains", [P, 2])
        tanhs = sb("tanhs", [P, 2])
        qk = sb("qk", [P, 2])
        qk_scale = sb("qk_scale", [P, 1])
        b1_rows = sb("b1_rows", [E * KF, P])
        b1T = sb("b1T", [P, E * KF])
        b2_all = sb("b2_all", [S, E, D])
        logits = sb("logits", [S, B * E])
        x1 = sb("x1", [S, 2, D])
        x2 = sb("x2", [S, 2, D])
        carry = sb("carry", [S, P, 5], BF16)
        ids_i = sb("ids_i", [S, B * E], I32)
        tok_i = sb("tok_i", [S, B * E], I32)
        slots_i = sb("slots_i", [S, CAP], I32)
        slots16 = sb("slots16", [S, CAP], F16)

        persistent = stack
        stack = persistent.enter_context(ExitStack())
        wkv = sb("wkv", [P, 2, KD, 2 * INNER], F32R)
        wq = sb("wq", [P, 2, KD, INNER], F32R)
        wo = sb("wo", [P, 2, KI, D], F32R)
        ctx_w = sb("ctx_w", [P, 2, D])
        lat_w = sb("lat_w", [P, 2, D])
        o_w = sb("o_w", [P, 2, D])
        mask8 = sb("mask8", [S, B * M], U8)
        ctx_in = sb("ctx_in", [CP, 2, R, D])
        x_in = sb("x_in", [S, 2, D])
        x_res = sb("x_res", [S, 2, D])
        stat = sb("stat", [P, 4, 6])
        mean_var = sb("mean_var", [P, 4, 2])
        var_eps = sb("var_eps", [P, 4])
        rstd = sb("rstd", [P, 4])
        stat2 = sb("stat2", [P, 6])
        mean_var2 = sb("mean_var2", [P, 2])
        var_eps2 = sb("var_eps2", [P, 1])
        rstd2 = sb("rstd2", [P, 1])
        z0 = sb("z0", [P, 4, D])
        xn = sb("xn", [S, D])
        z = sb("z", [P, 4, D])
        xT = sb("xT", [P, 2, KD, KP], F32R)
        sq = sb("sq", [P, 2, INNER])
        ss = sb("ss", [P, 5, H])
        ss_max = sb("ss_max", [P, 5, H])
        rnorm = sb("rnorm", [P, 5, H])
        kraw = sb("kraw", [P, 3, INNER])
        kn = sb("kn", [P, 2, INNER])
        qn = sb("qn", [S, INNER])
        kT = sb("kT", [P, 2, 2, KI, KP], F32R)
        qT = sb("qT", [P, 2, 2, KI, S], F32R)
        V = sb("V", [P, 2, KT, INNER])
        nm = sb("nm", [S, 2, KP])
        negs = sb("negs", [S, 2, KP])
        least = sb("least", [S, H])
        prob = sb("prob", [S, 2, KP])
        den = sb("den", [S, 2, H])
        rden = sb("rden", [S, H])
        pT = sb("pT", [P, 2, KT, S])
        on = sb("on", [S, INNER])
        oT = sb("oT", [P, 2, KI, S], F32R)
        stat_o = sb("stat_o", [S, 6])
        mv_o = sb("mv_o", [S, 2])
        ve_o = sb("ve_o", [S, 1])
        rstd_o = sb("rstd_o", [S, 1])
        y_o = sb("y_o", [S, D])
        stat_g = sb("stat_g", [S, 6])
        mv_g = sb("mv_g", [S, 2])
        ve_g = sb("ve_g", [S, 1])
        rstd_g = sb("rstd_g", [S, 1])
        x2T = sb("x2T", [P, KD, S])
        stack.close()
        stack = persistent

        tied = sb("tied", [S, B * E])
        score = sb("score", [P, S])
        fold = sb("fold", [P, S], I32)
        key = sb("key", [P, S], I32)
        half_i = sb("half_i", [P, 2, S], I32)
        hi_f = sb("hi_f", [P, S])
        lo_f = sb("lo_f", [P, S])
        hit = sb("hit", [P, TRIES, S])
        cand = sb("cand", [P, TRIES])
        ahead = sb("ahead", [P, TRIES])
        tries = sb("tries", [P, TRIES])
        step = sb("step", [P, TRIES])
        passed = sb("passed", [P, 1])
        reached = sb("reached", [P, TRIES])
        count = sb("count", [P, TRIES], BF16)
        bound = sb("bound", [P, 1])
        need = sb("need", [P, 1])
        earlier = sb("earlier", [P, 1])
        gt_b = sb("gt_b", [P, S], BF16)
        eq_b = sb("eq_b", [P, S], BF16)
        eq_count = sb("eq_count", [P, 1], BF16)
        gt_count = sb("gt_count", [P, 1], BF16)
        first_eq = sb("first_eq", [P, S])
        chosen = sb("chosen", [P, S], BF16)
        chosen_count = sb("chosen_count", [P, 1])
        before_c = sb("before_c", [P, P], BF16)
        eqT = sb("eqT", [S, P], BF16)
        chosenT = sb("chosenT", [S, P], BF16)
        place = sb("place", [S, P])
        sig = sb("sig", [S, P])
        rest = sb("rest", [S, P])
        onehot = sb("onehot", [S, B, CAP], BF16)
        carry_e = sb("carry_e", [S, 2, B, 5], BF16)
        idx_f = sb("idx_f", [S, ST])
        idx = sb("idx", [S, 2, ST], I32)
        idx_y = sb("idx_y", [S, 2, ST], I32)
        gate_s = sb("gate_s", [S, ST])
        gate_v = sb("gate_v", [S, 2, ST])
        ex = sb("ex", [S, 2, ST, D])
        exT = sb("exT", [P, 2, KD, CAP], F32R)
        w1 = sb("w1", [P, 2, 2, KD, FF], F32R)
        w2 = sb("w2", [P, 2, 2, KF, D], F32R)
        hid = sb("hid", [P, 2, CAP])
        hidT = sb("hidT", [P, 2, KF, CAP], F32R)
        y_b = sb("y_b", [S, ST, D])
        y = sb("y", [S, 2, ST, D])

        bankS = ps("bankS", [P, 2, 512])
        bankP = ps("bankP", [P, 512])
        bankT = [ps("bankT0", [P, 512]), ps("bankT1", [P, 512])]
        bankK = ps("bankK", [P, 512])
        bankV = ps("bankV", [P, 512])
        bankO = ps("bankO", [P, 512])
        bankY = (bankK, bankV)
        bankX = (bankP, bankT[0])

        raw_in = [sem("raw_in0"), sem("raw_in1")]
        res_in = [sem("res_in0"), sem("res_in1")]
        small_in = sem("small_in")
        qk_in = sem("qk_in")
        wkv_in, wq_in, wo_in = sem("wkv_in"), sem("wq_in"), sem("wo_in")
        mask_in = sem("mask_in")
        x1_out = [sem("x1_out0"), sem("x1_out1")]
        x2_out = [sem("x2_out0"), sem("x2_out1")]
        w1_in, w2_in = sem("w1_in"), sem("w2_in")
        rows_in = sem("rows_in")
        ex_in = [sem("ex_in0"), sem("ex_in1")]
        y_out = [sem("y_out0"), sem("y_out1")]
        iota_done = sem("iota_done")

        waited = sem("waited")

        def settle(eng):
            eng.sem_inc(waited, 1)

        const_done = sem("const_done")
        pool_set = sem("pool_set")
        tanh_done = sem("tanh_done")
        qk_done = sem("qk_done")
        stat_done, mv_done, rstd_done = sem("stat_done"), sem("mv_done"), sem("rstd_done")
        xn_done, z0_done = sem("xn_done"), sem("z0_done")
        stat2_done, mv2_done, rstd2_done, z0x_done = sem("stat2_done"), sem("mv2_done"), sem("rstd2_done"), sem("z0x_done")
        eps_done, eps2_done = sem("eps_done"), sem("eps2_done")
        zc_mul, zc_done, zl_mul, zl_done = sem("zc_mul"), sem("zc_done"), sem("zl_mul"), sem("zl_done")
        t_full, t_free = [sem("t_full0"), sem("t_full1")], [sem("t_free0"), sem("t_free1")]
        k_full, k_free = sem("k_full"), sem("k_free")
        kn_done = sem("kn_done")
        sq_done, ss_done, max_done, rn_done = sem("sq_done"), sem("ss_done"), sem("max_done"), sem("rn_done")
        v_full, v_free = sem("v_full"), sem("v_free")
        nm_done = sem("nm_done")
        s_full, neg_done, exp_done = sem("s_full"), sem("neg_done"), sem("exp_done")
        p_full, p_free = sem("p_full"), sem("p_free")
        pv_done = sem("pv_done")
        rden_done, on_done = sem("rden_done"), sem("on_done")
        wo_full, wo_stat, wo_mv, wo_eps, wo_rstd, wo_free = (
            sem(n) for n in ("wo_full", "wo_stat", "wo_mv", "wo_eps", "wo_rstd", "wo_free"))
        yw_done, yb_done, x1_done = sem("yw_done"), sem("yb_done"), sem("x1_done")
        g_stat, g_mv, g_eps, g_rstd, x2_done = (sem(n) for n in ("g_stat", "g_mv", "g_eps", "g_rstd", "x2_done"))
        t_high = sem("t_high")
        w_high, w_low = sem("w_high"), sem("w_low")
        v_step = sem("v_step")
        score_full = sem("score_full")
        counted, totalled = sem("counted"), sem("totalled")
        eqT_full, eqT_copied, prefix_full = sem("eqT_full"), sem("eqT_copied"), sem("prefix_full")
        chosen_full, chosenT_copied, place_full = sem("chosen_full"), sem("chosenT_copied"), sem("place_full")
        tied_done, eq_done, chosen_done = sem("tied_done"), sem("eq_done"), sem("chosen_done")
        sig_done = sem("sig_done")
        gates_step = sem("gates_step")
        b1_full, b1_done = sem("b1_full"), sem("b1_done")
        hot_done, id_full, idx_done = sem("hot_done"), sem("id_full"), sem("idx_done")
        ext_full, ext_free = sem("ext_full"), sem("ext_free")
        ext_high = sem("ext_high")
        h_full, h_free, hid_done = sem("h_full"), sem("h_free"), sem("hid_done")
        hid_high = sem("hid_high")
        w1_high, w1_low, w2_high, w2_low = sem("w1_high"), sem("w1_low"), sem("w2_high"), sem("w2_low")
        carry_done = sem("carry_done")
        y_full, y_free, y_done = sem("y_full"), sem("y_free"), sem("y_done")
        v_exp, gate_sum = sem("v_exp"), sem("gate_sum")

        N_SMALL = 7
        block = stack.enter_context(nc.Block())

        wkv_raw = raw1[:, :].rearrange("p (k n) -> p k n", k=KD)
        wq_raw = raw2[:, 0:KD * INNER].rearrange("p (k n) -> p k n", k=KD)
        wo_raw = raw2[:, KD * INNER:KD * INNER + KI * D].rearrange("p (k n) -> p k n", k=KI)

        def pieces(n, width, flat=False):
            if flat:
                return lambda bank: bank[:, 0:n * width]
            return lambda bank: bank[:, 0:n * width].rearrange("p (c k) -> p c k", c=n)

        def products(out, lhs, rhs, first, last):
            for n, (a, b) in enumerate(((0, 0), (0, 1), (1, 0))):
                mm = nc.tensor.matmul(out, lhs(a), rhs(b), start=first and n == 0, stop=last and n == 2)
            return mm

        @block.sync
        def _(sp):
            def load_raw(slot, k):
                b, par, n = slot.at(k)
                wait_for(sp, z0_done, b - 1)
                wait_for(sp, xn_done, b - 1)
                sp.dma_start(ctx_in[:, par, :, :], ctx_1024[b].rearrange("(p r) d -> p r d", r=R)).then_inc(raw_in[par], 16)
                sp.dma_start(x_in[:, par, :], x[b]).then_inc(raw_in[par], 16)

            def load_res(slot, k):
                b, par, n = slot.at(k)
                wait_for(sp, x1_done, b - 1)
                sp.dma_start(x_res[:, par, :], x[b]).then_inc(res_in[par], 16)

            for par in range(2):
                sp.sem_inc(x1_out[par], 16)
                sp.sem_inc(x2_out[par], 16)

            start = Slot(0, 0, B)
            load_raw(start, 0)
            for n, row in enumerate((ln_x_w, ln_x_b)):
                sp.dma_start(ctx_w[:, n, :], row.partition_broadcast(P)).then_inc(rows_in, 16)
            for n, row in enumerate((ln_l_w, ln_l_b)):
                sp.dma_start(lat_w[:, n, :], row.partition_broadcast(P)).then_inc(rows_in, 16)
            sp.dma_start(wkv_raw, Wkv.rearrange("(k p) n -> p k n", p=P)).then_inc(wkv_in, 16)
            load_raw(start, 1)
            sp.dma_start(wq_raw, Wq.rearrange("(k p) n -> p k n", p=P)).then_inc(wq_in, 16)
            for n, row in enumerate((ln_o_w, ln_o_b)):
                sp.dma_start(o_w[:, n, :], row.partition_broadcast(P)).then_inc(small_in, 16)
            for n, g in enumerate((g_xattn, g_ffn)):
                sp.dma_start(gains[:, n:n + 1], g.partition_broadcast(P)).then_inc(small_in, 16)
            for n, s_ in enumerate((q_scale, k_scale)):
                for half in range(P // DH):
                    sp.dma_start(qk[half * DH:(half + 1) * DH, n:n + 1], s_.rearrange("(p o) -> p o", o=1)).then_inc(qk_in, 16)
            sp.dma_start(mask8[:, :], mask.rearrange("b m -> (b m)").partition_broadcast(S)).then_inc(mask_in, 16)
            sp.dma_start(wo_raw, Wo.rearrange("(k p) n -> p k n", p=P)).then_inc(wo_in, 16)
            sp.dma_start(wg[:, :, :], Wg.rearrange("(k p) n -> p k n", p=P)).then_inc(small_in, 16)
            sp.dma_start(b1_rows[:, :], b1.rearrange("e (k p) -> (e k) p", p=P)).then_inc(small_in, 16)
            sp.dma_start(b2_all[:, :, :], b2.partition_broadcast(S)).then_inc(small_in, 16)
            sp.dma_start(x_res[:, 0, :], x[0]).then_inc(res_in[0], 16)

            def do(slot):
                if slot.gate:
                    b, par, n = slot.at(-2)
                    wait_for(sp, x2_done, b + 1)
                    sp.dma_start(tokens.rearrange("(b t) d -> b t d", t=S)[b], x2[:, par, :]).then_inc(x2_out[par], 16)
                if slot.steady or 2 <= slot.s + 4 < B:
                    load_raw(slot, 4)
                if slot.tail:
                    b, par, n = slot.at(-1)
                    wait_for(sp, x1_done, b + 1)
                    sp.dma_start(out[b], x1[:, par, :]).then_inc(x1_out[par], 16)
                if slot.steady or 1 <= slot.s + 1 < B:
                    load_res(slot, 1)

            for slot in FIRST:
                do(slot)
            sp.wait_ge(w_low, 3)
            sp.dma_start(raw1[:, :].rearrange("p (k n) -> p k n", k=KD), W1[0].rearrange("(k p) n -> p k n", p=P)).then_inc(w1_in, 16)
            sp.dma_start(raw2[:, :].rearrange("p (k n) -> p k n", k=KF), W2[0].rearrange("(k p) n -> p k n", p=P)).then_inc(w2_in, 16)
            with sp.Fori(LOOP[0], LOOP[1] - 1) as half:
                for par in range(2):
                    do(Slot(half, par, B, steady=True))
            for slot in [Slot(B // 2 - 2, 0, B), Slot(B // 2 - 2, 1, B)] + LAST:
                do(slot)

            def load_expert(e):
                wait_for(sp, w1_low, e)
                sp.dma_start(raw1[:, :].rearrange("p (k n) -> p k n", k=KD), W1[e].rearrange("(k p) n -> p k n", p=P)).then_inc(w1_in, 16)
                wait_for(sp, w2_low, e)
                sp.dma_start(raw2[:, :].rearrange("p (k n) -> p k n", k=KF), W2[e].rearrange("(k p) n -> p k n", p=P)).then_inc(w2_in, 16)

            with sp.Fori(1, E) as e:
                load_expert(e)

        @block.gpsimd
        def _(pool):
            nc.gpsimd.iota(diff[:, :], [[1, P]], base=P, channel_multiplier=-1).then_inc(iota_done, 1)
            nc.gpsimd.memset(minus_half[:, :], -0.5)
            nc.gpsimd.memset(var_eps[:, :], 1.0).then_inc(pool_set, 1)
            nc.gpsimd.iota(slots_i[:, :], [[1, CAP]], base=1, channel_multiplier=0)
            nc.gpsimd.iota(ids_i[:, :], [[1, B], [0, E]], base=0, channel_multiplier=0)
            nc.gpsimd.iota(tok_i[:, :], [[0, B * E]], base=0, channel_multiplier=1).then_inc(iota_done, 1)
            pool.wait_ge(pool_set, 1)

            def do(slot):
                if slot.gate:
                    b, par, n = slot.at(-2)
                    wait_for(pool, g_mv, b + 1)
                    settle(pool)
                    nc.gpsimd.tensor_scalar(ve_g[:, :], mv_g[:, 1:2], LN_EPS, None, ALU.add).then_inc(g_eps, 1)
                    wait_for(pool, g_eps, b + 1)
                    nc.gpsimd.tensor_tensor(rstd_g[:, :], ve_g[:, :], minus_half[0:S, 0:1], ALU.pow).then_inc(g_rstd, 1)
                if slot.norm:
                    b, _, _ = slot.at(2)
                    wait_for(pool, mv_done, b + 1)
                    settle(pool)
                    nc.gpsimd.tensor_scalar(var_eps[0:CP, 0:R], mean_var[0:CP, 0:R, 1], LN_EPS, None, ALU.add)
                    nc.gpsimd.tensor_scalar(var_eps[0:S, R:R + 1], mean_var[0:S, R, 1:2], LN_EPS, None, ALU.add).then_inc(eps_done, 1)
                    wait_for(pool, eps_done, b + 1)
                    nc.gpsimd.tensor_tensor(rstd[:, :], var_eps[:, :], minus_half[:, 0:4], ALU.pow).then_inc(rstd_done, 1)

                def rnorms(m):
                    b, _, _ = slot.at(1)
                    rows = KR if m < KT else S
                    wait_for(pool, ss_done, 5 * b + m + 1)
                    settle(pool)
                    nc.gpsimd.tensor_scalar(ss_max[0:rows, m, :], ss[0:rows, m, :], L2_EPS ** 2, None, ALU.max).then_inc(max_done, 1)
                    wait_for(pool, max_done, 5 * b + m + 1)
                    nc.gpsimd.tensor_tensor(rnorm[0:rows, m, :], ss_max[0:rows, m, :], minus_half[0:rows, 0:H], ALU.pow).then_inc(rn_done, 1)

                def context_times():
                    b, _, _ = slot.at(2)
                    wait_for(pool, rows_in, 16 * 4)
                    wait_for(pool, z0_done, b + 1)
                    if slot.project:
                        for kc in range(KD):
                            wait_for(pool, t_full[t_bank_of(f"xT{kc}")], t_number(slot, f"xT{kc}"))
                    w_row = ctx_w[0:CP, 0:1, :].to_broadcast([CP, R, D])
                    nc.gpsimd.tensor_tensor(z[0:CP, 0:R, :], z0[0:CP, 0:R, :], w_row, ALU.mult).then_inc(zc_mul, 1)

                def context_plus():
                    b, _, _ = slot.at(2)
                    wait_for(pool, zc_mul, b + 1)
                    b_row = ctx_w[0:CP, 1:2, :].to_broadcast([CP, R, D])
                    nc.gpsimd.tensor_tensor(z[0:CP, 0:R, :], z[0:CP, 0:R, :], b_row, ALU.add).then_inc(zc_done, 1)

                def latents_rstd():
                    b, _, _ = slot.at(2)
                    wait_for(pool, mv2_done, b + 1)
                    settle(pool)
                    nc.gpsimd.tensor_scalar(var_eps2[0:S, :], mean_var2[0:S, 1:2], LN_EPS, None, ALU.add).then_inc(eps2_done, 1)
                    wait_for(pool, eps2_done, b + 1)
                    nc.gpsimd.tensor_tensor(rstd2[0:S, :], var_eps2[0:S, :], minus_half[0:S, 0:1], ALU.pow).then_inc(rstd2_done, 1)

                def latents_affine():
                    b, _, _ = slot.at(2)
                    wait_for(pool, z0x_done, b + 1)
                    nc.gpsimd.tensor_tensor(z[0:S, R, :], z0[0:S, R, :], lat_w[0:S, 0, :], ALU.mult).then_inc(zl_mul, 1)
                    wait_for(pool, zl_mul, b + 1)
                    nc.gpsimd.tensor_tensor(z[0:S, R, :], z[0:S, R, :], lat_w[0:S, 1, :], ALU.add).then_inc(zl_done, 1)

                def output_rstd():
                    b, par, n = slot.at(-1)
                    wait_for(pool, wo_mv, b + 1)
                    settle(pool)
                    nc.gpsimd.tensor_scalar(ve_o[:, :], mv_o[:, 1:2], LN_EPS, None, ALU.add).then_inc(wo_eps, 1)
                    wait_for(pool, wo_eps, b + 1)
                    nc.gpsimd.tensor_tensor(rstd_o[:, :], ve_o[:, :], minus_half[0:S, 0:1], ALU.pow).then_inc(wo_rstd, 1)

                def residual():
                    b, par, n = slot.at(-1)
                    wait_for(pool, wo_free, b + 1)
                    wait_for(pool, const_done, 2)
                    wait_for(pool, x1_out[par], 16 * (n + 1))
                    nc.gpsimd.tensor_tensor(x1[:, par, :], y_o[:, :], o_w[0:S, 0, :], ALU.mult).then_inc(yw_done, 1)
                    wait_for(pool, yw_done, b + 1)
                    nc.gpsimd.tensor_tensor(x1[:, par, :], x1[:, par, :], o_w[0:S, 1, :], ALU.add).then_inc(yb_done, 1)
                    wait_for(pool, yb_done, b + 1)
                    wait_for(pool, res_in[par], 16 * (n + 1))
                    nc.gpsimd.tensor_tensor(x1[:, par, :], x1[:, par, :], x_res[:, par, :], ALU.add).then_inc(x1_done, 1)

                if not slot.tail:
                    if slot.project:
                        for m in range(KT + 1):
                            rnorms(m)
                    if slot.norm:
                        if not slot.project:
                            latents_rstd()
                        context_times()
                        context_plus()
                        if slot.project:
                            latents_rstd()
                        latents_affine()
                    return
                if slot.project:
                    rnorms(0)
                    rnorms(1)
                if slot.norm:
                    context_times()
                if slot.project:
                    rnorms(2)
                if slot.norm:
                    context_plus()
                if slot.project:
                    rnorms(3)
                if slot.norm:
                    latents_rstd()
                output_rstd()
                if slot.project:
                    rnorms(4)
                if slot.norm:
                    latents_affine()
                residual()

            run_slots(pool, do)

            def gather(e, par, n):
                wait_for(pool, idx_done, e + 1)
                wait_for(pool, ext_full, 2 * (e - 1))
                settle(pool)
                for t in range(ST):
                    nc.gpsimd.indirect_dma_start(
                        ex[:, par, t, :], None, tokens[:, :],
                        bass.IndirectOffsetOnAxis(ap=idx[:, par, t:t + 1], axis=0),
                        bounds_check=TOK - 1).then_inc(ex_in[par], 16)

            def scatter(e, par, n):
                wait_for(pool, y_done, e + 1)
                if par:
                    wait_for(pool, y_out[0], 16 * ST * (n + 1))
                else:
                    wait_for(pool, y_out[1], 16 * ST * n)
                settle(pool)
                for t in range(ST):
                    nc.gpsimd.indirect_dma_start(
                        out_rows[:, :], bass.IndirectOffsetOnAxis(ap=idx_y[:, par, t:t + 1], axis=0),
                        y[:, par, t, :], None, bounds_check=TOK - 1,
                        compute_op=ALU.add).then_inc(y_out[par], 16)

            def lows(e, par):
                wait_for(pool, w1_high, e + 1)
                nc.gpsimd.tensor_tensor(w1[:, par, 1, :, :].rearrange("p k n -> p (k n)"), raw1[:, :],
                                        w1[:, par, 0, :, :].rearrange("p k n -> p (k n)").bitcast(F32),
                                        ALU.subtract).then_inc(w1_low, 1)
                wait_for(pool, w2_high, e + 1)
                nc.gpsimd.tensor_tensor(w2[:, par, 1, :, :].rearrange("p k n -> p (k n)"), raw2[:, :],
                                        w2[:, par, 0, :, :].rearrange("p k n -> p (k n)").bitcast(F32),
                                        ALU.subtract).then_inc(w2_low, 1)

            for bank in range(2):
                pool.wait_ge(t_free[bank], T_ALL[bank])
            lows(0, 0)
            steps = 0
            for part in range(3):
                if part == 0:
                    pool.wait_ge(sig_done, 1)
                    left = sig
                else:
                    pool.wait_ge(gates_step, steps)
                    nc.gpsimd.tensor_tensor(rest[:, :], left[:, :], carry[:, :, 1 + part], ALU.subtract).then_inc(gates_step, 1)
                    steps += 1
                    pool.wait_ge(gates_step, steps)
                    left = rest
                nc.gpsimd.tensor_copy(carry[:, :, 2 + part], left[:, :]).then_inc(gates_step, 1)
                steps += 1
            for par in range(2):
                pool.wait_ge(x2_out[par], 16 * (B // 2 + 1))
            gather(0, 0, 0)
            for par in range(2):
                pool.wait_ge(x1_out[par], 16 * (B // 2 + 1))
            gather(1, 1, 0)
            lows(1, 1)
            gather(2, 0, 1)
            scatter(0, 0, 0)
            lows(2, 0)
            with pool.Fori(1, E // 2 - 1) as n:
                gather(2 * n + 1, 1, n)
                scatter(2 * n - 1, 1, n - 1)
                lows(2 * n + 1, 1)
                gather(2 * n + 2, 0, n + 1)
                scatter(2 * n, 0, n)
                lows(2 * n + 2, 0)
            n = E // 2 - 1
            gather(2 * n + 1, 1, n)
            scatter(2 * n - 1, 1, n - 1)
            lows(2 * n + 1, 1)
            scatter(2 * n, 0, n)
            scatter(2 * n + 1, 1, n)
            for par in range(2):
                pool.wait_ge(y_out[par], 16 * ST * (E // 2))

        @block.scalar
        def _(act):
            act.wait_ge(wkv_in, 16)
            nc.scalar.activation(wkv[:, 0, :, :], wkv_raw, ACT.Copy).then_inc(w_high, 1)
            act.wait_ge(wq_in, 16)
            nc.scalar.activation(wq[:, 0, :, :], wq_raw, ACT.Copy).then_inc(w_high, 1)

            def small_products():
                act.wait_ge(small_in, 16 * N_SMALL)
                nc.scalar.activation(tanhs[:, :], gains[:, :], ACT.Tanh).then_inc(tanh_done, 1)
                act.wait_ge(wo_in, 16)
                nc.scalar.activation(wo[:, 0, :, :], wo_raw, ACT.Copy).then_inc(w_high, 1)

            def empty_t(slot, name, dst, cols):
                bank = t_bank_of(name)
                wait_for(act, t_full[bank], t_number(slot, name))
                nc.scalar.activation(dst, cols(bankT[bank]), ACT.Copy).then_inc(t_free[bank], 1)

            def high_t(slot, name, dst, cols, **kw):
                bank = t_bank_of(name)
                wait_for(act, t_full[bank], t_number(slot, name))
                nc.scalar.activation(dst, cols(bankT[bank]), ACT.Copy, **kw).then_inc(t_high, 1)

            def take_k(slot, m):
                b, _, _ = slot.at(1)
                rows = KR if m < KT else S
                wait_for(act, k_full, 5 * b + m + 1)
                wait_for(act, ss_done, 5 * b + (m - 1 if m else 0))
                nc.scalar.activation(sq[0:rows, m % 2, :], bankK[0:rows, 0:INNER], ACT.Square).then_inc(sq_done, 1)
                wait_for(act, kn_done, 5 * b + (m - 2 if m < 2 else m - 1 if m < KT else 0))
                nc.scalar.activation(kraw[0:rows, m % 2 if m < KT else 2, :], bankK[0:rows, 0:INNER], ACT.Copy).then_inc(k_free, 1)

            def empty_v(slot, t):
                b, par, _ = slot.at(1)
                wait_for(act, v_full, KT * b + t + 1)
                nc.scalar.activation(V[0:KR, par, t, :], bankV[0:KR, 0:INNER], ACT.Copy).then_inc(v_free, 1)

            def empty_k(slot, t):
                b, par, _ = slot.at(1)
                high_t(slot, f"kT{t}", kT[:, par, 0, :, t * KR:(t + 1) * KR], pieces(KI, KR))

            def exp(slot, h):
                b, par, _ = slot.at(0)
                wait_for(act, neg_done, H * b + h + 1)
                wait_for(act, p_full, H * b + h - 1)
                if h == 0:
                    wait_for(act, rden_done, b - 1)
                nc.scalar.activation(prob[:, h % 2, :], negs[:, h % 2, :], ACT.Exp, bias=least[:, h:h + 1],
                                     scale=-1.0, accum_out=den[:, par, h:h + 1]).then_inc(exp_done, 1)

            def empty_p(n, h):
                wait_for(act, p_full, n)
                wait_for(act, pv_done, n - 2)
                nc.scalar.activation(pT[0:KR, h % 2, :, :],
                                     bankP[0:KR, 0:KT * S].rearrange("p (t s) -> p t s", t=KT),
                                     ACT.Copy).then_inc(p_free, 1)

            def do(slot):
                for h in range(H):
                    if not slot.steady and slot.s == -1 and h == 1:
                        small_products()
                    if h == 0 and slot.project:
                        high_t(slot, "xT0", xT[:, 0, 0, 0:KEYS], pieces(1, KEYS, flat=True))
                    if h == 3 and slot.gate:
                        empty_t(slot, "x2T", x2T[:, :, :], pieces(KD, S))
                    if slot.project:
                        if h == 5:
                            empty_k(slot, 2)
                        if h == 6:
                            empty_k(slot, 3)
                        if h == 7:
                            b, par, _ = slot.at(1)
                            wait_for(act, qk_done, 1)
                            high_t(slot, "qT", qT[:, par, 0, :, :], pieces(KI, S), scale=qk_scale[:, 0:1])
                    if slot.heads:
                        exp(slot, h)
                    if slot.project:
                        if h == 2:
                            take_k(slot, 1)
                        if h == 3:
                            take_k(slot, 2)
                        if h == 4:
                            take_k(slot, 3)
                        if h == 5:
                            take_k(slot, 4)
                    if h == 4 and slot.gate:
                        b, _, _ = slot.at(-2)
                        empty_t(slot, "gate", logits[:, bass.ds(b * E, E)], lambda bank: bank[0:S, 0:E])
                    b, _, _ = slot.at(0)
                    if h == 0 and slot.tail:
                        empty_p(H * b, H - 1)
                    if h > 0 and slot.heads:
                        empty_p(H * b + h, h - 1)
                    if h == 3 and slot.tail:
                        high_t(slot, "oT", oT[:, 0, :, :], pieces(KI, S))
                    if slot.project:
                        if h == 0:
                            high_t(slot, "xT1", xT[:, 0, 1, 0:KEYS], pieces(1, KEYS, flat=True))
                        if h == 1:
                            take_k(slot, 0)
                            empty_v(slot, 0)
                        if h == 2:
                            empty_v(slot, 1)
                        if h == 3:
                            empty_k(slot, 0)
                        if h == 4:
                            empty_k(slot, 1)
                        if h == 6:
                            empty_v(slot, 2)
                        if h == 7:
                            empty_v(slot, 3)

            run_slots(act, do)

            for bank in range(2):
                act.wait_ge(t_free[bank], T_ALL[bank])
            nc.scalar.activation(sig[:, :], logits[:, :], ACT.Sigmoid).then_inc(sig_done, 1)

            def highs(e, par):
                wait_for(act, w1_in, 16 * (e + 1))
                wait_for(act, h_full, KF * (e - 1))
                nc.scalar.activation(w1[:, par, 0, :, :].rearrange("p k n -> p (k n)"), raw1[:, :], ACT.Copy).then_inc(w1_high, 1)
                wait_for(act, w2_in, 16 * (e + 1))
                wait_for(act, y_full, 2 * (e - 1))
                nc.scalar.activation(w2[:, par, 0, :, :].rearrange("p k n -> p (k n)"), raw2[:, :], ACT.Copy).then_inc(w2_high, 1)

            def high_ex(e):
                for kc in range(KD):
                    wait_for(act, ext_full, 2 * e + kc + 1)
                    nc.scalar.activation(exT[:, 0, kc, :], bankX[kc][:, 0:CAP], ACT.Copy).then_inc(ext_high, 1)

            def hidden(e):
                for f in range(KF):
                    wait_for(act, h_full, KF * e + f + 1)
                    wait_for(act, hid_done, KF * e + f - 1)
                    nc.scalar.activation(hid[:, f % 2, :], bankS[:, f % 2, 0:CAP], ACT.Gelu,
                                         bias=b1T[:, bass.ds(e * KF + f, 1)]).then_inc(h_free, 1)

            highs(0, 0)
            act.wait_ge(b1_full, 1)
            nc.scalar.activation(b1T[:, :], bankT[1][:, 0:E * KF], ACT.Copy).then_inc(b1_done, 1)
            act.wait_ge(b1_done, 1)
            high_ex(0)
            hidden(0)
            highs(1, 1)
            with act.Fori(0, E // 2 - 1) as n:
                for par in range(2):
                    high_ex(2 * n + 1 + par)
                    hidden(2 * n + 1 + par)
                    highs(2 * n + 2 + par, par)
            high_ex(E - 1)
            hidden(E - 1)

        @block.vector
        def _(dve):
            dve.wait_ge(iota_done, 1)
            nc.vector.tensor_scalar(ident[:, :], diff[:, :], float(P), None, ALU.is_equal)
            nc.vector.tensor_scalar(same[:, :], diff[:, :], E - 1, None, ALU.bitwise_and).then_inc(v_step, 1)
            nc.vector.memset(nm[:, :, M:KEYS], 0.0)
            nc.vector.memset(nm[:, :, KEYS:KP], MASKED)
            nc.vector.memset(xT[:, :, :, KEYS:KP].bitcast(F32), 0.0)
            nc.vector.memset(ones_b[:, :], 1.0)
            nc.vector.tensor_scalar(upto[:, :], diff[:, :], float(P), None, ALU.is_ge)
            nc.vector.tensor_scalar(before_e[:, :], diff[:, :], float(P), None, ALU.is_gt).then_inc(const_done, 1)
            n_steps = [1]

            def link(ins):
                n_steps[0] += 1
                ins.then_inc(v_step, 1)
                dve.wait_ge(v_step, n_steps[0])

            dve.wait_ge(v_step, 1)
            link(nc.vector.tensor_scalar(same_e[:, :], same[:, :], 0.0, None, ALU.is_equal))
            link(nc.vector.tensor_tensor(before_e[:, :], before_e[:, :], same_e[:, :], ALU.mult))
            link(nc.vector.tensor_copy(ident_b[:, :], ident[:, :]))
            dve.wait_ge(iota_done, 2)
            nc.vector.tensor_copy(slots16[:, :], slots_i[:, :])
            nc.vector.tensor_copy(carry[:, :, 0], ids_i[:, :])
            link(nc.vector.tensor_copy(carry[:, :, 1], tok_i[:, :]))

            def norm_begin(slot):
                b, par, n = slot.at(2)
                wait_for(dve, raw_in[par], 32 * (n + 1))
                for r in range(R):
                    nc.vector.bn_stats(stat[0:CP, r, :], ctx_in[:, par, r, :])
                nc.vector.bn_stats(stat[0:S, R, :], x_in[:, par, :]).then_inc(stat_done, 1)
                wait_for(dve, stat_done, b + 1)
                wait_for(dve, eps_done, b)
                settle(dve)
                for r in range(R):
                    nc.vector.bn_aggr(mean_var[0:CP, r, :], stat[0:CP, r, :])
                nc.vector.bn_aggr(mean_var[0:S, R, :], stat[0:S, R, :]).then_inc(mv_done, 1)

            def norm_rows(slot):
                b, par, n = slot.at(2)
                wait_for(dve, rstd_done, b + 1)
                wait_for(dve, zc_mul, b)
                nc.vector.tensor_scalar(xn[:, :], x_in[:, par, :], mean_var[0:S, R, 0:1], rstd[0:S, R:R + 1],
                                        ALU.subtract, ALU.mult).then_inc(xn_done, 1)
                for r in range(R):
                    last = nc.vector.tensor_scalar(z0[0:CP, r, :], ctx_in[:, par, r, :], mean_var[0:CP, r, 0:1],
                                                   rstd[0:CP, r:r + 1], ALU.subtract, ALU.mult)
                last.then_inc(z0_done, 1)
                wait_for(dve, xn_done, b + 1)
                nc.vector.bn_stats(stat2[0:S, :], xn[:, :]).then_inc(stat2_done, 1)

            def norm_again(slot):
                b, _, _ = slot.at(2)
                wait_for(dve, stat2_done, b + 1)
                wait_for(dve, eps2_done, b)
                settle(dve)
                nc.vector.bn_aggr(mean_var2[0:S, :], stat2[0:S, :]).then_inc(mv2_done, 1)

            def norm_end(slot):
                b, _, _ = slot.at(2)
                wait_for(dve, rstd2_done, b + 1)
                wait_for(dve, zl_mul, b)
                nc.vector.tensor_scalar(z0[0:S, R, :], xn[:, :], mean_var2[0:S, 0:1], rstd2[0:S, :],
                                        ALU.subtract, ALU.mult).then_inc(z0x_done, 1)

            def sum_squares(slot, m):
                b, _, _ = slot.at(1)
                rows = KR if m < KT else S
                wait_for(dve, sq_done, 5 * b + m + 1)
                wait_for(dve, max_done, 5 * (b - 1) + m + 1)
                nc.vector.tensor_reduce(ss[0:rows, m, :], sq[0:rows, m % 2, :].rearrange("p (h d) -> p h d", h=H),
                                        AX.X, ALU.add).then_inc(ss_done, 1)

            def unit(slot, m):
                b, _, _ = slot.at(1)
                rows = KR if m < KT else S
                wait_for(dve, rn_done, 5 * b + m + 1)
                src = kraw[0:rows, m % 2 if m < KT else 2, :].rearrange("p (h d) -> p h d", h=H)
                scale = rnorm[0:rows, m, :].unsqueeze(2).to_broadcast([rows, H, DH])
                if m < KT:
                    if m >= 2:
                        wait_for(dve, t_full[t_bank_of(f"kT{m - 2}")], t_number(slot, f"kT{m - 2}"))
                    dst = kn[0:rows, m % 2, :]
                else:
                    dst = qn[:, :]
                wait_for(dve, k_free, 5 * b + m + 1)
                nc.vector.tensor_tensor(dst.rearrange("p (h d) -> p h d", h=H), src, scale, ALU.mult).then_inc(kn_done, 1)

            def mask_row(slot):
                b, par, _ = slot.at(1)
                wait_for(dve, mask_in, 16)
                nc.vector.tensor_scalar(nm[:, par, 0:M].rearrange("s (r p) -> s r p", r=R),
                                        mask8[:, bass.ds(b * M, M)].rearrange("s (p r) -> s r p", r=R),
                                        0.0, MASKED, ALU.is_equal, ALU.mult).then_inc(nm_done, 1)

            def negated(slot, h):
                b, par, _ = slot.at(0)
                if h == 0:
                    wait_for(dve, nm_done, b + 1)
                wait_for(dve, s_full, H * b + h + 1)
                wait_for(dve, exp_done, H * b + h - 1)
                settle(dve)
                nc.vector.tensor_tensor_reduce(negs[:, h % 2, :], bankS[0:S, h % 2, 0:KP], nm[:, par, :], 1.0, MIN_START,
                                               ALU.add, ALU.min, least[:, h:h + 1]).then_inc(neg_done, 1)

            def divide(slot):
                b, par, _ = slot.at(-1)
                wait_for(dve, exp_done, H * (b + 1))
                nc.vector.reciprocal(rden[:, :], den[:, par, :]).then_inc(rden_done, 1)
                wait_for(dve, rden_done, b + 1)
                wait_for(dve, pv_done, H * (b + 1))
                if slot.s is not None and (slot.gate):
                    wait_for(dve, wo_full, b)
                nc.vector.tensor_tensor(on[:, :].rearrange("s (h d) -> s h d", h=H),
                                        bankO[0:S, 0:INNER].rearrange("s (h d) -> s h d", h=H),
                                        rden[:, :].unsqueeze(2).to_broadcast([S, H, DH]), ALU.mult).then_inc(on_done, 1)

            def out_stats(slot):
                b, _, _ = slot.at(-1)
                wait_for(dve, wo_full, b + 1)
                nc.vector.bn_stats(stat_o[:, :], bankV[0:S, 0:D]).then_inc(wo_stat, 1)
                wait_for(dve, wo_stat, b + 1)
                settle(dve)
                nc.vector.bn_aggr(mv_o[:, :], stat_o[:, :]).then_inc(wo_mv, 1)

            def out_norm(slot):
                b, _, _ = slot.at(-1)
                wait_for(dve, wo_rstd, b + 1)
                wait_for(dve, yw_done, b)
                nc.vector.tensor_scalar(y_o[:, :], bankV[0:S, 0:D], mv_o[:, 0:1], rstd_o[:, :],
                                        ALU.subtract, ALU.mult).then_inc(wo_free, 1)

            def gate_stats(slot):
                b, par, _ = slot.at(-2)
                wait_for(dve, x1_done, b + 1)
                nc.vector.bn_stats(stat_g[:, :], x1[:, par, :]).then_inc(g_stat, 1)
                wait_for(dve, g_stat, b + 1)
                settle(dve)
                nc.vector.bn_aggr(mv_g[:, :], stat_g[:, :]).then_inc(g_mv, 1)

            def gate_norm(slot):
                b, par, n = slot.at(-2)
                wait_for(dve, g_rstd, b + 1)
                wait_for(dve, x2_out[par], 16 * (n + 1))
                nc.vector.tensor_scalar(x2[:, par, :], x1[:, par, :], mv_g[:, 0:1], rstd_g[:, :],
                                        ALU.subtract, ALU.mult).then_inc(x2_done, 1)

            def low_t(slot, name, dst, cols, high, scale=None):
                bank = t_bank_of(name)
                wait_for(dve, t_high, high_number(slot, name))
                if scale is None:
                    nc.vector.tensor_tensor(dst, cols(bankT[bank]), high.bitcast(F32), ALU.subtract).then_inc(t_free[bank], 1)
                else:
                    nc.vector.scalar_tensor_tensor(out=dst, in0=cols(bankT[bank]), scalar=scale, in1=high.bitcast(F32),
                                                   op0=ALU.mult, op1=ALU.subtract).then_inc(t_free[bank], 1)

            def high_number(slot, name):
                names = [n for n in T_ORDER if n not in ("x2T", "gate") and n in t_present(slot, t_bank_of(n))]
                if slot.steady or 1 <= slot.s <= B - 1:
                    before = 14 + (slot.s - 1) * 8
                else:
                    before = 7 * (slot.s + 1) if slot.s < 1 else 14 + (B - 2) * 8 + (slot.s - B + 1)
                return before + names.index(name) + 1

            def low_x(slot, kc):
                low_t(slot, f"xT{kc}", xT[:, 1, kc, 0:KEYS], pieces(1, KEYS, flat=True), xT[:, 0, kc, 0:KEYS])

            def low_k(slot, t):
                b, par, _ = slot.at(1)
                cols = slice(t * KR, (t + 1) * KR)
                low_t(slot, f"kT{t}", kT[:, par, 1, :, cols], pieces(KI, KR), kT[:, par, 0, :, cols])

            def low_q(slot):
                b, par, _ = slot.at(1)
                low_t(slot, "qT", qT[:, par, 1, :, :], pieces(KI, S), qT[:, par, 0, :, :], scale=qk_scale[:, 0:1])

            def low_o(slot):
                low_t(slot, "oT", oT[:, 1, :, :], pieces(KI, S), oT[:, 0, :, :])

            def low_weights(n, parts, raw):
                dve.wait_ge(w_high, n + 1)
                nc.vector.tensor_tensor(parts[:, 1, :, :], raw, parts[:, 0, :, :].bitcast(F32), ALU.subtract).then_inc(w_low, 1)

            def small_products():
                dve.wait_ge(tanh_done, 1)
                dve.wait_ge(small_in, 16 * N_SMALL)
                nc.vector.tensor_scalar(o_w[:, :, :], o_w[:, :, :], tanhs[:, 0:1], None, ALU.mult).then_inc(const_done, 1)
                dve.wait_ge(w_high, 3)
                nc.vector.tensor_tensor(wo[:, 1, :, :], wo_raw, wo[:, 0, :, :].bitcast(F32), ALU.subtract).then_inc(w_low, 1)

            def do(slot):
                if not slot.steady and slot.s == -1:
                    dve.wait_ge(qk_in, 16 * 4)
                    nc.vector.tensor_scalar(qk_scale[:, :], qk[:, 0:1], qk[:, 1:2], -SCALE, ALU.mult, ALU.mult).then_inc(qk_done, 1)
                for h in range(H):
                    if not slot.steady and slot.s == -1 and h == 1:
                        small_products()
                    if not slot.steady and slot.s == -2 and h == 4:
                        low_weights(0, wkv, wkv_raw)
                    if not slot.steady and slot.s == -2 and h == 7:
                        low_weights(1, wq, wq_raw)
                    if slot.heads:
                        negated(slot, h)
                    if h == 0 and slot.project:
                        low_x(slot, 0)
                        low_x(slot, 1)
                    if h == 1:
                        if slot.gate:
                            gate_stats(slot)
                        if slot.norm:
                            norm_begin(slot)
                        if slot.project:
                            sum_squares(slot, 0)
                    if h == 2:
                        if slot.tail:
                            divide(slot)
                        if slot.gate:
                            gate_norm(slot)
                        if slot.project:
                            sum_squares(slot, 1)
                            unit(slot, 0)
                        if slot.norm:
                            norm_rows(slot)
                    if h == 3:
                        if slot.project:
                            unit(slot, 1)
                            sum_squares(slot, 2)
                        if slot.tail:
                            low_o(slot)
                        if slot.project:
                            low_k(slot, 0)
                        if slot.norm:
                            norm_again(slot)
                    if h == 4 and slot.project:
                        sum_squares(slot, 3)
                        unit(slot, 2)
                        low_k(slot, 1)
                    if h == 5:
                        if slot.tail:
                            out_stats(slot)
                        if slot.project:
                            low_k(slot, 2)
                            sum_squares(slot, 4)
                            unit(slot, 3)
                            mask_row(slot)
                        if slot.tail:
                            out_norm(slot)
                    if h == 6:
                        if slot.project:
                            unit(slot, 4)
                            low_k(slot, 3)
                        if slot.norm:
                            norm_end(slot)
                    if h == 7 and slot.project:
                        low_q(slot)

            run_slots(dve, do)

            for bank in range(2):
                dve.wait_ge(t_free[bank], T_ALL[bank])
            nc.vector.tensor_scalar(tied[:, :], logits[:, :], SIGMOID_ONE, 0.0, ALU.min, ALU.add).then_inc(tied_done, 1)
            dve.wait_ge(score_full, 1)
            link(nc.vector.tensor_copy(score[:, :], bankT[1][:, 0:S]))
            bits = score[:, :].bitcast(I32)
            link(nc.vector.tensor_scalar(fold[:, :], bits, 31, 0x7FFFFFFF, ALU.arith_shift_right, ALU.bitwise_and))
            link(nc.vector.tensor_tensor(key[:, :], bits, fold[:, :], ALU.bitwise_xor))
            nc.vector.tensor_scalar(half_i[:, 0, :], key[:, :], 16, None, ALU.arith_shift_right)
            link(nc.vector.tensor_scalar(half_i[:, 1, :], key[:, :], 0xFFFF, None, ALU.bitwise_and))
            nc.vector.tensor_scalar(hi_f[:, :], half_i[:, 0, :], HI_UNIT, None, ALU.mult)
            link(nc.vector.tensor_copy(lo_f[:, :], half_i[:, 1, :]))

            def search(values, start, unit, base):
                top = 2.0 ** (BITS - 2) * unit
                for n in range(TRIES):
                    nc.vector.memset(cand[:, n:n + 1], start + (n + 1) * top)
                    nc.vector.memset(tries[:, n:n + 1], (n + 1) * top)
                link(nc.vector.memset(step[:, :], top))
                first = n_steps[0]
                with dve.Fori(0, BITS // 4) as i:
                    for m in range(2):
                        with nc.allow_low_precision(reason="counts up to 112 are exact"):
                            for n in range(TRIES):
                                last = nc.vector.tensor_scalar(hit[:, n, :], values, cand[:, n:n + 1], None, ALU.is_ge,
                                                               ALU.add, accum_out=count[:, n:n + 1])
                            last.then_inc(counted, 1)
                        nc.vector.scalar_tensor_tensor(out=ahead[:, :], in0=tries[:, :], scalar=-0.75, in1=cand[:, :],
                                                       op0=ALU.mult, op1=ALU.add)
                        nc.vector.tensor_scalar(tries[:, :], tries[:, :], 0.25, None, ALU.mult)
                        dve.wait_ge(totalled, base + 2 * i + m + 1)
                        nc.vector.tensor_scalar(reached[:, :], bankO[:, 0:TRIES], float(CAP), None, ALU.is_ge, ALU.add,
                                                accum_out=passed[:, :]).then_inc(v_step, 1)
                        dve.wait_ge(v_step, first + 4 * i + 2 * m + 1)
                        nc.vector.scalar_tensor_tensor(out=cand[:, :], in0=step[:, :], scalar=passed[:, :], in1=ahead[:, :],
                                                       op0=ALU.mult, op1=ALU.add)
                        nc.vector.tensor_scalar(step[:, :], step[:, :], 0.25, None, ALU.mult).then_inc(v_step, 1)
                        dve.wait_ge(v_step, first + 4 * i + 2 * m + 2)
                n_steps[0] = first + BITS

            search(hi_f[:, :], -2.0 ** (BITS - 1) * HI_UNIT, HI_UNIT, 0)
            link(nc.vector.tensor_scalar(bound[:, :], cand[:, 0:1], -0.25 * HI_UNIT, None, ALU.add))
            link(nc.vector.scalar_tensor_tensor(out=lo_f[:, :], in0=hi_f[:, :], scalar=bound[:, :], in1=lo_f[:, :],
                                                op0=ALU.subtract, op1=ALU.add))
            search(lo_f[:, :], 0.0, 1.0, BITS // 2)
            link(nc.vector.tensor_scalar(bound[:, :], cand[:, 0:1], -0.25, None, ALU.add))
            with nc.allow_low_precision(reason="counts up to 112 are exact"):
                nc.vector.tensor_scalar(eq_b[:, :], lo_f[:, :], bound[:, :], None, ALU.is_equal, ALU.add,
                                        accum_out=eq_count[:, :]).then_inc(eq_done, 1)
                nc.vector.tensor_scalar(gt_b[:, :], lo_f[:, :], bound[:, :], None, ALU.is_gt, ALU.add,
                                        accum_out=gt_count[:, :]).then_inc(eq_done, 1)
            dve.wait_ge(eqT_full, 1)
            nc.vector.tensor_copy(eqT[:, :], bankP[0:S, 0:P // 2].bitcast(BF16)).then_inc(eqT_copied, 1)
            dve.wait_ge(prefix_full, 1)
            link(nc.vector.tensor_copy(earlier[:, :], bankO[:, 1:2]))
            link(nc.vector.tensor_scalar(need[:, :], bankO[:, 0:1], -1.0, float(CAP), ALU.mult, ALU.add))
            link(nc.vector.tensor_scalar(first_eq[:, :], bankS[:, 0, 0:S], earlier[:, :], need[:, :], ALU.add, ALU.is_le))
            link(nc.vector.tensor_tensor(first_eq[:, :], first_eq[:, :], eq_b[:, :], ALU.mult))
            link(nc.vector.tensor_tensor(first_eq[:, :], first_eq[:, :], gt_b[:, :], ALU.add))
            link(nc.vector.tensor_scalar(chosen[:, :], first_eq[:, :], 1.0, None, ALU.mult, ALU.add,
                                         accum_out=chosen_count[:, :]))
            nc.vector.tensor_scalar(before_c[:, :], before_e[:, :], chosen_count[:, :], None, ALU.mult).then_inc(chosen_done, 1)
            dve.wait_ge(chosen_full, 1)
            link(nc.vector.tensor_copy(chosenT[:, :], bankP[0:S, 0:P // 2].bitcast(BF16)))
            nc.vector.tensor_copy(first_eq[0:S, 0:1], chosenT[:, 0:1]).then_inc(chosenT_copied, 1)
            dve.wait_ge(place_full, 1)
            link(nc.vector.tensor_tensor(place[:, :], bankS[0:S, 0, 0:P], chosenT[:, :], ALU.mult))

            dve.wait_ge(gates_step, 5)

            def hot(e, par):
                wait_for(dve, id_full, e)
                nc.vector.tensor_copy(carry_e[:, par, :, :], carry[:, :, :].rearrange(
                    "s (b e) c -> s b (e c)", e=E)[:, :, bass.ds(e * 5, 5)]).then_inc(carry_done, 1)
                for b in range(B):
                    last = nc.vector.tensor_scalar(onehot[:, b, :], slots16[:, :], place[:, bass.ds(b * E + e, 1)],
                                                   None, ALU.is_equal)
                    if b % HOT == HOT - 1:
                        last.then_inc(hot_done, 1)

            def lows_ex(e):
                for kc in range(KD):
                    wait_for(dve, ext_high, 2 * e + kc + 1)
                    nc.vector.tensor_tensor(exT[:, 1, kc, :], bankX[kc][:, 0:CAP], exT[:, 0, kc, :].bitcast(F32),
                                            ALU.subtract).then_inc(ext_free, 1)

            def split_hidden(e):
                for f in range(KF):
                    wait_for(dve, h_free, KF * e + f + 1)
                    wait_for(dve, y_full, 2 * e)
                    nc.vector.tensor_copy(hidT[:, 0, f, :], hid[:, f % 2, :]).then_inc(hid_high, 1)
                    wait_for(dve, hid_high, KF * e + f + 1)
                    nc.vector.tensor_tensor(hidT[:, 1, f, :], hid[:, f % 2, :], hidT[:, 0, f, :].bitcast(F32),
                                            ALU.subtract).then_inc(hid_done, 1)

            def ids(e, par, n):
                wait_for(dve, id_full, e + 1)
                wait_for(dve, ex_in[par], 16 * ST * n)
                got = bankO[0:S, 0:8 * ST].rearrange("s (t c) -> s t c", c=8)
                nc.vector.tensor_copy(idx_f[:, :], got[:, :, 1])
                nc.vector.tensor_copy(gate_s[:, :], got[:, :, 2]).then_inc(v_exp, 1)
                wait_for(dve, v_exp, 2 * e + 1)
                nc.vector.scalar_tensor_tensor(out=idx[:, par, :], in0=got[:, :, 0], scalar=float(S), in1=idx_f[:, :],
                                               op0=ALU.mult, op1=ALU.add).then_inc(idx_done, 1)
                nc.vector.tensor_tensor(gate_s[:, :], got[:, :, 3], gate_s[:, :], ALU.add).then_inc(v_exp, 1)
                wait_for(dve, v_exp, 2 * e + 2)
                nc.vector.tensor_tensor(gate_v[:, par, :], got[:, :, 4], gate_s[:, :], ALU.add).then_inc(gate_sum, 1)
                wait_for(dve, gate_sum, 2 * e + 1)
                nc.vector.tensor_scalar(gate_v[:, par, :], gate_v[:, par, :], tanhs[0:S, 1:2], None, ALU.mult).then_inc(gate_sum, 1)

            def results(e, par, n):
                wait_for(dve, y_out[par], 16 * ST * n)
                nc.vector.tensor_copy(idx_y[:, par, :], idx[:, par, :])
                wait_for(dve, y_done, e)
                for half in range(2):
                    wait_for(dve, y_full, 2 * e + half + 1)
                    nc.vector.tensor_tensor(y_b[:, 2 * half:2 * half + 2, :],
                                            bankY[half][0:S, 0:2 * D].rearrange("s (t d) -> s t d", t=2),
                                            b2_all[:, bass.ds(e, 1), :].to_broadcast([S, 2, D]), ALU.add).then_inc(y_free, 1)
                wait_for(dve, y_free, 2 * e + 2)
                wait_for(dve, gate_sum, 2 * e + 2)
                for t in range(ST):
                    last = nc.vector.tensor_scalar(y[:, par, t, :], y_b[:, t, :], gate_v[:, par, t:t + 1], None, ALU.mult)
                last.then_inc(y_done, 1)

            def expert(e, par, n, more=2):
                split_hidden(e)
                if more:
                    lows_ex(e + 1)
                if more > 1:
                    hot(e + 2, par)
                results(e, par, n)
                if more > 1:
                    ids(e + 2, par, n + 1)

            hot(0, 0)
            ids(0, 0, 0)
            hot(1, 1)
            ids(1, 1, 0)
            lows_ex(0)
            for par in range(2):
                expert(par, par, 0)
            with dve.Fori(1, E // 2 - 1) as n:
                for par in range(2):
                    expert(2 * n + par, par, n)
            n = E // 2 - 1
            expert(2 * n, 0, n, more=1)
            expert(2 * n + 1, 1, n, more=0)

        @block.tensor
        def _(pe):
            pe.wait_ge(const_done, 1)

            def t_bank(slot, name):
                bank = t_bank_of(name)
                wait_for(pe, t_free[bank], t_number(slot, name) - 1)
                return bankT[bank], t_full[bank]

            def t_taken(slot, name):
                wait_for(pe, t_free[t_bank_of(name)], t_number(slot, name))

            def transpose_x(slot, kc):
                b, _, _ = slot.at(1)
                wait_for(pe, zc_done, b + 1)
                wait_for(pe, zl_done, b + 1)
                bank, full = t_bank(slot, f"xT{kc}")
                for r in range(R):
                    nc.tensor.transpose(bank[:, r * CP:(r + 1) * CP], z[0:CP, r, kc * P:(kc + 1) * P], ident[0:CP, 0:CP])
                nc.tensor.transpose(bank[:, M:KEYS], z[0:S, R, kc * P:(kc + 1) * P], ident[0:S, 0:S]).then_inc(full, 1)

            def keys(slot, t):
                b, _, _ = slot.at(1)
                for kc in range(KD):
                    t_taken(slot, f"xT{kc}")
                wait_for(pe, w_low, 1)
                wait_for(pe, k_free, 5 * b + t)
                for kc in range(KD):
                    last = products(bankK[0:KR, 0:INNER], lambda a: xT[:, a, kc, t * KR:(t + 1) * KR],
                                    lambda a: wkv[:, a, kc, 0:INNER], kc == 0, kc == KD - 1)
                last.then_inc(k_full, 1)

            def queries(slot):
                b, _, _ = slot.at(1)
                wait_for(pe, w_low, 2)
                wait_for(pe, k_free, 5 * b + KT)
                for kc in range(KD):
                    last = products(bankK[0:S, 0:INNER], lambda a: xT[:, a, kc, M:KEYS], lambda a: wq[:, a, kc, :],
                                    kc == 0, kc == KD - 1)
                last.then_inc(k_full, 1)

            def values(slot, t):
                b, _, _ = slot.at(1)
                if t != 2 or not slot.tail:
                    wait_for(pe, v_free, KT * b + t)
                else:
                    wait_for(pe, wo_free, b - 1)
                for kc in range(KD):
                    last = products(bankV[0:KR, 0:INNER], lambda a: xT[:, a, kc, t * KR:(t + 1) * KR],
                                    lambda a: wkv[:, a, kc, INNER:], kc == 0, kc == KD - 1)
                last.then_inc(v_full, 1)

            def transpose_k(slot, t):
                b, _, _ = slot.at(1)
                wait_for(pe, kn_done, 5 * b + t + 1)
                bank, full = t_bank(slot, f"kT{t}")
                for c in range(KI):
                    last = nc.tensor.transpose(bank[:, c * KR:(c + 1) * KR], kn[0:KR, t % 2, c * P:(c + 1) * P],
                                               ident[0:KR, 0:KR])
                last.then_inc(full, 1)

            def transpose_q(slot):
                b, _, _ = slot.at(1)
                wait_for(pe, kn_done, 5 * b + KT + 1)
                bank, full = t_bank(slot, "qT")
                for c in range(KI):
                    last = nc.tensor.transpose(bank[:, c * S:(c + 1) * S], qn[:, c * P:(c + 1) * P], ident[0:S, 0:S])
                last.then_inc(full, 1)

            def scores(slot, h):
                b, par, _ = slot.at(0)
                if h == 0:
                    for bank in range(2):
                        wait_for(pe, t_free[bank], t_before(slot, bank))
                wait_for(pe, neg_done, H * b + h - 1)
                r = DH * (h % 2)
                products(bankS[0:S, h % 2, 0:KP], lambda a: qT[r:r + DH, par, a, h // 2, :],
                         lambda a: kT[r:r + DH, par, a, h // 2, :], True, True).then_inc(s_full, 1)

            def transpose_p(n, h):
                wait_for(pe, exp_done, n)
                wait_for(pe, p_free, n - 1)
                for t in range(KT):
                    last = nc.tensor.transpose(bankP[0:KR, t * S:(t + 1) * S], prob[:, h % 2, t * KR:(t + 1) * KR],
                                               ident[0:S, 0:S])
                last.then_inc(p_full, 1)

            def attend(n, b, par, h):
                wait_for(pe, p_free, n)
                if h == 0:
                    wait_for(pe, on_done, b)
                    wait_for(pe, v_free, KT * (b + 1))
                for t in range(KT):
                    last = nc.tensor.matmul(bankO[0:S, h * DH:(h + 1) * DH], pT[0:KR, h % 2, t, :],
                                            V[0:KR, par, t, h * DH:(h + 1) * DH], start=(t == 0), stop=(t == KT - 1))
                last.then_inc(pv_done, 1)

            def transpose_o(slot):
                b, _, _ = slot.at(-1)
                wait_for(pe, on_done, b + 1)
                bank, full = t_bank(slot, "oT")
                for c in range(KI):
                    last = nc.tensor.transpose(bank[:, c * S:(c + 1) * S], on[:, c * P:(c + 1) * P], ident[0:S, 0:S])
                last.then_inc(full, 1)

            def project_out(slot):
                b, _, _ = slot.at(-1)
                wait_for(pe, w_low, 3)
                t_taken(slot, "oT")
                if slot.project:
                    wait_for(pe, v_free, KT * (b + 2) + 2)
                else:
                    wait_for(pe, v_free, KT * B)
                    wait_for(pe, wo_free, b)
                for c in range(KI):
                    last = products(bankV[0:S, 0:D], lambda a: oT[:, a, c, :], lambda a: wo[:, a, c, :],
                                    c == 0, c == KI - 1)
                last.then_inc(wo_full, 1)

            def transpose_x2(slot):
                b, par, _ = slot.at(-2)
                wait_for(pe, x2_done, b + 1)
                bank, full = t_bank(slot, "x2T")
                for kc in range(KD):
                    last = nc.tensor.transpose(bank[:, kc * S:(kc + 1) * S], x2[:, par, kc * P:(kc + 1) * P], ident[0:S, 0:S])
                last.then_inc(full, 1)

            def gate_logits(slot):
                wait_for(pe, small_in, 16 * N_SMALL)
                t_taken(slot, "x2T")
                bank, full = t_bank(slot, "gate")
                for kc in range(KD):
                    last = nc.tensor.matmul(bank[0:S, 0:E], x2T[:, kc, :], wg[:, kc, :], start=(kc == 0), stop=(kc == KD - 1))
                last.then_inc(full, 1)

            def do(slot):
                for h in range(H):
                    b, par, _ = slot.at(0)
                    if slot.heads:
                        scores(slot, h)
                    if slot.project and h == 0:
                        transpose_x(slot, 0)
                    if h == 3 and slot.gate:
                        transpose_x2(slot)
                    if slot.project:
                        if h == 2:
                            keys(slot, 1)
                        if h == 3:
                            keys(slot, 2)
                        if h == 4:
                            keys(slot, 3)
                        if h == 5:
                            transpose_k(slot, 2)
                            queries(slot)
                        if h == 6:
                            transpose_k(slot, 3)
                        if h == 7:
                            transpose_q(slot)
                    if h == 4 and slot.gate:
                        gate_logits(slot)
                    if h == 0 and slot.tail:
                        transpose_p(H * b, H - 1)
                    if h > 0 and slot.heads:
                        transpose_p(H * b + h, h - 1)
                    if h < 2 and slot.tail:
                        b1_, par1, _ = slot.at(-1)
                        attend(H * b - 1 + h, b1_, par1, H - 2 + h)
                    if h >= 2 and slot.heads:
                        attend(H * b + h - 1, b, par, h - 2)
                    if h == 3 and slot.tail:
                        transpose_o(slot)
                    if slot.project:
                        if h == 0:
                            transpose_x(slot, 1)
                        if h == 1:
                            keys(slot, 0)
                            values(slot, 0)
                        if h == 2:
                            values(slot, 1)
                        if h == 3:
                            transpose_k(slot, 0)
                        if h == 4:
                            transpose_k(slot, 1)
                    if h == 4 and slot.tail:
                        project_out(slot)
                    if slot.project:
                        if h == 6:
                            values(slot, 2)
                        if h == 7:
                            values(slot, 3)

            run_slots(pe, do)

            pe.wait_ge(tied_done, 1)
            nc.tensor.transpose(bankT[1][:, 0:S], tied[:, :], ident[0:S, 0:S]).then_inc(score_full, 1)
            with pe.Fori(0, BITS) as i:
                pe.wait_ge(counted, i + 1)
                nc.tensor.matmul(bankO[:, 0:TRIES], same_e[:, :], count[:, :], start=True, stop=True).then_inc(totalled, 1)
            pe.wait_ge(eq_done, 1)
            nc.tensor.transpose(bankP[0:S, 0:P // 2].bitcast(BF16), eq_b[:, :], ident_b[:, :]).then_inc(eqT_full, 1)
            pe.wait_ge(eq_done, 2)
            nc.tensor.matmul(bankO[:, 0:1], same_e[:, :], gt_count[:, :], start=True, stop=True)
            nc.tensor.matmul(bankO[:, 1:2], before_e[:, :], eq_count[:, :], start=True, stop=True)
            pe.wait_ge(eqT_copied, 1)
            nc.tensor.matmul(bankS[:, 0, 0:S], eqT[:, :], upto[0:S, 0:S], start=True, stop=True).then_inc(prefix_full, 1)
            pe.wait_ge(chosen_done, 1)
            nc.tensor.transpose(bankP[0:S, 0:P // 2].bitcast(BF16), chosen[:, :], ident_b[:, :]).then_inc(chosen_full, 1)
            pe.wait_ge(chosenT_copied, 1)
            nc.tensor.matmul(bankS[0:S, 0, 0:P], upto[0:S, 0:S], chosenT[:, :], start=True, stop=False)
            nc.tensor.matmul(bankS[0:S, 0, 0:P], ones_b[:, :], before_c[:, :], start=False, stop=True).then_inc(place_full, 1)
            nc.tensor.transpose(bankT[1][:, 0:E * KF], b1_rows[:, :], ident[0:E * KF, 0:E * KF]).then_inc(b1_full, 1)

            def find(e, par):
                wait_for(pe, carry_done, e + 1)
                wait_for(pe, gate_sum, 2 * e)
                for b in range(B):
                    if b % HOT == 0:
                        wait_for(pe, hot_done, e * (B // HOT) + b // HOT + 1)
                    for t in range(ST):
                        last = nc.tensor.matmul(bankO[0:S, 8 * t:8 * t + 5], onehot[:, b, t * S:(t + 1) * S],
                                                carry_e[:, par, b, :], start=(b == 0 and t == 0), stop=(b == B - 1),
                                                skip_group_check=True)
                last.then_inc(id_full, 1)

            def transpose_ex(e, par, n):
                wait_for(pe, ex_in[par], 16 * ST * (n + 1))
                wait_for(pe, ext_free, 2 * e)
                for kc in range(KD):
                    for t in range(ST):
                        last = nc.tensor.transpose(bankX[kc][:, t * S:(t + 1) * S], ex[:, par, t, kc * P:(kc + 1) * P],
                                                   ident[0:S, 0:S])
                    last.then_inc(ext_full, 1)

            def expert_in(e, par, n):
                wait_for(pe, w1_low, e + 1)
                wait_for(pe, ext_free, 2 * (e + 1))
                for f in range(KF):
                    wait_for(pe, h_free, KF * e + f - 1)
                    for kc in range(KD):
                        last = products(bankS[:, f % 2, 0:CAP], lambda a: w1[:, par, a, kc, f * P:(f + 1) * P],
                                        lambda a: exT[:, a, kc, :], kc == 0, kc == KD - 1)
                    last.then_inc(h_full, 1)

            def expert_out(e, par, n):
                wait_for(pe, w2_low, e + 1)
                for half in range(2):
                    wait_for(pe, y_free, 2 * (e - 1) + half + 1)
                    for t in range(2):
                        rows = (2 * half + t) * S
                        for f in range(KF):
                            if half == 0 and t == 0:
                                wait_for(pe, hid_done, KF * e + f + 1)
                            last = products(bankY[half][0:S, t * D:(t + 1) * D], lambda a: hidT[:, a, f, rows:rows + S],
                                            lambda a: w2[:, par, a, f, :], f == 0, f == KF - 1)
                    last.then_inc(y_full, 1)

            find(0, 0)
            find(1, 1)
            transpose_ex(0, 0, 0)

            def expert(e, par, n, more=2):
                expert_in(e, par, n)
                if more:
                    transpose_ex(e + 1, 1 - par, n + par)
                expert_out(e, par, n)
                if more > 1:
                    find(e + 2, par)

            for par in range(2):
                expert(par, par, 0)
            with pe.Fori(1, E // 2 - 1) as n:
                for par in range(2):
                    expert(2 * n + par, par, n)
            expert(E - 2, 0, E // 2 - 1, more=1)
            expert(E - 1, 1, E // 2 - 1, more=0)


_INS = ['x', 'ctx_1024', 'mask_BxS2_bk0', 'g_xattn', 'g_ffn', 'L0_xattn_ln_x_w', 'L0_xattn_ln_x_b',
        'L0_xattn_ln_l_w', 'L0_xattn_ln_l_b', 'L0_xattn_Wq', 'L0_xattn_Wkv', 'L0_xattn_q_scale',
        'L0_xattn_k_scale', 'L0_xattn_Wo', 'L0_xattn_ln_o_w', 'L0_xattn_ln_o_b', 'L0_ffn_Wg', 'L0_ffn_W1',
        'L0_ffn_b1', 'L0_ffn_W2', 'L0_ffn_b2']
_OUTS = [((16, 112, 256), 'float32')]


def kernel(**inputs):
    import numpy as _np
    import concourse.bacc as _bacc
    from concourse import mybir as _mybir
    from concourse.bass_utils import run_bass_kernel_spmd as _run

    nc = _bacc.Bacc("TRN2", target_bir_lowering=False, num_devices=1)
    arrays, args = {}, []
    for name in _INS:
        a = _np.ascontiguousarray(inputs[name])
        arrays[f"in_{name}_dram"] = a
        args.append(nc.dram_tensor(f"in_{name}_dram", a.shape, _mybir.dt.from_np(a.dtype), kind="ExternalInput").ap())
    for i, (shape, dtype) in enumerate(_OUTS):
        dt = _mybir.dt.from_np(_np.dtype(dtype))
        args.append(nc.dram_tensor(f"out_{i}_dram", shape, dt, kind="ExternalOutput").ap())
    flamingo_block_kernel(nc, *args)
    r = _run(nc, [arrays], core_ids=[0])
    got = tuple(r.results[0][f"out_{i}_dram"] for i in range(len(_OUTS)))
    return got[0]
```

```python
from contextlib import ExitStack

import concourse.bass as bass
from concourse import mybir

ALU = mybir.AluOpType
ACT = mybir.ActivationFunctionType
AX = mybir.AxisListType
F32 = mybir.dt.float32
F32R = mybir.dt.float32r
BF16 = mybir.dt.bfloat16
F16 = mybir.dt.float16
I32 = mybir.dt.int32
U32 = mybir.dt.uint32
U8 = mybir.dt.uint8

P = 128
LN_EPS = 1e-5
L2_EPS = 1e-12
SCALE = 8.0
MASKED = 1e30
MIN_START = 3e38
SIGMOID_ONE = 17.328680
HI_UNIT = 2.0 ** 17


class Slot:

    def __init__(self, half, par, batches, steady=False):
        self.half, self.par, self.steady = half, par, steady
        self.s = s = 2 * half + par
        self.norm = steady or 0 <= s + 2 < batches
        self.project = steady or 0 <= s + 1 < batches
        self.heads = steady or 0 <= s < batches
        self.tail = steady or 0 <= s - 1 < batches
        self.gate = steady or 0 <= s - 2 < batches

    def at(self, k):
        return self.s + k, (self.par + k) % 2, self.half + (self.par + k) // 2


def flamingo_block_kernel(
    nc, x, ctx_1024, mask, g_xattn, g_ffn, ln_x_w, ln_x_b, ln_l_w, ln_l_b, Wq, Wkv, q_scale, k_scale,
    Wo, ln_o_w, ln_o_b, Wg, W1, b1, W2, b2, out,
):
    B, S, D = x.shape
    M = ctx_1024.shape[1]
    DH = q_scale.shape[0]
    INNER = Wq.shape[1]
    H = INNER // DH
    E, _, FF = W1.shape
    KD = D // P
    KI = INNER // P
    KF = FF // P
    R = 3
    CP = M // R
    KEYS = M + S
    KT = 4
    KR = (KEYS + KT - 1) // KT
    KP = KR * KT
    TOK = B * S
    CAP = TOK * 2 // E
    ST = CAP // S
    HOT = 4
    TRIES = 3
    BITS = 16
    assert CP * R == M and ST * S == CAP and B * E == P and KEYS < 512

    tokens = nc.dram_tensor("tokens_scratch", [TOK, D], F32).ap()
    out_rows = out.rearrange("b t d -> (b t) d")

    T_ORDER = ("kT0", "oT", "kT1", "kT2", "kT3", "qT", "x2T", "gate", "xT0", "xT1")
    V_FIRST = 3

    def t_bank_of(name):
        return T_ORDER.index(name) % 2

    def t_present(slot, bank):
        return [n for n in T_ORDER[bank::2]
                if (slot.tail if n == "oT" else slot.gate if n in ("x2T", "gate")
                    else slot.norm if n in ("xT0", "xT1") else slot.project)]

    FIRST = [Slot(-1, 0, B), Slot(-1, 1, B), Slot(0, 0, B), Slot(0, 1, B)]
    LOOP = (1, B // 2 - 1)
    LAST = [Slot(B // 2 - 1, 0, B), Slot(B // 2 - 1, 1, B), Slot(B // 2, 0, B), Slot(B // 2, 1, B)]

    def t_before(slot, bank):
        start = sum(len(t_present(s, bank)) for s in FIRST)
        if slot.steady or 2 <= slot.s <= B - 2:
            return start + (slot.s - 2) * (len(T_ORDER) // 2)
        if slot.s < 2:
            return sum(len(t_present(s, bank)) for s in FIRST if s.s < slot.s)
        return start + sum(len(t_present(Slot(s // 2, s % 2, B), bank)) for s in range(2, slot.s))

    def t_number(slot, name):
        bank = t_bank_of(name)
        return t_before(slot, bank) + t_present(slot, bank).index(name) + 1

    def highs_present(slot):
        return [n for n in T_ORDER if n not in ("x2T", "gate") and n in t_present(slot, t_bank_of(n))]

    def high_number(slot, name):
        if slot.steady or 2 <= slot.s <= B - 2:
            before = sum(len(highs_present(s)) for s in FIRST) + (slot.s - 2) * 8
        else:
            before = sum(len(highs_present(Slot(s // 2, s % 2, B))) for s in range(-2, slot.s))
        return before + highs_present(slot).index(name) + 1

    T_ALL = [t_before(Slot(B // 2 + 1, 0, B), bank) for bank in range(2)]

    def wait_for(eng, sem, count):
        if isinstance(count, int) and count <= 0:
            return
        eng.wait_ge(sem, count)

    def run_slots(eng, do):
        for slot in FIRST:
            do(slot)
        with eng.Fori(*LOOP) as half:
            for par in range(2):
                do(Slot(half, par, B, steady=True))
        for slot in LAST:
            do(slot)

    with ExitStack() as stack:
        def sb(name, shape, dt=F32):
            return stack.enter_context(nc.sbuf_tensor(name, shape, dt))

        def ps(name, shape, dt=F32):
            return stack.enter_context(nc.psum_tensor(name, shape, dt))

        def sem(name):
            return stack.enter_context(nc.semaphore(name))

        diff = sb("diff", [P, P], I32)
        same = sb("same", [P, P], I32)
        ident = sb("ident", [P, P])
        ident_b = sb("ident_b", [P, P], BF16)
        same_e = sb("same_e", [P, P], BF16)
        before_e = sb("before_e", [P, P], BF16)
        upto = sb("upto", [P, P], BF16)
        ones_b = sb("ones_b", [P, S], BF16)
        minus_half = sb("minus_half", [P, 8])
        raw1 = sb("raw1", [P, KD * FF])
        raw2 = sb("raw2", [P, KF * D])
        wg = sb("wg", [P, KD, E])
        gains = sb("gains", [P, 2])
        tanhs = sb("tanhs", [P, 2])
        qk = sb("qk", [P, 2])
        qk_scale = sb("qk_scale", [P, 1])
        b1_rows = sb("b1_rows", [E * KF, P])
        b1T = sb("b1T", [P, E * KF])
        logits = sb("logits", [S, B * E])
        x1 = sb("x1", [S, 2, D])
        x2 = sb("x2", [S, 2, D])
        carry = sb("carry", [S, P, 5], BF16)
        ids_i = sb("ids_i", [S, B * E], I32)
        tok_i = sb("tok_i", [S, B * E], I32)
        slots_i = sb("slots_i", [S, CAP], I32)
        slots16 = sb("slots16", [S, CAP], F16)

        persistent = stack
        stack = persistent.enter_context(ExitStack())
        wkv = sb("wkv", [P, 2, KD, 2 * INNER], F32R)
        wq = sb("wq", [P, 2, KD, INNER], F32R)
        wo = sb("wo", [P, 2, KI, D], F32R)
        ctx_w = sb("ctx_w", [P, 2, D])
        lat_w = sb("lat_w", [P, 2, D])
        o_w = sb("o_w", [P, 2, D])
        mask8 = sb("mask8", [S, B * M], U8)
        ctx_in = sb("ctx_in", [CP, 2, R, D])
        x_in = sb("x_in", [S, 2, D])
        x_res = sb("x_res", [S, 2, D])
        stat = sb("stat", [P, 4, 6])
        mean_var = sb("mean_var", [P, 4, 2])
        var_eps = sb("var_eps", [P, 4])
        rstd = sb("rstd", [P, 4])
        stat2 = sb("stat2", [P, 6])
        mean_var2 = sb("mean_var2", [P, 2])
        var_eps2 = sb("var_eps2", [P, 1])
        rstd2 = sb("rstd2", [P, 1])
        z0 = sb("z0", [P, 4, D])
        xn = sb("xn", [S, D])
        z = sb("z", [P, 4, D])
        xT = sb("xT", [P, 2, 2, KD, KP], F32R)
        sq = sb("sq", [P, 2, INNER])
        ss = sb("ss", [P, 5, H])
        ss_max = sb("ss_max", [P, 5, H])
        rnorm = sb("rnorm", [P, 5, H])
        kraw = sb("kraw", [P, 2, INNER])
        kn = sb("kn", [P, 2, INNER])
        qn = sb("qn", [S, INNER])
        kT = sb("kT", [P, 2, 2, KI, KP], F32R)
        qT = sb("qT", [P, 2, 2, KI, S], F32R)
        qT_low = sb("qT_low", [P, 2, KI, S], F32R)
        V = sb("V", [P, 2, KT, INNER])
        nm = sb("nm", [S, 2, KP])
        negs = sb("negs", [S, 2, KP])
        least = sb("least", [S, H])
        prob = sb("prob", [S, 2, KP])
        den = sb("den", [S, 2, H])
        rden = sb("rden", [S, H])
        pT = sb("pT", [P, 2, KT, S])
        on = sb("on", [S, INNER])
        oT = sb("oT", [P, 2, KI, S], F32R)
        stat_o = sb("stat_o", [S, 6])
        mv_o = sb("mv_o", [S, 2])
        ve_o = sb("ve_o", [S, 1])
        rstd_o = sb("rstd_o", [S, 1])
        y_o = sb("y_o", [S, D])
        stat_g = sb("stat_g", [S, 6])
        mv_g = sb("mv_g", [S, 2])
        ve_g = sb("ve_g", [S, 1])
        rstd_g = sb("rstd_g", [S, 1])
        x2T = sb("x2T", [P, KD, S])
        stack.close()
        stack = persistent

        tied = sb("tied", [S, B * E])
        score = sb("score", [P, S])
        fold = sb("fold", [P, S], I32)
        key = sb("key", [P, S], I32)
        half_i = sb("half_i", [P, 2, S], I32)
        hi_f = sb("hi_f", [P, S])
        lo_f = sb("lo_f", [P, S])
        hit = sb("hit", [P, TRIES, S])
        cand = sb("cand", [P, TRIES])
        ahead = sb("ahead", [P, TRIES])
        tries = sb("tries", [P, TRIES])
        step = sb("step", [P, TRIES])
        passed = sb("passed", [P, 1])
        reached = sb("reached", [P, TRIES])
        count = sb("count", [P, TRIES], BF16)
        bound = sb("bound", [P, 1])
        earlier = sb("earlier", [P, 1])
        gt_b = sb("gt_b", [P, S], BF16)
        eq_b = sb("eq_b", [P, S], BF16)
        eq_count = sb("eq_count", [P, 1], BF16)
        gt_count = sb("gt_count", [P, 1], BF16)
        first_eq = sb("first_eq", [P, S])
        chosen = sb("chosen", [P, S], BF16)
        chosen_count = sb("chosen_count", [P, 1])
        before_c = sb("before_c", [P, P], BF16)
        eqT = sb("eqT", [S, P], BF16)
        chosenT = sb("chosenT", [S, P], BF16)
        place = sb("place", [S, P])
        sig = sb("sig", [S, P])
        rest = sb("rest", [S, P])
        b2_all = sb("b2_all", [S, E, D])
        onehot = sb("onehot", [S, B, CAP], BF16)
        carry_e = sb("carry_e", [S, 2, B, 5], BF16)
        idx_f = sb("idx_f", [S, ST])
        idx = sb("idx", [S, 2, ST], I32)
        idx_y = sb("idx_y", [S, 2, ST], I32)
        gate_s = sb("gate_s", [S, ST])
        gate_v = sb("gate_v", [S, 2, ST])
        ex = sb("ex", [S, 2, ST, D])
        exT = sb("exT", [P, 2, KD, CAP], F32R)
        w1 = sb("w1", [P, 2, 2, KD, FF], F32R)
        w2 = sb("w2", [P, 2, 2, KF, D], F32R)
        hid = sb("hid", [P, 2, CAP])
        hidT = sb("hidT", [P, 2, KF, CAP], F32R)
        y_b = sb("y_b", [S, ST, D])
        y = sb("y", [S, 2, ST, D])

        bankS = ps("bankS", [P, 2, 512])
        bankP = ps("bankP", [P, 512])
        bankT = [ps("bankT0", [P, 512]), ps("bankT1", [P, 512])]
        bankK = ps("bankK", [P, 512])
        bankV = ps("bankV", [P, 512])
        bankO = ps("bankO", [P, 512])
        bankY = (bankK, bankV)
        bankX = (bankP, bankT[0])

        raw_in = [sem("raw_in0"), sem("raw_in1")]
        res_in = [sem("res_in0"), sem("res_in1")]
        small_in = sem("small_in")
        qk_in = sem("qk_in")
        wkv_in, wq_in, wo_in = sem("wkv_in"), sem("wq_in"), sem("wo_in")
        mask_in = sem("mask_in")
        x1_out = [sem("x1_out0"), sem("x1_out1")]
        x2_out = [sem("x2_out0"), sem("x2_out1")]
        w1_in, w2_in = sem("w1_in"), sem("w2_in")
        rows_in = sem("rows_in")
        b2_in = sem("b2_in")
        ex_in = [sem("ex_in0"), sem("ex_in1")]
        y_out = [sem("y_out0"), sem("y_out1")]
        iota_done = sem("iota_done")

        waited = sem("waited")

        def settle(eng):
            eng.sem_inc(waited, 1)

        const_done = sem("const_done")
        pool_set = sem("pool_set")
        tanh_done = sem("tanh_done")
        qk_done = sem("qk_done")
        stat_done, mv_done, rstd_done = sem("stat_done"), sem("mv_done"), sem("rstd_done")
        xn_done, z0_done = sem("xn_done"), sem("z0_done")
        stat2_done, mv2_done, rstd2_done, z0x_done = sem("stat2_done"), sem("mv2_done"), sem("rstd2_done"), sem("z0x_done")
        eps_done, eps2_done = sem("eps_done"), sem("eps2_done")
        zc_mul, zc_done, zl_mul, zl_done = sem("zc_mul"), sem("zc_done"), sem("zl_mul"), sem("zl_done")
        t_full, t_free = [sem("t_full0"), sem("t_full1")], [sem("t_free0"), sem("t_free1")]
        k_full, k_free = sem("k_full"), sem("k_free")
        kn_done = sem("kn_done")
        sq_done, ss_done, max_done, rn_done = sem("sq_done"), sem("ss_done"), sem("max_done"), sem("rn_done")
        v_full, v_free = sem("v_full"), sem("v_free")
        nm_done = sem("nm_done")
        s_full, neg_done, exp_done = sem("s_full"), sem("neg_done"), sem("exp_done")
        p_full, p_free = sem("p_full"), sem("p_free")
        pv_done = sem("pv_done")
        rden_done, on_done = sem("rden_done"), sem("on_done")
        wo_full, wo_stat, wo_mv, wo_eps, wo_rstd, wo_free = (
            sem(n) for n in ("wo_full", "wo_stat", "wo_mv", "wo_eps", "wo_rstd", "wo_free"))
        yw_done, yb_done, x1_done = sem("yw_done"), sem("yb_done"), sem("x1_done")
        g_stat, g_mv, g_eps, g_rstd, x2_done = (sem(n) for n in ("g_stat", "g_mv", "g_eps", "g_rstd", "x2_done"))
        t_high = sem("t_high")
        q_twice = sem("q_twice")
        w_high, w_low = sem("w_high"), sem("w_low")
        v_step = sem("v_step")
        score_full = sem("score_full")
        counted, totalled = sem("counted"), sem("totalled")
        eqT_full, eqT_copied, prefix_full = sem("eqT_full"), sem("eqT_copied"), sem("prefix_full")
        chosen_full, chosenT_copied, place_full = sem("chosen_full"), sem("chosenT_copied"), sem("place_full")
        tied_done, eq_done, chosen_done = sem("tied_done"), sem("eq_done"), sem("chosen_done")
        sig_done = sem("sig_done")
        gates_step = sem("gates_step")
        b1_full, b1_done = sem("b1_full"), sem("b1_done")
        hot_done, id_full, idx_done = sem("hot_done"), sem("id_full"), sem("idx_done")
        ext_full, ext_free = sem("ext_full"), sem("ext_free")
        ext_high = sem("ext_high")
        h_full, h_free, hid_done = sem("h_full"), sem("h_free"), sem("hid_done")
        hid_high = sem("hid_high")
        w1_high, w1_low, w2_high, w2_low = sem("w1_high"), sem("w1_low"), sem("w2_high"), sem("w2_low")
        carry_done = sem("carry_done")
        y_full, y_free, y_done = sem("y_full"), sem("y_free"), sem("y_done")
        v_exp, gate_sum = sem("v_exp"), sem("gate_sum")

        N_SMALL = 6
        block = stack.enter_context(nc.Block())

        wkv_raw = raw1[:, :].rearrange("p (k n) -> p k n", k=KD)
        wq_raw = raw2[:, 0:KD * INNER].rearrange("p (k n) -> p k n", k=KD)
        wo_raw = raw2[:, KD * INNER:KD * INNER + KI * D].rearrange("p (k n) -> p k n", k=KI)

        SIDES = (slice(0, DH), slice(DH, P))

        def pieces(n, width, flat=False):
            if flat:
                return lambda bank: bank[:, 0:n * width]
            return lambda bank: bank[:, 0:n * width].rearrange("p (c k) -> p c k", c=n)

        def products(out, lhs, rhs, first, last):
            for n, (a, b) in enumerate(((0, 0), (0, 1), (1, 0))):
                mm = nc.tensor.matmul(out, lhs(a), rhs(b), start=first and n == 0, stop=last and n == 2)
            return mm

        @block.sync
        def _(sp):
            def load_raw(slot, k):
                b, par, n = slot.at(k)
                wait_for(sp, z0_done, b - 1)
                wait_for(sp, xn_done, b - 1)
                sp.dma_start(ctx_in[:, par, :, :], ctx_1024[b].rearrange("(p r) d -> p r d", r=R)).then_inc(raw_in[par], 16)
                sp.dma_start(x_in[:, par, :], x[b]).then_inc(raw_in[par], 16)

            def load_res(slot, k):
                b, par, n = slot.at(k)
                wait_for(sp, x1_done, b - 1)
                sp.dma_start(x_res[:, par, :], x[b]).then_inc(res_in[par], 16)

            for par in range(2):
                sp.sem_inc(x1_out[par], 16)
                sp.sem_inc(x2_out[par], 16)

            start = Slot(0, 0, B)
            load_raw(start, 0)
            for n, row in enumerate((ln_x_w, ln_x_b)):
                sp.dma_start(ctx_w[:, n, :], row.partition_broadcast(P)).then_inc(rows_in, 16)
            for n, row in enumerate((ln_l_w, ln_l_b)):
                sp.dma_start(lat_w[:, n, :], row.partition_broadcast(P)).then_inc(rows_in, 16)
            sp.dma_start(wkv_raw, Wkv.rearrange("(k p) n -> p k n", p=P)).then_inc(wkv_in, 16)
            load_raw(start, 1)
            sp.dma_start(wq_raw, Wq.rearrange("(k p) n -> p k n", p=P)).then_inc(wq_in, 16)
            for n, row in enumerate((ln_o_w, ln_o_b)):
                sp.dma_start(o_w[:, n, :], row.partition_broadcast(P)).then_inc(small_in, 16)
            for n, g in enumerate((g_xattn, g_ffn)):
                sp.dma_start(gains[:, n:n + 1], g.partition_broadcast(P)).then_inc(small_in, 16)
            for n, s_ in enumerate((q_scale, k_scale)):
                for half in range(P // DH):
                    sp.dma_start(qk[half * DH:(half + 1) * DH, n:n + 1], s_.rearrange("(p o) -> p o", o=1)).then_inc(qk_in, 16)
            sp.dma_start(mask8[:, :], mask.rearrange("b m -> (b m)").partition_broadcast(S)).then_inc(mask_in, 16)
            sp.dma_start(wo_raw, Wo.rearrange("(k p) n -> p k n", p=P)).then_inc(wo_in, 16)
            sp.dma_start(wg[:, :, :], Wg.rearrange("(k p) n -> p k n", p=P)).then_inc(small_in, 16)
            sp.dma_start(b1_rows[:, :], b1.rearrange("e (k p) -> (e k) p", p=P)).then_inc(small_in, 16)
            sp.dma_start(x_res[:, 0, :], x[0]).then_inc(res_in[0], 16)

            def do(slot):
                if slot.gate:
                    b, par, n = slot.at(-2)
                    wait_for(sp, x2_done, b + 1)
                    sp.dma_start(tokens.rearrange("(b t) d -> b t d", t=S)[b], x2[:, par, :]).then_inc(x2_out[par], 16)
                if slot.steady or 2 <= slot.s + 4 < B:
                    load_raw(slot, 4)
                if slot.tail:
                    b, par, n = slot.at(-1)
                    wait_for(sp, x1_done, b + 1)
                    sp.dma_start(out[b], x1[:, par, :]).then_inc(x1_out[par], 16)
                if slot.steady or 1 <= slot.s + 1 < B:
                    load_res(slot, 1)

            for slot in FIRST:
                do(slot)
            sp.wait_ge(w_low, 3)
            sp.dma_start(raw1[:, :].rearrange("p (k n) -> p k n", k=KD), W1[0].rearrange("(k p) n -> p k n", p=P)).then_inc(w1_in, 16)
            sp.dma_start(raw2[:, :].rearrange("p (k n) -> p k n", k=KF), W2[0].rearrange("(k p) n -> p k n", p=P)).then_inc(w2_in, 16)
            with sp.Fori(LOOP[0], LOOP[1] - 1) as half:
                for par in range(2):
                    do(Slot(half, par, B, steady=True))
            for slot in [Slot(B // 2 - 2, 0, B), Slot(B // 2 - 2, 1, B)] + LAST:
                do(slot)

            for bank in range(2):
                sp.wait_ge(t_free[bank], T_ALL[bank])
            sp.dma_start(b2_all[:, :, :], b2.partition_broadcast(S)).then_inc(b2_in, 16)

            def load_expert(e):
                wait_for(sp, w1_low, e)
                sp.dma_start(raw1[:, :].rearrange("p (k n) -> p k n", k=KD), W1[e].rearrange("(k p) n -> p k n", p=P)).then_inc(w1_in, 16)
                wait_for(sp, w2_low, e)
                sp.dma_start(raw2[:, :].rearrange("p (k n) -> p k n", k=KF), W2[e].rearrange("(k p) n -> p k n", p=P)).then_inc(w2_in, 16)

            with sp.Fori(1, E) as e:
                load_expert(e)

        @block.gpsimd
        def _(pool):
            nc.gpsimd.iota(diff[:, :], [[1, P]], base=P, channel_multiplier=-1).then_inc(iota_done, 1)
            nc.gpsimd.memset(minus_half[:, :], -0.5)
            nc.gpsimd.memset(var_eps[:, :], 1.0).then_inc(pool_set, 1)
            nc.gpsimd.iota(slots_i[:, :], [[1, CAP]], base=1, channel_multiplier=0)
            nc.gpsimd.iota(ids_i[:, :], [[1, B], [0, E]], base=0, channel_multiplier=0)
            nc.gpsimd.iota(tok_i[:, :], [[0, B * E]], base=0, channel_multiplier=1).then_inc(iota_done, 1)
            pool.wait_ge(pool_set, 1)

            def do(slot):
                def rnorms(m):
                    b, _, _ = slot.at(1)
                    rows = KR if m < KT else S
                    wait_for(pool, ss_done, 5 * b + m + 1)
                    settle(pool)
                    nc.gpsimd.tensor_scalar(ss_max[0:rows, m, :], ss[0:rows, m, :], L2_EPS ** 2, None, ALU.max).then_inc(max_done, 1)
                    wait_for(pool, max_done, 5 * b + m + 1)
                    nc.gpsimd.tensor_tensor(rnorm[0:rows, m, :], ss_max[0:rows, m, :], minus_half[0:rows, 0:H], ALU.pow).then_inc(rn_done, 1)

                def context_times():
                    b, _, _ = slot.at(2)
                    wait_for(pool, rows_in, 16 * 4)
                    wait_for(pool, z0_done, b + 1)
                    for bank in range(2):
                        wait_for(pool, t_full[bank], t_before(slot, bank))
                    w_row = ctx_w[0:CP, 0:1, :].to_broadcast([CP, R, D])
                    nc.gpsimd.tensor_tensor(z[0:CP, 0:R, :], z0[0:CP, 0:R, :], w_row, ALU.mult).then_inc(zc_mul, 1)

                def context_plus():
                    b, _, _ = slot.at(2)
                    wait_for(pool, zc_mul, b + 1)
                    b_row = ctx_w[0:CP, 1:2, :].to_broadcast([CP, R, D])
                    nc.gpsimd.tensor_tensor(z[0:CP, 0:R, :], z[0:CP, 0:R, :], b_row, ALU.add).then_inc(zc_done, 1)

                def latents_rstd():
                    b, _, _ = slot.at(2)
                    wait_for(pool, mv2_done, b + 1)
                    settle(pool)
                    nc.gpsimd.tensor_scalar(var_eps2[0:S, :], mean_var2[0:S, 1:2], LN_EPS, None, ALU.add).then_inc(eps2_done, 1)
                    wait_for(pool, eps2_done, b + 1)
                    nc.gpsimd.tensor_tensor(rstd2[0:S, :], var_eps2[0:S, :], minus_half[0:S, 0:1], ALU.pow).then_inc(rstd2_done, 1)

                def latents_affine():
                    b, _, _ = slot.at(2)
                    wait_for(pool, z0x_done, b + 1)
                    nc.gpsimd.tensor_tensor(z[0:S, R, :], z0[0:S, R, :], lat_w[0:S, 0, :], ALU.mult).then_inc(zl_mul, 1)
                    wait_for(pool, zl_mul, b + 1)
                    nc.gpsimd.tensor_tensor(z[0:S, R, :], z[0:S, R, :], lat_w[0:S, 1, :], ALU.add).then_inc(zl_done, 1)

                def output_rstd():
                    b, par, n = slot.at(-1)
                    wait_for(pool, wo_mv, b + 1)
                    settle(pool)
                    nc.gpsimd.tensor_scalar(ve_o[:, :], mv_o[:, 1:2], LN_EPS, None, ALU.add).then_inc(wo_eps, 1)
                    wait_for(pool, wo_eps, b + 1)
                    nc.gpsimd.tensor_tensor(rstd_o[:, :], ve_o[:, :], minus_half[0:S, 0:1], ALU.pow).then_inc(wo_rstd, 1)

                def residual():
                    b, par, n = slot.at(-1)
                    wait_for(pool, wo_free, b + 1)
                    wait_for(pool, const_done, 2)
                    wait_for(pool, x1_out[par], 16 * (n + 1))
                    nc.gpsimd.tensor_tensor(x1[:, par, :], y_o[:, :], o_w[0:S, 0, :], ALU.mult).then_inc(yw_done, 1)
                    wait_for(pool, yw_done, b + 1)
                    nc.gpsimd.tensor_tensor(x1[:, par, :], x1[:, par, :], o_w[0:S, 1, :], ALU.add).then_inc(yb_done, 1)
                    wait_for(pool, yb_done, b + 1)
                    wait_for(pool, res_in[par], 16 * (n + 1))
                    nc.gpsimd.tensor_tensor(x1[:, par, :], x1[:, par, :], x_res[:, par, :], ALU.add).then_inc(x1_done, 1)

                def gate_rstd():
                    b, par, n = slot.at(-2)
                    wait_for(pool, g_mv, b + 1)
                    settle(pool)
                    nc.gpsimd.tensor_scalar(ve_g[:, :], mv_g[:, 1:2], LN_EPS, None, ALU.add).then_inc(g_eps, 1)
                    wait_for(pool, g_eps, b + 1)
                    nc.gpsimd.tensor_tensor(rstd_g[:, :], ve_g[:, :], minus_half[0:S, 0:1], ALU.pow).then_inc(g_rstd, 1)

                def norm_rstd():
                    b, _, _ = slot.at(2)
                    wait_for(pool, mv_done, b + 1)
                    settle(pool)
                    nc.gpsimd.tensor_scalar(var_eps[0:CP, 0:R], mean_var[0:CP, 0:R, 1], LN_EPS, None, ALU.add)
                    nc.gpsimd.tensor_scalar(var_eps[0:S, R:R + 1], mean_var[0:S, R, 1:2], LN_EPS, None, ALU.add).then_inc(eps_done, 1)
                    wait_for(pool, eps_done, b + 1)
                    nc.gpsimd.tensor_tensor(rstd[:, :], var_eps[:, :], minus_half[:, 0:4], ALU.pow).then_inc(rstd_done, 1)

                if slot.norm:
                    norm_rstd()
                if slot.project:
                    rnorms(0)
                if slot.norm:
                    context_times()
                if slot.project:
                    rnorms(1)
                    rnorms(2)
                if slot.norm:
                    context_plus()
                if slot.gate:
                    gate_rstd()
                if slot.norm:
                    latents_rstd()
                if slot.project:
                    rnorms(3)
                    rnorms(4)
                if slot.norm:
                    latents_affine()
                if slot.tail:
                    output_rstd()
                    residual()

            run_slots(pool, do)

            def gather(e, par, n):
                wait_for(pool, idx_done, e + 1)
                wait_for(pool, ext_full, 2 * (e - 1))
                settle(pool)
                for t in range(ST):
                    nc.gpsimd.indirect_dma_start(
                        ex[:, par, t, :], None, tokens[:, :],
                        bass.IndirectOffsetOnAxis(ap=idx[:, par, t:t + 1], axis=0),
                        bounds_check=TOK - 1).then_inc(ex_in[par], 16)

            def scatter(e, par, n):
                if par:
                    wait_for(pool, y_out[0], 16 * ST * (n + 1))
                else:
                    wait_for(pool, y_out[1], 16 * ST * n)
                for t in range(ST):
                    if t % 2 == 0:
                        wait_for(pool, y_done, 2 * e + t // 2 + 1)
                        settle(pool)
                    nc.gpsimd.indirect_dma_start(
                        out_rows[:, :], bass.IndirectOffsetOnAxis(ap=idx_y[:, par, t:t + 1], axis=0),
                        y[:, par, t, :], None, bounds_check=TOK - 1,
                        compute_op=ALU.add).then_inc(y_out[par], 16)

            def lows(e, par):
                wait_for(pool, w1_high, e + 1)
                nc.gpsimd.tensor_tensor(w1[:, par, 1, :, :].rearrange("p k n -> p (k n)"), raw1[:, :],
                                        w1[:, par, 0, :, :].rearrange("p k n -> p (k n)").bitcast(F32),
                                        ALU.subtract).then_inc(w1_low, 1)
                wait_for(pool, w2_high, e + 1)
                nc.gpsimd.tensor_tensor(w2[:, par, 1, :, :].rearrange("p k n -> p (k n)"), raw2[:, :],
                                        w2[:, par, 0, :, :].rearrange("p k n -> p (k n)").bitcast(F32),
                                        ALU.subtract).then_inc(w2_low, 1)

            for bank in range(2):
                pool.wait_ge(t_free[bank], T_ALL[bank])
            lows(0, 0)
            steps = 0
            for part in range(3):
                if part == 0:
                    pool.wait_ge(sig_done, 1)
                    left = sig
                else:
                    pool.wait_ge(gates_step, steps)
                    nc.gpsimd.tensor_tensor(rest[:, :], left[:, :], carry[:, :, 1 + part], ALU.subtract).then_inc(gates_step, 1)
                    steps += 1
                    pool.wait_ge(gates_step, steps)
                    left = rest
                nc.gpsimd.tensor_copy(carry[:, :, 2 + part], left[:, :]).then_inc(gates_step, 1)
                steps += 1
            for par in range(2):
                pool.wait_ge(x2_out[par], 16 * (B // 2 + 1))
            gather(0, 0, 0)
            for par in range(2):
                pool.wait_ge(x1_out[par], 16 * (B // 2 + 1))
            gather(1, 1, 0)
            lows(1, 1)
            gather(2, 0, 1)
            scatter(0, 0, 0)
            lows(2, 0)
            with pool.Fori(1, E // 2 - 1) as n:
                gather(2 * n + 1, 1, n)
                scatter(2 * n - 1, 1, n - 1)
                lows(2 * n + 1, 1)
                gather(2 * n + 2, 0, n + 1)
                scatter(2 * n, 0, n)
                lows(2 * n + 2, 0)
            n = E // 2 - 1
            gather(2 * n + 1, 1, n)
            scatter(2 * n - 1, 1, n - 1)
            lows(2 * n + 1, 1)
            scatter(2 * n, 0, n)
            scatter(2 * n + 1, 1, n)
            for par in range(2):
                pool.wait_ge(y_out[par], 16 * ST * (E // 2))

        @block.scalar
        def _(act):
            act.wait_ge(wkv_in, 16)
            nc.scalar.activation(wkv[:, 0, :, :], wkv_raw, ACT.Copy).then_inc(w_high, 1)
            act.wait_ge(wq_in, 16)
            nc.scalar.activation(wq[:, 0, :, :], wq_raw, ACT.Copy).then_inc(w_high, 1)

            def small_products():
                act.wait_ge(small_in, 16 * N_SMALL)
                nc.scalar.activation(tanhs[:, :], gains[:, :], ACT.Tanh).then_inc(tanh_done, 1)
                act.wait_ge(wo_in, 16)
                nc.scalar.activation(wo[:, 0, :, :], wo_raw, ACT.Copy).then_inc(w_high, 1)

            def empty_t(slot, name, dst, cols):
                bank = t_bank_of(name)
                wait_for(act, t_full[bank], t_number(slot, name))
                nc.scalar.activation(dst, cols(bankT[bank]), ACT.Copy).then_inc(t_free[bank], 1)

            def high_t(slot, name, dst, cols, **kw):
                bank = t_bank_of(name)
                wait_for(act, t_full[bank], t_number(slot, name))
                nc.scalar.activation(dst, cols(bankT[bank]), ACT.Copy, **kw).then_inc(t_high, 1)

            def take_k(slot, m):
                b, _, _ = slot.at(1)
                rows = KR if m < KT else S
                wait_for(act, k_full, 5 * b + m + 1)
                wait_for(act, ss_done, 5 * b + (m - 1 if m else 0))
                nc.scalar.activation(sq[0:rows, m % 2, :], bankK[0:rows, 0:INNER], ACT.Square).then_inc(sq_done, 1)
                wait_for(act, kn_done, 5 * b + (m - 1 if m >= 2 else -m))
                nc.scalar.activation(kraw[0:rows, m % 2, :], bankK[0:rows, 0:INNER], ACT.Copy).then_inc(k_free, 1)

            def empty_v(slot, t):
                b, par, _ = slot.at(1)
                wait_for(act, v_full, KT * b + t + 1)
                if t == 0:
                    wait_for(act, pv_done, H * (b - 1))
                nc.scalar.activation(V[0:KR, par, t, :], bankV[0:KR, 0:INNER], ACT.Copy).then_inc(v_free, 1)

            def empty_k(slot, t):
                b, par, _ = slot.at(1)
                wait_for(act, t_full[t_bank_of(f"kT{t}")], t_number(slot, f"kT{t}"))
                for side, rows in enumerate(SIDES):
                    last = nc.scalar.activation(kT[rows, par, side, :, t * KR:(t + 1) * KR],
                                                pieces(KI, KR)(bankT[t_bank_of(f"kT{t}")])[rows], ACT.Copy)
                last.then_inc(t_high, 1)

            def empty_q(slot):
                b, par, _ = slot.at(1)
                wait_for(act, qk_done, 1)
                wait_for(act, t_full[t_bank_of("qT")], t_number(slot, "qT"))
                for side, rows in enumerate(SIDES):
                    last = nc.scalar.activation(qT[rows, par, side, :, :], pieces(KI, S)(bankT[t_bank_of("qT")])[rows],
                                                ACT.Copy, scale=qk_scale[rows, 0:1])
                last.then_inc(t_high, 1)

            def repeat_q(slot):
                b, par, _ = slot.at(1)
                wait_for(act, t_high, high_number(slot, "qT"))
                for side, rows in enumerate(SIDES):
                    last = nc.scalar.activation(qT[SIDES[1 - side], par, side, :, :],
                                                qT[rows, par, side, :, :].bitcast(F32), ACT.Copy)
                last.then_inc(q_twice, 1)

            def exp(slot, h):
                b, par, _ = slot.at(0)
                wait_for(act, neg_done, H * b + h + 1)
                wait_for(act, p_full, H * b + h - 1)
                if h == 0:
                    wait_for(act, rden_done, b - 1)
                nc.scalar.activation(prob[:, h % 2, :], negs[:, h % 2, :], ACT.Exp, bias=least[:, h:h + 1],
                                     scale=-1.0, accum_out=den[:, par, h:h + 1]).then_inc(exp_done, 1)

            def empty_p(n, h):
                wait_for(act, p_full, n)
                wait_for(act, pv_done, n - 2)
                nc.scalar.activation(pT[0:KR, h % 2, :, :],
                                     bankP[0:KR, 0:KT * S].rearrange("p (t s) -> p t s", t=KT),
                                     ACT.Copy).then_inc(p_free, 1)

            def empty_logits(slot):
                b, _, _ = slot.at(-2)
                empty_t(slot, "gate", logits[:, bass.ds(b * E, E)], lambda bank: bank[0:S, 0:E])

            def high_x(slot, kc):
                high_t(slot, f"xT{kc}", xT[:, slot.par, 0, kc, 0:KEYS], pieces(1, KEYS, flat=True))

            def do(slot):
                if not slot.steady and slot.s == -1:
                    small_products()
                done = H * slot.at(0)[0]
                if slot.heads:
                    exp(slot, 0)
                if slot.tail:
                    empty_p(done, H - 1)
                if slot.project:
                    take_k(slot, 0)
                if slot.heads:
                    empty_p(done + 1, 0)
                    exp(slot, 1)
                if slot.project:
                    take_k(slot, 1)
                    empty_v(slot, 0)
                if slot.heads:
                    empty_p(done + 2, 1)
                if slot.project:
                    take_k(slot, 2)
                    empty_k(slot, 0)
                if slot.heads:
                    exp(slot, 2)
                    exp(slot, 3)
                if slot.project:
                    empty_v(slot, 1)
                    take_k(slot, 3)
                if slot.tail:
                    high_t(slot, "oT", oT[:, 0, :, :], pieces(KI, S))
                if slot.project:
                    empty_k(slot, 1)
                if slot.heads:
                    empty_p(done + 3, 2)
                    exp(slot, 4)
                if slot.project:
                    take_k(slot, 4)
                if slot.heads:
                    empty_p(done + 4, 3)
                if slot.project:
                    empty_k(slot, 2)
                if slot.heads:
                    empty_p(done + 5, 4)
                    exp(slot, 5)
                if slot.project:
                    empty_k(slot, 3)
                    empty_v(slot, 2)
                if slot.heads:
                    empty_p(done + 6, 5)
                if slot.project:
                    empty_q(slot)
                if slot.heads:
                    exp(slot, 6)
                if slot.gate:
                    empty_t(slot, "x2T", x2T[:, :, :], pieces(KD, S))
                if slot.heads:
                    empty_p(done + 7, 6)
                if slot.gate:
                    empty_logits(slot)
                if slot.project:
                    repeat_q(slot)
                if slot.heads:
                    exp(slot, 7)
                if slot.norm:
                    high_x(slot, 0)
                    high_x(slot, 1)
                if slot.project:
                    empty_v(slot, 3)

            run_slots(act, do)

            for bank in range(2):
                act.wait_ge(t_free[bank], T_ALL[bank])
            nc.scalar.activation(sig[:, :], logits[:, :], ACT.Sigmoid).then_inc(sig_done, 1)

            def highs(e, par):
                wait_for(act, w1_in, 16 * (e + 1))
                wait_for(act, h_full, KF * (e - 1))
                nc.scalar.activation(w1[:, par, 0, :, :].rearrange("p k n -> p (k n)"), raw1[:, :], ACT.Copy).then_inc(w1_high, 1)
                wait_for(act, w2_in, 16 * (e + 1))
                wait_for(act, y_full, 2 * (e - 1))
                nc.scalar.activation(w2[:, par, 0, :, :].rearrange("p k n -> p (k n)"), raw2[:, :], ACT.Copy).then_inc(w2_high, 1)

            def high_ex(e):
                for kc in range(KD):
                    wait_for(act, ext_full, 2 * e + kc + 1)
                    nc.scalar.activation(exT[:, 0, kc, :], bankX[kc][:, 0:CAP], ACT.Copy).then_inc(ext_high, 1)

            def hidden(e):
                for f in range(KF):
                    wait_for(act, h_full, KF * e + f + 1)
                    wait_for(act, hid_done, KF * e + f - 1)
                    nc.scalar.activation(hid[:, f % 2, :], bankS[:, f % 2, 0:CAP], ACT.Gelu,
                                         bias=b1T[:, bass.ds(e * KF + f, 1)]).then_inc(h_free, 1)

            highs(0, 0)
            act.wait_ge(b1_full, 1)
            nc.scalar.activation(b1T[:, :], bankT[1][:, 0:E * KF], ACT.Copy).then_inc(b1_done, 1)
            act.wait_ge(b1_done, 1)
            high_ex(0)
            hidden(0)
            highs(1, 1)
            with act.Fori(0, E // 2 - 1) as n:
                for par in range(2):
                    high_ex(2 * n + 1 + par)
                    hidden(2 * n + 1 + par)
                    highs(2 * n + 2 + par, par)
            high_ex(E - 1)
            hidden(E - 1)

        @block.vector
        def _(dve):
            dve.wait_ge(iota_done, 1)
            nc.vector.tensor_scalar(ident[:, :], diff[:, :], float(P), None, ALU.is_equal)
            nc.vector.tensor_scalar(same[:, :], diff[:, :], E - 1, None, ALU.bitwise_and).then_inc(v_step, 1)
            nc.vector.memset(nm[:, :, M:KEYS], 0.0)
            nc.vector.memset(nm[:, :, KEYS:KP], MASKED)
            nc.vector.memset(xT[:, :, :, :, KEYS:KP].bitcast(F32), 0.0)
            nc.vector.memset(ones_b[:, :], 1.0)
            nc.vector.tensor_scalar(upto[:, :], diff[:, :], float(P), None, ALU.is_ge)
            nc.vector.tensor_scalar(before_e[:, :], diff[:, :], float(P), None, ALU.is_gt).then_inc(const_done, 1)
            n_steps = [1]

            def link(ins):
                n_steps[0] += 1
                ins.then_inc(v_step, 1)
                dve.wait_ge(v_step, n_steps[0])

            dve.wait_ge(v_step, 1)
            link(nc.vector.tensor_scalar(same_e[:, :], same[:, :], 0.0, None, ALU.is_equal))
            link(nc.vector.tensor_tensor(before_e[:, :], before_e[:, :], same_e[:, :], ALU.mult))
            link(nc.vector.tensor_copy(ident_b[:, :], ident[:, :]))
            dve.wait_ge(iota_done, 2)
            nc.vector.tensor_copy(slots16[:, :], slots_i[:, :])
            nc.vector.tensor_copy(carry[:, :, 0], ids_i[:, :])
            link(nc.vector.tensor_copy(carry[:, :, 1], tok_i[:, :]))

            def norm_begin(slot):
                b, par, n = slot.at(2)
                wait_for(dve, raw_in[par], 32 * (n + 1))
                for r in range(R):
                    nc.vector.bn_stats(stat[0:CP, r, :], ctx_in[:, par, r, :])
                nc.vector.bn_stats(stat[0:S, R, :], x_in[:, par, :]).then_inc(stat_done, 1)
                wait_for(dve, stat_done, b + 1)
                wait_for(dve, eps_done, b)
                settle(dve)
                for r in range(R):
                    nc.vector.bn_aggr(mean_var[0:CP, r, :], stat[0:CP, r, :])
                nc.vector.bn_aggr(mean_var[0:S, R, :], stat[0:S, R, :]).then_inc(mv_done, 1)

            def norm_rows(slot):
                b, par, n = slot.at(2)
                wait_for(dve, rstd_done, b + 1)
                wait_for(dve, zc_mul, b)
                nc.vector.tensor_scalar(xn[:, :], x_in[:, par, :], mean_var[0:S, R, 0:1], rstd[0:S, R:R + 1],
                                        ALU.subtract, ALU.mult).then_inc(xn_done, 1)
                for r in range(R):
                    last = nc.vector.tensor_scalar(z0[0:CP, r, :], ctx_in[:, par, r, :], mean_var[0:CP, r, 0:1],
                                                   rstd[0:CP, r:r + 1], ALU.subtract, ALU.mult)
                last.then_inc(z0_done, 1)
                wait_for(dve, xn_done, b + 1)
                nc.vector.bn_stats(stat2[0:S, :], xn[:, :]).then_inc(stat2_done, 1)

            def norm_again(slot):
                b, _, _ = slot.at(2)
                wait_for(dve, stat2_done, b + 1)
                wait_for(dve, eps2_done, b)
                settle(dve)
                nc.vector.bn_aggr(mean_var2[0:S, :], stat2[0:S, :]).then_inc(mv2_done, 1)

            def norm_end(slot):
                b, _, _ = slot.at(2)
                wait_for(dve, rstd2_done, b + 1)
                wait_for(dve, zl_mul, b)
                nc.vector.tensor_scalar(z0[0:S, R, :], xn[:, :], mean_var2[0:S, 0:1], rstd2[0:S, :],
                                        ALU.subtract, ALU.mult).then_inc(z0x_done, 1)

            def sum_squares(slot, m):
                b, _, _ = slot.at(1)
                rows = KR if m < KT else S
                wait_for(dve, sq_done, 5 * b + m + 1)
                wait_for(dve, max_done, 5 * (b - 1) + m + 1)
                nc.vector.tensor_reduce(ss[0:rows, m, :], sq[0:rows, m % 2, :].rearrange("p (h d) -> p h d", h=H),
                                        AX.X, ALU.add).then_inc(ss_done, 1)

            def unit(slot, m):
                b, _, _ = slot.at(1)
                rows = KR if m < KT else S
                wait_for(dve, rn_done, 5 * b + m + 1)
                src = kraw[0:rows, m % 2, :].rearrange("p (h d) -> p h d", h=H)
                scale = rnorm[0:rows, m, :].unsqueeze(2).to_broadcast([rows, H, DH])
                if m < KT:
                    if m >= 2:
                        wait_for(dve, t_full[t_bank_of(f"kT{m - 2}")], t_number(slot, f"kT{m - 2}"))
                    dst = kn[0:rows, m % 2, :]
                else:
                    dst = qn[:, :]
                wait_for(dve, k_free, 5 * b + m + 1)
                nc.vector.tensor_tensor(dst.rearrange("p (h d) -> p h d", h=H), src, scale, ALU.mult).then_inc(kn_done, 1)

            def mask_row(slot):
                b, par, _ = slot.at(1)
                wait_for(dve, mask_in, 16)
                nc.vector.tensor_scalar(nm[:, par, 0:M].rearrange("s (r p) -> s r p", r=R),
                                        mask8[:, bass.ds(b * M, M)].rearrange("s (p r) -> s r p", r=R),
                                        0.0, MASKED, ALU.is_equal, ALU.mult).then_inc(nm_done, 1)

            def negated(slot, h):
                b, par, _ = slot.at(0)
                if h == 0:
                    wait_for(dve, nm_done, b + 1)
                wait_for(dve, s_full, H * b + h + 1)
                wait_for(dve, exp_done, H * b + h - 1)
                settle(dve)
                nc.vector.tensor_tensor_reduce(negs[:, h % 2, :], bankS[0:S, h % 2, 0:KP], nm[:, par, :], 1.0, MIN_START,
                                               ALU.add, ALU.min, least[:, h:h + 1]).then_inc(neg_done, 1)

            def divide(slot):
                b, par, _ = slot.at(-1)
                wait_for(dve, exp_done, H * (b + 1))
                nc.vector.reciprocal(rden[:, :], den[:, par, :]).then_inc(rden_done, 1)
                wait_for(dve, rden_done, b + 1)
                wait_for(dve, pv_done, H * (b + 1))
                if slot.s is not None and (slot.gate):
                    wait_for(dve, wo_full, b)
                nc.vector.tensor_tensor(on[:, :].rearrange("s (h d) -> s h d", h=H),
                                        bankO[0:S, 0:INNER].rearrange("s (h d) -> s h d", h=H),
                                        rden[:, :].unsqueeze(2).to_broadcast([S, H, DH]), ALU.mult).then_inc(on_done, 1)

            def out_stats(slot):
                b, _, _ = slot.at(-1)
                wait_for(dve, wo_full, b + 1)
                nc.vector.bn_stats(stat_o[:, :], bankV[0:S, 0:D]).then_inc(wo_stat, 1)
                wait_for(dve, wo_stat, b + 1)
                settle(dve)
                nc.vector.bn_aggr(mv_o[:, :], stat_o[:, :]).then_inc(wo_mv, 1)

            def out_norm(slot):
                b, _, _ = slot.at(-1)
                wait_for(dve, wo_rstd, b + 1)
                wait_for(dve, yw_done, b)
                nc.vector.tensor_scalar(y_o[:, :], bankV[0:S, 0:D], mv_o[:, 0:1], rstd_o[:, :],
                                        ALU.subtract, ALU.mult).then_inc(wo_free, 1)

            def gate_stats(slot):
                b, par, _ = slot.at(-2)
                wait_for(dve, x1_done, b + 1)
                nc.vector.bn_stats(stat_g[:, :], x1[:, par, :]).then_inc(g_stat, 1)
                wait_for(dve, g_stat, b + 1)
                settle(dve)
                nc.vector.bn_aggr(mv_g[:, :], stat_g[:, :]).then_inc(g_mv, 1)

            def gate_norm(slot):
                b, par, n = slot.at(-2)
                wait_for(dve, g_rstd, b + 1)
                wait_for(dve, x2_out[par], 16 * (n + 1))
                nc.vector.tensor_scalar(x2[:, par, :], x1[:, par, :], mv_g[:, 0:1], rstd_g[:, :],
                                        ALU.subtract, ALU.mult).then_inc(x2_done, 1)

            def low_t(slot, name, dst, cols, high):
                bank = t_bank_of(name)
                wait_for(dve, t_high, high_number(slot, name))
                nc.vector.tensor_tensor(dst, cols(bankT[bank]), high.bitcast(F32), ALU.subtract).then_inc(t_free[bank], 1)

            def low_x(slot, kc):
                low_t(slot, f"xT{kc}", xT[:, slot.par, 1, kc, 0:KEYS], pieces(1, KEYS, flat=True),
                      xT[:, slot.par, 0, kc, 0:KEYS])

            def low_k(slot, t):
                b, par, _ = slot.at(1)
                cols = slice(t * KR, (t + 1) * KR)
                bank = t_bank_of(f"kT{t}")
                wait_for(dve, t_high, high_number(slot, f"kT{t}"))
                for side, rows in enumerate(SIDES):
                    last = nc.vector.tensor_tensor(kT[SIDES[1 - side], par, side, :, cols], pieces(KI, KR)(bankT[bank])[rows],
                                                   kT[rows, par, side, :, cols].bitcast(F32), ALU.subtract)
                last.then_inc(t_free[bank], 1)

            def low_q(slot):
                b, par, _ = slot.at(1)
                bank = t_bank_of("qT")
                wait_for(dve, t_high, high_number(slot, "qT"))
                for side, rows in enumerate(SIDES):
                    last = nc.vector.scalar_tensor_tensor(
                        out=qT_low[rows, par, :, :], in0=pieces(KI, S)(bankT[bank])[rows], scalar=qk_scale[rows, 0:1],
                        in1=qT[rows, par, side, :, :].bitcast(F32), op0=ALU.mult, op1=ALU.subtract)
                last.then_inc(t_free[bank], 1)

            def low_o(slot):
                low_t(slot, "oT", oT[:, 1, :, :], pieces(KI, S), oT[:, 0, :, :])

            def low_weights(n, parts, raw):
                dve.wait_ge(w_high, n + 1)
                nc.vector.tensor_tensor(parts[:, 1, :, :], raw, parts[:, 0, :, :].bitcast(F32), ALU.subtract).then_inc(w_low, 1)

            def small_products():
                dve.wait_ge(tanh_done, 1)
                dve.wait_ge(small_in, 16 * N_SMALL)
                nc.vector.tensor_scalar(o_w[:, :, :], o_w[:, :, :], tanhs[:, 0:1], None, ALU.mult).then_inc(const_done, 1)
                dve.wait_ge(w_high, 3)
                nc.vector.tensor_tensor(wo[:, 1, :, :], wo_raw, wo[:, 0, :, :].bitcast(F32), ALU.subtract).then_inc(w_low, 1)

            def do(slot):
                if not slot.steady and slot.s == -1:
                    dve.wait_ge(qk_in, 16 * 4)
                    nc.vector.tensor_scalar(qk_scale[:, :], qk[:, 0:1], qk[:, 1:2], -SCALE, ALU.mult, ALU.mult).then_inc(qk_done, 1)
                if not slot.steady and slot.s == -1:
                    low_weights(1, wq, wq_raw)
                    small_products()
                if slot.heads:
                    negated(slot, 0)
                if slot.norm:
                    norm_begin(slot)
                if slot.tail:
                    divide(slot)
                if slot.heads:
                    negated(slot, 1)
                if slot.project:
                    sum_squares(slot, 0)
                if slot.norm:
                    norm_rows(slot)
                if slot.project:
                    sum_squares(slot, 1)
                    unit(slot, 0)
                if slot.heads:
                    negated(slot, 2)
                if slot.project:
                    sum_squares(slot, 2)
                if slot.gate:
                    gate_stats(slot)
                if slot.heads:
                    negated(slot, 3)
                if slot.norm:
                    norm_again(slot)
                if slot.project:
                    unit(slot, 1)
                    low_k(slot, 0)
                    unit(slot, 2)
                if slot.heads:
                    negated(slot, 4)
                if slot.project:
                    sum_squares(slot, 3)
                if slot.tail:
                    low_o(slot)
                if slot.project:
                    sum_squares(slot, 4)
                    low_k(slot, 1)
                    unit(slot, 3)
                if slot.heads:
                    negated(slot, 5)
                if slot.project:
                    low_k(slot, 2)
                    unit(slot, 4)
                if slot.norm:
                    norm_end(slot)
                if slot.gate:
                    gate_norm(slot)
                if slot.project:
                    low_k(slot, 3)
                if slot.heads:
                    negated(slot, 6)
                if slot.project:
                    low_q(slot)
                if slot.tail:
                    out_stats(slot)
                if slot.heads:
                    negated(slot, 7)
                if slot.tail:
                    out_norm(slot)
                if slot.project:
                    mask_row(slot)
                if not slot.steady and slot.s == -2:
                    low_weights(0, wkv, wkv_raw)
                if slot.norm:
                    low_x(slot, 0)
                    low_x(slot, 1)

            run_slots(dve, do)

            for bank in range(2):
                dve.wait_ge(t_free[bank], T_ALL[bank])
            nc.vector.tensor_scalar(tied[:, :], logits[:, :], SIGMOID_ONE, 0.0, ALU.min, ALU.add).then_inc(tied_done, 1)
            dve.wait_ge(score_full, 1)
            link(nc.vector.tensor_copy(score[:, :], bankT[1][:, 0:S]))
            bits = score[:, :].bitcast(I32)
            link(nc.vector.tensor_scalar(fold[:, :], bits, 31, 0x7FFFFFFF, ALU.arith_shift_right, ALU.bitwise_and))
            link(nc.vector.tensor_tensor(key[:, :], bits, fold[:, :], ALU.bitwise_xor))
            nc.vector.tensor_scalar(half_i[:, 0, :], key[:, :], 16, None, ALU.arith_shift_right)
            link(nc.vector.tensor_scalar(half_i[:, 1, :], key[:, :], 0xFFFF, None, ALU.bitwise_and))
            nc.vector.tensor_scalar(hi_f[:, :], half_i[:, 0, :], HI_UNIT, None, ALU.mult)
            link(nc.vector.tensor_copy(lo_f[:, :], half_i[:, 1, :]))

            def search(values, start, unit, base):
                top = 2.0 ** (BITS - 2) * unit
                for n in range(TRIES):
                    nc.vector.memset(cand[:, n:n + 1], start + (n + 1) * top)
                    nc.vector.memset(tries[:, n:n + 1], (n + 1) * top)
                link(nc.vector.memset(step[:, :], top))
                first = n_steps[0]
                with dve.Fori(0, BITS // 4) as i:
                    for m in range(2):
                        with nc.allow_low_precision(reason="counts up to 112 are exact"):
                            for n in range(TRIES):
                                last = nc.vector.tensor_scalar(hit[:, n, :], values, cand[:, n:n + 1], None, ALU.is_ge,
                                                               ALU.add, accum_out=count[:, n:n + 1])
                            last.then_inc(counted, 1)
                        nc.vector.scalar_tensor_tensor(out=ahead[:, :], in0=tries[:, :], scalar=-0.75, in1=cand[:, :],
                                                       op0=ALU.mult, op1=ALU.add)
                        nc.vector.tensor_scalar(tries[:, :], tries[:, :], 0.25, None, ALU.mult)
                        dve.wait_ge(totalled, base + 2 * i + m + 1)
                        nc.vector.tensor_scalar(reached[:, :], bankO[:, 0:TRIES], float(CAP), None, ALU.is_ge, ALU.add,
                                                accum_out=passed[:, :]).then_inc(v_step, 1)
                        dve.wait_ge(v_step, first + 4 * i + 2 * m + 1)
                        nc.vector.scalar_tensor_tensor(out=cand[:, :], in0=step[:, :], scalar=passed[:, :], in1=ahead[:, :],
                                                       op0=ALU.mult, op1=ALU.add)
                        nc.vector.tensor_scalar(step[:, :], step[:, :], 0.25, None, ALU.mult).then_inc(v_step, 1)
                        dve.wait_ge(v_step, first + 4 * i + 2 * m + 2)
                n_steps[0] = first + BITS

            search(hi_f[:, :], -2.0 ** (BITS - 1) * HI_UNIT, HI_UNIT, 0)
            link(nc.vector.tensor_scalar(bound[:, :], cand[:, 0:1], -0.25 * HI_UNIT, None, ALU.add))
            link(nc.vector.scalar_tensor_tensor(out=lo_f[:, :], in0=hi_f[:, :], scalar=bound[:, :], in1=lo_f[:, :],
                                                op0=ALU.subtract, op1=ALU.add))
            search(lo_f[:, :], 0.0, 1.0, BITS // 2)
            link(nc.vector.tensor_scalar(bound[:, :], cand[:, 0:1], -0.25, None, ALU.add))
            with nc.allow_low_precision(reason="counts up to 112 are exact"):
                nc.vector.tensor_scalar(eq_b[:, :], lo_f[:, :], bound[:, :], None, ALU.is_equal, ALU.add,
                                        accum_out=eq_count[:, :]).then_inc(eq_done, 1)
                nc.vector.tensor_scalar(gt_b[:, :], lo_f[:, :], bound[:, :], None, ALU.is_gt, ALU.add,
                                        accum_out=gt_count[:, :]).then_inc(eq_done, 1)
            dve.wait_ge(eqT_full, 1)
            nc.vector.tensor_copy(eqT[:, :], bankP[0:S, 0:P // 2].bitcast(BF16)).then_inc(eqT_copied, 1)
            dve.wait_ge(prefix_full, 1)
            link(nc.vector.tensor_copy(earlier[:, :], bankO[:, 0:1]))
            link(nc.vector.tensor_scalar(first_eq[:, :], bankS[:, 0, 0:S], earlier[:, :], float(CAP), ALU.add, ALU.is_le))
            link(nc.vector.tensor_tensor(first_eq[:, :], first_eq[:, :], eq_b[:, :], ALU.mult))
            link(nc.vector.tensor_tensor(first_eq[:, :], first_eq[:, :], gt_b[:, :], ALU.add))
            link(nc.vector.tensor_scalar(chosen[:, :], first_eq[:, :], 1.0, None, ALU.mult, ALU.add,
                                         accum_out=chosen_count[:, :]))
            nc.vector.tensor_scalar(before_c[:, :], before_e[:, :], chosen_count[:, :], None, ALU.mult).then_inc(chosen_done, 1)
            dve.wait_ge(chosen_full, 1)
            link(nc.vector.tensor_copy(chosenT[:, :], bankP[0:S, 0:P // 2].bitcast(BF16)))
            nc.vector.tensor_copy(first_eq[0:S, 0:1], chosenT[:, 0:1]).then_inc(chosenT_copied, 1)
            dve.wait_ge(place_full, 1)
            link(nc.vector.tensor_tensor(place[:, :], bankS[0:S, 0, 0:P], chosenT[:, :], ALU.mult))

            dve.wait_ge(gates_step, 5)

            def hot(e, par):
                wait_for(dve, id_full, e)
                nc.vector.tensor_copy(carry_e[:, par, :, :], carry[:, :, :].rearrange(
                    "s (b e) c -> s b (e c)", e=E)[:, :, bass.ds(e * 5, 5)]).then_inc(carry_done, 1)
                for b in range(B):
                    last = nc.vector.tensor_scalar(onehot[:, b, :], slots16[:, :], place[:, bass.ds(b * E + e, 1)],
                                                   None, ALU.is_equal)
                    if b % HOT == HOT - 1:
                        last.then_inc(hot_done, 1)

            def lows_ex(e):
                for kc in range(KD):
                    wait_for(dve, ext_high, 2 * e + kc + 1)
                    nc.vector.tensor_tensor(exT[:, 1, kc, :], bankX[kc][:, 0:CAP], exT[:, 0, kc, :].bitcast(F32),
                                            ALU.subtract).then_inc(ext_free, 1)

            def split_hidden(e):
                for f in range(KF):
                    wait_for(dve, h_free, KF * e + f + 1)
                    wait_for(dve, y_full, 2 * e)
                    nc.vector.tensor_copy(hidT[:, 0, f, :], hid[:, f % 2, :]).then_inc(hid_high, 1)
                    wait_for(dve, hid_high, KF * e + f + 1)
                    nc.vector.tensor_tensor(hidT[:, 1, f, :], hid[:, f % 2, :], hidT[:, 0, f, :].bitcast(F32),
                                            ALU.subtract).then_inc(hid_done, 1)

            def ids(e, par, n):
                wait_for(dve, id_full, e + 1)
                wait_for(dve, ex_in[par], 16 * ST * n)
                got = bankO[0:S, 0:8 * ST].rearrange("s (t c) -> s t c", c=8)
                nc.vector.tensor_copy(idx_f[:, :], got[:, :, 1])
                nc.vector.tensor_copy(gate_s[:, :], got[:, :, 2]).then_inc(v_exp, 1)
                wait_for(dve, v_exp, 2 * e + 1)
                nc.vector.scalar_tensor_tensor(out=idx[:, par, :], in0=got[:, :, 0], scalar=float(S), in1=idx_f[:, :],
                                               op0=ALU.mult, op1=ALU.add).then_inc(idx_done, 1)
                nc.vector.tensor_tensor(gate_s[:, :], got[:, :, 3], gate_s[:, :], ALU.add).then_inc(v_exp, 1)
                wait_for(dve, v_exp, 2 * e + 2)
                nc.vector.tensor_tensor(gate_v[:, par, :], got[:, :, 4], gate_s[:, :], ALU.add).then_inc(gate_sum, 1)
                wait_for(dve, gate_sum, 2 * e + 1)
                nc.vector.tensor_scalar(gate_v[:, par, :], gate_v[:, par, :], tanhs[0:S, 1:2], None, ALU.mult).then_inc(gate_sum, 1)

            def results(e, par, n):
                wait_for(dve, y_out[par], 16 * ST * n)
                nc.vector.tensor_copy(idx_y[:, par, :], idx[:, par, :])
                wait_for(dve, gate_sum, 2 * e + 2)
                for half in range(2):
                    tiles = range(2 * half, 2 * half + 2)
                    wait_for(dve, y_full, 2 * e + half + 1)
                    wait_for(dve, y_done, 2 * (e - 1) + half + 1)
                    nc.vector.tensor_tensor(y_b[:, tiles[0]:tiles[-1] + 1, :],
                                            bankY[half][0:S, 0:2 * D].rearrange("s (t d) -> s t d", t=2),
                                            b2_all[:, bass.ds(e, 1), :].to_broadcast([S, 2, D]), ALU.add).then_inc(y_free, 1)
                    wait_for(dve, y_free, 2 * e + half + 1)
                    for t in tiles:
                        last = nc.vector.tensor_scalar(y[:, par, t, :], y_b[:, t, :], gate_v[:, par, t:t + 1], None, ALU.mult)
                    last.then_inc(y_done, 1)

            def expert(e, par, n, more=2):
                split_hidden(e)
                if more:
                    lows_ex(e + 1)
                if more > 1:
                    hot(e + 2, par)
                results(e, par, n)
                if more > 1:
                    ids(e + 2, par, n + 1)

            hot(0, 0)
            ids(0, 0, 0)
            dve.wait_ge(b2_in, 16)
            hot(1, 1)
            ids(1, 1, 0)
            lows_ex(0)
            for par in range(2):
                expert(par, par, 0)
            with dve.Fori(1, E // 2 - 1) as n:
                for par in range(2):
                    expert(2 * n + par, par, n)
            n = E // 2 - 1
            expert(2 * n, 0, n, more=1)
            expert(2 * n + 1, 1, n, more=0)

        @block.tensor
        def _(pe):
            pe.wait_ge(const_done, 1)

            def t_bank(slot, name):
                bank = t_bank_of(name)
                wait_for(pe, t_free[bank], t_number(slot, name) - 1)
                return bankT[bank], t_full[bank]

            def t_taken(slot, name):
                wait_for(pe, t_free[t_bank_of(name)], t_number(slot, name))

            def transpose_x(slot, kc):
                b, _, _ = slot.at(2)
                wait_for(pe, zc_done, b + 1)
                wait_for(pe, zl_done, b + 1)
                bank, full = t_bank(slot, f"xT{kc}")
                for r in range(R):
                    nc.tensor.transpose(bank[:, r * CP:(r + 1) * CP], z[0:CP, r, kc * P:(kc + 1) * P], ident[0:CP, 0:CP])
                nc.tensor.transpose(bank[:, M:KEYS], z[0:S, R, kc * P:(kc + 1) * P], ident[0:S, 0:S]).then_inc(full, 1)

            def keys(slot, t):
                b, _, _ = slot.at(1)
                if t == 0:
                    for bank in range(2):
                        wait_for(pe, t_free[bank], t_before(slot, bank))
                wait_for(pe, w_low, 1)
                wait_for(pe, k_free, 5 * b + t)
                for kc in range(KD):
                    last = products(bankK[0:KR, 0:INNER], lambda a: xT[:, 1 - slot.par, a, kc, t * KR:(t + 1) * KR],
                                    lambda a: wkv[:, a, kc, 0:INNER], kc == 0, kc == KD - 1)
                last.then_inc(k_full, 1)

            def queries(slot):
                b, _, _ = slot.at(1)
                wait_for(pe, w_low, 2)
                wait_for(pe, k_free, 5 * b + KT)
                for kc in range(KD):
                    last = products(bankK[0:S, 0:INNER], lambda a: xT[:, 1 - slot.par, a, kc, M:KEYS], lambda a: wq[:, a, kc, :],
                                    kc == 0, kc == KD - 1)
                last.then_inc(k_full, 1)

            def values(slot, t):
                b, _, _ = slot.at(1)
                if t != V_FIRST or not slot.tail:
                    wait_for(pe, v_free, KT * b + t)
                else:
                    wait_for(pe, wo_free, b - 1)
                for kc in range(KD):
                    last = products(bankV[0:KR, 0:INNER], lambda a: xT[:, 1 - slot.par, a, kc, t * KR:(t + 1) * KR],
                                    lambda a: wkv[:, a, kc, INNER:], kc == 0, kc == KD - 1)
                last.then_inc(v_full, 1)

            def transpose_k(slot, t):
                b, _, _ = slot.at(1)
                wait_for(pe, kn_done, 5 * b + t + 1)
                bank, full = t_bank(slot, f"kT{t}")
                for c in range(KI):
                    last = nc.tensor.transpose(bank[:, c * KR:(c + 1) * KR], kn[0:KR, t % 2, c * P:(c + 1) * P],
                                               ident[0:KR, 0:KR])
                last.then_inc(full, 1)

            def transpose_q(slot):
                b, _, _ = slot.at(1)
                wait_for(pe, kn_done, 5 * b + KT + 1)
                bank, full = t_bank(slot, "qT")
                for c in range(KI):
                    last = nc.tensor.transpose(bank[:, c * S:(c + 1) * S], qn[:, c * P:(c + 1) * P], ident[0:S, 0:S])
                last.then_inc(full, 1)

            def scores(slot, h):
                b, par, _ = slot.at(0)
                if h == 0:
                    for bank in range(2):
                        wait_for(pe, t_free[bank], t_before(slot, bank) - (1 if slot.steady or slot.s + 1 < B else 0))
                    wait_for(pe, q_twice, b + 1)
                wait_for(pe, neg_done, H * b + h - 1)
                side, rows = h % 2, SIDES[h % 2]
                nc.tensor.matmul(bankS[0:S, h % 2, 0:KP], qT[:, par, side, h // 2, :], kT[:, par, side, h // 2, :],
                                 start=True, stop=False)
                nc.tensor.matmul(bankS[0:S, h % 2, 0:KP], qT_low[rows, par, h // 2, :], kT[rows, par, side, h // 2, :],
                                 start=False, stop=True).then_inc(s_full, 1)

            def transpose_p(n, h):
                wait_for(pe, exp_done, n)
                wait_for(pe, p_free, n - 1)
                for t in range(KT):
                    last = nc.tensor.transpose(bankP[0:KR, t * S:(t + 1) * S], prob[:, h % 2, t * KR:(t + 1) * KR],
                                               ident[0:S, 0:S])
                last.then_inc(p_full, 1)

            def attend(slot, k, h):
                b, par, _ = slot.at(k)
                wait_for(pe, p_free, H * b + h + 1)
                if h == 0:
                    wait_for(pe, on_done, b)
                    wait_for(pe, v_free, KT * (b + 1))
                for t in range(KT):
                    last = nc.tensor.matmul(bankO[0:S, h * DH:(h + 1) * DH], pT[0:KR, h % 2, t, :],
                                            V[0:KR, par, t, h * DH:(h + 1) * DH], start=(t == 0), stop=(t == KT - 1))
                last.then_inc(pv_done, 1)

            def transpose_o(slot):
                b, _, _ = slot.at(-1)
                wait_for(pe, on_done, b + 1)
                bank, full = t_bank(slot, "oT")
                for c in range(KI):
                    last = nc.tensor.transpose(bank[:, c * S:(c + 1) * S], on[:, c * P:(c + 1) * P], ident[0:S, 0:S])
                last.then_inc(full, 1)

            def project_out(slot):
                b, _, _ = slot.at(-1)
                wait_for(pe, w_low, 3)
                t_taken(slot, "oT")
                if slot.project:
                    wait_for(pe, v_free, KT * (b + 2) + V_FIRST)
                else:
                    wait_for(pe, v_free, KT * B)
                    wait_for(pe, wo_free, b)
                for c in range(KI):
                    last = products(bankV[0:S, 0:D], lambda a: oT[:, a, c, :], lambda a: wo[:, a, c, :],
                                    c == 0, c == KI - 1)
                last.then_inc(wo_full, 1)

            def transpose_x2(slot):
                b, par, _ = slot.at(-2)
                wait_for(pe, x2_done, b + 1)
                bank, full = t_bank(slot, "x2T")
                for kc in range(KD):
                    last = nc.tensor.transpose(bank[:, kc * S:(kc + 1) * S], x2[:, par, kc * P:(kc + 1) * P], ident[0:S, 0:S])
                last.then_inc(full, 1)

            def gate_logits(slot):
                wait_for(pe, small_in, 16 * N_SMALL)
                t_taken(slot, "x2T")
                bank, full = t_bank(slot, "gate")
                for kc in range(KD):
                    last = nc.tensor.matmul(bank[0:S, 0:E], x2T[:, kc, :], wg[:, kc, :], start=(kc == 0), stop=(kc == KD - 1))
                last.then_inc(full, 1)

            def do(slot):
                done = H * slot.at(0)[0]
                if slot.heads:
                    scores(slot, 0)
                if slot.tail:
                    attend(slot, -1, H - 2)
                    transpose_p(done, H - 1)
                if slot.project:
                    keys(slot, 0)
                if slot.heads:
                    scores(slot, 1)
                if slot.tail:
                    attend(slot, -1, H - 1)
                if slot.heads:
                    transpose_p(done + 1, 0)
                if slot.project:
                    keys(slot, 1)
                    values(slot, 0)
                if slot.heads:
                    transpose_p(done + 2, 1)
                    scores(slot, 2)
                if slot.project:
                    keys(slot, 2)
                if slot.heads:
                    attend(slot, 0, 0)
                if slot.project:
                    transpose_k(slot, 0)
                if slot.heads:
                    scores(slot, 3)
                if slot.project:
                    values(slot, 1)
                    keys(slot, 3)
                if slot.heads:
                    transpose_p(done + 3, 2)
                    scores(slot, 4)
                if slot.tail:
                    transpose_o(slot)
                if slot.project:
                    transpose_k(slot, 1)
                    queries(slot)
                if slot.heads:
                    attend(slot, 0, 1)
                    transpose_p(done + 4, 3)
                    attend(slot, 0, 2)
                if slot.project:
                    transpose_k(slot, 2)
                if slot.heads:
                    scores(slot, 5)
                    transpose_p(done + 5, 4)
                if slot.project:
                    values(slot, 2)
                if slot.heads:
                    attend(slot, 0, 3)
                if slot.project:
                    transpose_k(slot, 3)
                if slot.heads:
                    scores(slot, 6)
                    transpose_p(done + 6, 5)
                    attend(slot, 0, 4)
                if slot.project:
                    transpose_q(slot)
                if slot.tail:
                    project_out(slot)
                if slot.gate:
                    transpose_x2(slot)
                if slot.heads:
                    scores(slot, 7)
                    transpose_p(done + 7, 6)
                if slot.gate:
                    gate_logits(slot)
                if slot.norm:
                    transpose_x(slot, 0)
                    transpose_x(slot, 1)
                if slot.heads:
                    attend(slot, 0, 5)
                if slot.project:
                    values(slot, 3)

            run_slots(pe, do)

            pe.wait_ge(tied_done, 1)
            nc.tensor.transpose(bankT[1][:, 0:S], tied[:, :], ident[0:S, 0:S]).then_inc(score_full, 1)
            with pe.Fori(0, BITS) as i:
                pe.wait_ge(counted, i + 1)
                nc.tensor.matmul(bankO[:, 0:TRIES], same_e[:, :], count[:, :], start=True, stop=True).then_inc(totalled, 1)
            pe.wait_ge(eq_done, 1)
            nc.tensor.transpose(bankP[0:S, 0:P // 2].bitcast(BF16), eq_b[:, :], ident_b[:, :]).then_inc(eqT_full, 1)
            pe.wait_ge(eq_done, 2)
            nc.tensor.matmul(bankO[:, 0:1], same_e[:, :], gt_count[:, :], start=True, stop=False)
            nc.tensor.matmul(bankO[:, 0:1], before_e[:, :], eq_count[:, :], start=False, stop=True)
            pe.wait_ge(eqT_copied, 1)
            nc.tensor.matmul(bankS[:, 0, 0:S], eqT[:, :], upto[0:S, 0:S], start=True, stop=True).then_inc(prefix_full, 1)
            pe.wait_ge(chosen_done, 1)
            nc.tensor.transpose(bankP[0:S, 0:P // 2].bitcast(BF16), chosen[:, :], ident_b[:, :]).then_inc(chosen_full, 1)
            pe.wait_ge(chosenT_copied, 1)
            nc.tensor.matmul(bankS[0:S, 0, 0:P], upto[0:S, 0:S], chosenT[:, :], start=True, stop=False)
            nc.tensor.matmul(bankS[0:S, 0, 0:P], ones_b[:, :], before_c[:, :], start=False, stop=True).then_inc(place_full, 1)
            nc.tensor.transpose(bankT[1][:, 0:E * KF], b1_rows[:, :], ident[0:E * KF, 0:E * KF]).then_inc(b1_full, 1)

            def find(e, par):
                wait_for(pe, carry_done, e + 1)
                wait_for(pe, gate_sum, 2 * e)
                for b in range(B):
                    if b % HOT == 0:
                        wait_for(pe, hot_done, e * (B // HOT) + b // HOT + 1)
                    for t in range(ST):
                        last = nc.tensor.matmul(bankO[0:S, 8 * t:8 * t + 5], onehot[:, b, t * S:(t + 1) * S],
                                                carry_e[:, par, b, :], start=(b == 0 and t == 0), stop=(b == B - 1),
                                                skip_group_check=True)
                last.then_inc(id_full, 1)

            def transpose_ex(e, par, n):
                wait_for(pe, ex_in[par], 16 * ST * (n + 1))
                wait_for(pe, ext_free, 2 * e)
                for kc in range(KD):
                    for t in range(ST):
                        last = nc.tensor.transpose(bankX[kc][:, t * S:(t + 1) * S], ex[:, par, t, kc * P:(kc + 1) * P],
                                                   ident[0:S, 0:S])
                    last.then_inc(ext_full, 1)

            def expert_in(e, par, n):
                wait_for(pe, w1_low, e + 1)
                wait_for(pe, ext_free, 2 * (e + 1))
                for f in range(KF):
                    wait_for(pe, h_free, KF * e + f - 1)
                    for kc in range(KD):
                        last = products(bankS[:, f % 2, 0:CAP], lambda a: w1[:, par, a, kc, f * P:(f + 1) * P],
                                        lambda a: exT[:, a, kc, :], kc == 0, kc == KD - 1)
                    last.then_inc(h_full, 1)

            def expert_out(e, par, n):
                wait_for(pe, w2_low, e + 1)
                for half in range(2):
                    wait_for(pe, y_free, 2 * (e - 1) + half + 1)
                    for t in range(2):
                        rows = (2 * half + t) * S
                        for f in range(KF):
                            if half == 0 and t == 0:
                                wait_for(pe, hid_done, KF * e + f + 1)
                            last = products(bankY[half][0:S, t * D:(t + 1) * D], lambda a: hidT[:, a, f, rows:rows + S],
                                            lambda a: w2[:, par, a, f, :], f == 0, f == KF - 1)
                    last.then_inc(y_full, 1)

            find(0, 0)
            find(1, 1)
            transpose_ex(0, 0, 0)

            def expert(e, par, n, more=2):
                expert_in(e, par, n)
                if more:
                    transpose_ex(e + 1, 1 - par, n + par)
                expert_out(e, par, n)
                if more > 1:
                    find(e + 2, par)

            for par in range(2):
                expert(par, par, 0)
            with pe.Fori(1, E // 2 - 1) as n:
                for par in range(2):
                    expert(2 * n + par, par, n)
            expert(E - 2, 0, E // 2 - 1, more=1)
            expert(E - 1, 1, E // 2 - 1, more=0)


_INS = ['x', 'ctx_1024', 'mask_BxS2_bk0', 'g_xattn', 'g_ffn', 'L0_xattn_ln_x_w', 'L0_xattn_ln_x_b',
        'L0_xattn_ln_l_w', 'L0_xattn_ln_l_b', 'L0_xattn_Wq', 'L0_xattn_Wkv', 'L0_xattn_q_scale',
        'L0_xattn_k_scale', 'L0_xattn_Wo', 'L0_xattn_ln_o_w', 'L0_xattn_ln_o_b', 'L0_ffn_Wg', 'L0_ffn_W1',
        'L0_ffn_b1', 'L0_ffn_W2', 'L0_ffn_b2']
_OUTS = [((16, 112, 256), 'float32')]


def kernel(**inputs):
    import numpy as _np
    import concourse.bacc as _bacc
    from concourse import mybir as _mybir
    from concourse.bass_utils import run_bass_kernel_spmd as _run

    nc = _bacc.Bacc("TRN2", target_bir_lowering=False, num_devices=1)
    arrays, args = {}, []
    for name in _INS:
        a = _np.ascontiguousarray(inputs[name])
        arrays[f"in_{name}_dram"] = a
        args.append(nc.dram_tensor(f"in_{name}_dram", a.shape, _mybir.dt.from_np(a.dtype), kind="ExternalInput").ap())
    for i, (shape, dtype) in enumerate(_OUTS):
        dt = _mybir.dt.from_np(_np.dtype(dtype))
        args.append(nc.dram_tensor(f"out_{i}_dram", shape, dt, kind="ExternalOutput").ap())
    flamingo_block_kernel(nc, *args)
    r = _run(nc, [arrays], core_ids=[0])
    got = tuple(r.results[0][f"out_{i}_dram"] for i in range(len(_OUTS)))
    return got[0]
```
